# Optimizing a Trainium2 kernel written in Bass

```python
import numpy as np
import jax
import jax.numpy as jnp

def _softmax(x, axis=-1):
    return jax.nn.softmax(x, axis=axis)

def _gelu(x):
    return jax.nn.gelu(x, approximate=True)

def _silu(x):
    return jax.nn.silu(x)

def _sigmoid(x):
    return jax.nn.sigmoid(x)

def _layernorm(x, axis=-1, eps=1e-05):
    m = jnp.mean(x, axis=axis, keepdims=True)
    v = jnp.var(x, axis=axis, keepdims=True)
    return (x - m) / jnp.sqrt(v + eps)

def _scatter_add(tgt, idx, src, axis=0):
    return tgt.at[idx].add(src)

def _segment_sum(src, seg, n):
    return jax.ops.segment_sum(src, seg, n)
kernel_name = 'mk_decoder_preln_d2_seqx_r8_2b75ac'

def setup_inputs(seed: int=0):
    np.random.seed(seed)
    _w = jnp.asarray

    def _rec_inputs():
        import jax
        import jax.numpy as jnp
        _rk = jax.random.key(seed)
        x = 4.136e-05 + 0.9999 * jax.random.normal(jax.random.fold_in(_rk, 1), (1, 1024, 128), jnp.float32)
        _lenS = 1024 - jax.random.randint(jax.random.fold_in(_rk, 7), (1,), 0, max(1, 1024 // 4) + 1, jnp.int32)
        _lenS2 = 6404 - jax.random.randint(jax.random.fold_in(_rk, 8), (1,), 0, max(1, 6404 // 4) + 1, jnp.int32)
        _ctx_1024P = jax.random.normal(jax.random.fold_in(_rk, 11), (1, 16, 128), jnp.float32)
        _ctx_1024c = jax.random.dirichlet(jax.random.fold_in(_rk, 511), 0.3 * jnp.ones((16,), jnp.float32), (1, 6404))
        _ctx_1024t = jnp.einsum('bsk,bkd->bsd', _ctx_1024c, _ctx_1024P)
        _ctx_1024t = _ctx_1024t * jax.lax.rsqrt(jnp.mean(jnp.square(_ctx_1024t)) + 1e-12) * 0.953939
        ctx_1024 = -0.000125008 + 0.999885 * (_ctx_1024t + 0.3 * jax.random.normal(jax.random.fold_in(_rk, 611), (1, 6404, 128), jnp.float32))
        return (x, ctx_1024)
    x, ctx_1024 = _rec_inputs()

    def _L0_attn_setup():
        import jax, jax.numpy as jnp
        import numpy as np
        DIM = 128
        HEADS = 16
        SCALE = 3
        LP = 1
        HS = DIM // HEADS

        def layer_norm(x, g, b, eps=1e-06):
            m = x.mean(-1, keepdims=True)
            v = ((x - m) ** 2).mean(-1, keepdims=True)
            return (x - m) / jnp.sqrt(v + eps) * g + b

        def windows(x, reverse):
            T = x.shape[1]
            t = jnp.arange(T)[:, None]
            i = jnp.arange(SCALE)[None, :]
            idx = t + i * LP if reverse else t - i * LP
            valid = (idx >= 0) & (idx < T)
            w = jnp.take(x, jnp.clip(idx, 0, T - 1), axis=1)
            return w * valid[None, :, :, None].astype(x.dtype)

        def local_attn(q, k, v):
            B, T, S, _ = q.shape

            def split(x):
                return x.reshape(B, T, S, HEADS, HS).transpose(0, 1, 3, 2, 4)
            qh, kh, vh = (split(q), split(k), split(v))
            scores = jnp.einsum('bthqd,bthkd->bthqk', qh, kh) / np.float32(np.sqrt(HS))
            attn = jax.nn.softmax(scores, axis=-1)
            o = jnp.einsum('bthqk,bthkd->bthqd', attn, vh)
            return o.transpose(0, 1, 3, 2, 4).reshape(B, T, S, DIM)
        key = jax.random.key(seed)
        ks = jax.random.split(key, 12)
        s = 1.0 / np.sqrt(DIM)
        inp = {'input_feature': jax.random.normal(ks[0], (2, 512, DIM), jnp.float32), 'Wq': jax.random.normal(ks[1], (DIM, DIM), jnp.float32) * s, 'bq': jnp.zeros((DIM,), jnp.float32), 'Wk': jax.random.normal(ks[2], (DIM, DIM), jnp.float32) * s, 'bk': jnp.zeros((DIM,), jnp.float32), 'Wv': jax.random.normal(ks[3], (DIM, DIM), jnp.float32) * s, 'bv': jnp.zeros((DIM,), jnp.float32), 'Wfb': jax.random.normal(ks[4], (2 * DIM, DIM), jnp.float32) * s, 'bfb': jnp.zeros((DIM,), jnp.float32), 'Wo': jax.random.normal(ks[5], (DIM, DIM), jnp.float32) * s, 'bo': jnp.zeros((DIM,), jnp.float32), 'g1': jnp.ones((DIM,), jnp.float32), 'b1': jnp.zeros((DIM,), jnp.float32), 'g2': jnp.ones((DIM,), jnp.float32), 'b2': jnp.zeros((DIM,), jnp.float32)}
        return inp
    _L0_attn_all = _L0_attn_setup()
    _L0_attn_in = {k: v for k, v in _L0_attn_all.items() if k in ('Wq', 'bq', 'Wk', 'bk', 'Wv', 'bv', 'Wfb', 'bfb', 'Wo', 'bo', 'g1', 'b1', 'g2', 'b2')}
    del _L0_attn_all

    def _L0_xattn_setup():
        import jax, jax.numpy as jnp
        import numpy as np
        EPS = 1e-05
        key = jax.random.key(seed)
        ks = jax.random.split(key, 10)
        B, Nq, Nkv, D = (8, 128, 512, 128)
        s = 1.0 / np.sqrt(D)
        return {'img_feat': jax.random.normal(ks[0], (B, Nkv, D), jnp.float32), 'comb_feat': jax.random.normal(ks[1], (B, Nq, D), jnp.float32), 'Wq': jax.random.normal(ks[2], (D, D), jnp.float32) * s, 'bq': jnp.zeros((D,), jnp.float32), 'Wk': jax.random.normal(ks[3], (D, D), jnp.float32) * s, 'bk': jnp.zeros((D,), jnp.float32), 'Wv': jax.random.normal(ks[4], (D, D), jnp.float32) * s, 'bv': jnp.zeros((D,), jnp.float32), 'gamma': jnp.ones((D,), jnp.float32), 'beta': jnp.zeros((D,), jnp.float32)}
    _L0_xattn_all = _L0_xattn_setup()
    _L0_xattn_in = {k: v for k, v in _L0_xattn_all.items() if k in ('Wq', 'bq', 'Wk', 'bk', 'Wv', 'bv', 'gamma', 'beta')}
    del _L0_xattn_all

    def _L0_ffn_setup():
        import jax, jax.numpy as jnp
        import numpy as np
        B, N, D = (4, 256, 128)
        SPARSITY = 0.01
        key = jax.random.key(seed)
        k1, k2, k3 = jax.random.split(key, 3)
        x = jax.random.normal(k1, (B, N, D), dtype=jnp.float32)
        spatial = jax.random.normal(k2, (D, D), dtype=jnp.float32) * 0.02
        freq = jnp.fft.fft(spatial, axis=-1)
        k = int(D * SPARSITY)
        mag = jnp.abs(freq)
        kth = jax.lax.top_k(mag, k)[0][:, -1:]
        w_sparse = jnp.where(mag >= kth, freq, 0.0 + 0j)
        bias = jax.random.normal(k3, (D,), dtype=jnp.float32) * 0.01
        return {'x': x, 'w_freq_real': jnp.real(w_sparse).astype(jnp.float32), 'w_freq_imag': jnp.imag(w_sparse).astype(jnp.float32), 'bias': bias}
    _L0_ffn_all = _L0_ffn_setup()
    _L0_ffn_in = {k: v for k, v in _L0_ffn_all.items() if k in ('w_freq_real', 'w_freq_imag', 'bias')}
    del _L0_ffn_all

    def _L1_attn_setup():
        import jax, jax.numpy as jnp
        import numpy as np
        D_MODEL = 128
        NUM_HEADS = 16
        BATCH = 2
        SEQ = 256

        def _trunc_normal(key, shape, std):
            return jax.random.truncated_normal(key, -3.0, 3.0, shape, dtype=jnp.float32) * std
        key = jax.random.key(seed)
        kx, kq, kk, kv, ko = jax.random.split(key, 5)
        std = (2.0 / (D_MODEL + D_MODEL)) ** 0.5
        return {'X': jax.random.normal(kx, (BATCH, SEQ, D_MODEL), dtype=jnp.float32), 'q_proj': _trunc_normal(kq, (D_MODEL, D_MODEL), std), 'k_proj': _trunc_normal(kk, (D_MODEL, D_MODEL), std), 'v_proj': _trunc_normal(kv, (D_MODEL, D_MODEL), std), 'o_proj': _trunc_normal(ko, (D_MODEL, D_MODEL), std)}
    _L1_attn_all = _L1_attn_setup()
    _L1_attn_in = {k: v for k, v in _L1_attn_all.items() if k in ('q_proj', 'k_proj', 'v_proj', 'o_proj')}
    del _L1_attn_all

    def _L1_xattn_setup():
        import jax, jax.numpy as jnp
        import numpy as np
        key = jax.random.key(seed)
        k1, k2, k3, k4 = jax.random.split(key, 4)
        B, L1, L2, D = (32, 64, 64, 128)
        ix = jax.random.normal(k1, (B, L1, D), dtype=jnp.float32)
        iother = jax.random.normal(k2, (B, L2, D), dtype=jnp.float32)
        scale = 1.0 / np.sqrt(D)
        W = jax.random.uniform(k3, (D, D), dtype=jnp.float32, minval=-scale, maxval=scale)
        b = jax.random.uniform(k4, (D,), dtype=jnp.float32, minval=-scale, maxval=scale)
        return {'ix': ix, 'iother': iother, 'W': W, 'b': b}
    _L1_xattn_all = _L1_xattn_setup()
    _L1_xattn_in = {k: v for k, v in _L1_xattn_all.items() if k in ('W', 'b')}
    del _L1_xattn_all

    def _L1_ffn_setup():
        import jax, jax.numpy as jnp
        import numpy as np
        B, S, D, E, H, DO = (4, 256, 128, 8, 512, 128)
        TOP_K = 2
        LN_EPS = 1e-05
        key = jax.random.key(seed)
        ks = jax.random.split(key, 9)
        s = 0.02
        return {'x': jax.random.normal(ks[0], (B, S, D), dtype=jnp.float32), 'W1': jax.random.normal(ks[1], (E, D, H), dtype=jnp.float32) * s, 'b1': jnp.zeros((E, H), dtype=jnp.float32), 'W2': jax.random.normal(ks[2], (E, H, DO), dtype=jnp.float32) * s, 'b2': jnp.zeros((E, DO), dtype=jnp.float32), 'gate_W': jax.random.normal(ks[3], (D, E), dtype=jnp.float32) * s, 'shared_W': jax.random.normal(ks[4], (D, DO), dtype=jnp.float32) * s, 'shared_b': jnp.zeros((DO,), dtype=jnp.float32), 'gamma': jnp.ones((DO,), dtype=jnp.float32), 'beta': jnp.zeros((DO,), dtype=jnp.float32)}
    _L1_ffn_all = _L1_ffn_setup()
    _L1_ffn_in = {k: v for k, v in _L1_ffn_all.items() if k in ('W1', 'b1', 'W2', 'b2', 'gate_W', 'shared_W', 'shared_b', 'gamma', 'beta')}
    del _L1_ffn_all
    return {'x': x, 'ctx_1024': ctx_1024, 'L0_attn_Wq': _L0_attn_in['Wq'], 'L0_attn_bq': _L0_attn_in['bq'], 'L0_attn_Wk': _L0_attn_in['Wk'], 'L0_attn_bk': _L0_attn_in['bk'], 'L0_attn_Wv': _L0_attn_in['Wv'], 'L0_attn_bv': _L0_attn_in['bv'], 'L0_attn_Wfb': _L0_attn_in['Wfb'], 'L0_attn_bfb': _L0_attn_in['bfb'], 'L0_attn_Wo': _L0_attn_in['Wo'], 'L0_attn_bo': _L0_attn_in['bo'], 'L0_attn_g1': _L0_attn_in['g1'], 'L0_attn_b1': _L0_attn_in['b1'], 'L0_attn_g2': _L0_attn_in['g2'], 'L0_attn_b2': _L0_attn_in['b2'], 'L0_xattn_Wq': _L0_xattn_in['Wq'], 'L0_xattn_bq': _L0_xattn_in['bq'], 'L0_xattn_Wk': _L0_xattn_in['Wk'], 'L0_xattn_bk': _L0_xattn_in['bk'], 'L0_xattn_Wv': _L0_xattn_in['Wv'], 'L0_xattn_bv': _L0_xattn_in['bv'], 'L0_xattn_gamma': _L0_xattn_in['gamma'], 'L0_xattn_beta': _L0_xattn_in['beta'], 'L0_ffn_w_freq_real': _L0_ffn_in['w_freq_real'], 'L0_ffn_w_freq_imag': _L0_ffn_in['w_freq_imag'], 'L0_ffn_bias': _L0_ffn_in['bias'], 'L1_attn_q_proj': _L1_attn_in['q_proj'], 'L1_attn_k_proj': _L1_attn_in['k_proj'], 'L1_attn_v_proj': _L1_attn_in['v_proj'], 'L1_attn_o_proj': _L1_attn_in['o_proj'], 'L1_xattn_W': _L1_xattn_in['W'], 'L1_xattn_b': _L1_xattn_in['b'], 'L1_ffn_W1': _L1_ffn_in['W1'], 'L1_ffn_b1': _L1_ffn_in['b1'], 'L1_ffn_W2': _L1_ffn_in['W2'], 'L1_ffn_b2': _L1_ffn_in['b2'], 'L1_ffn_gate_W': _L1_ffn_in['gate_W'], 'L1_ffn_shared_W': _L1_ffn_in['shared_W'], 'L1_ffn_shared_b': _L1_ffn_in['shared_b'], 'L1_ffn_gamma': _L1_ffn_in['gamma'], 'L1_ffn_beta': _L1_ffn_in['beta']}

def reference(x, ctx_1024, L0_attn_Wq, L0_attn_bq, L0_attn_Wk, L0_attn_bk, L0_attn_Wv, L0_attn_bv, L0_attn_Wfb, L0_attn_bfb, L0_attn_Wo, L0_attn_bo, L0_attn_g1, L0_attn_b1, L0_attn_g2, L0_attn_b2, L0_xattn_Wq, L0_xattn_bq, L0_xattn_Wk, L0_xattn_bk, L0_xattn_Wv, L0_xattn_bv, L0_xattn_gamma, L0_xattn_beta, L0_ffn_w_freq_real, L0_ffn_w_freq_imag, L0_ffn_bias, L1_attn_q_proj, L1_attn_k_proj, L1_attn_v_proj, L1_attn_o_proj, L1_xattn_W, L1_xattn_b, L1_ffn_W1, L1_ffn_b1, L1_ffn_W2, L1_ffn_b2, L1_ffn_gate_W, L1_ffn_shared_W, L1_ffn_shared_b, L1_ffn_gamma, L1_ffn_beta):
    import jax
    import jax.numpy as jnp

    def _L0_attn_ref(input_feature, Wq, bq, Wk, bk, Wv, bv, Wfb, bfb, Wo, bo, g1, b1, g2, b2):
        import jax, jax.numpy as jnp
        import numpy as np
        DIM = 128
        HEADS = 16
        SCALE = 3
        LP = 1
        HS = DIM // HEADS

        def layer_norm(x, g, b, eps=1e-06):
            m = x.mean(-1, keepdims=True)
            v = ((x - m) ** 2).mean(-1, keepdims=True)
            return (x - m) / jnp.sqrt(v + eps) * g + b

        def windows(x, reverse):
            T = x.shape[1]
            t = jnp.arange(T)[:, None]
            i = jnp.arange(SCALE)[None, :]
            idx = t + i * LP if reverse else t - i * LP
            valid = (idx >= 0) & (idx < T)
            w = jnp.take(x, jnp.clip(idx, 0, T - 1), axis=1)
            return w * valid[None, :, :, None].astype(x.dtype)

        def local_attn(q, k, v):
            B, T, S, _ = q.shape

            def split(x):
                return x.reshape(B, T, S, HEADS, HS).transpose(0, 1, 3, 2, 4)
            qh, kh, vh = (split(q), split(k), split(v))
            scores = jnp.einsum('bthqd,bthkd->bthqk', qh, kh) / np.float32(np.sqrt(HS))
            attn = jax.nn.softmax(scores, axis=-1)
            o = jnp.einsum('bthqk,bthkd->bthqd', attn, vh)
            return o.transpose(0, 1, 3, 2, 4).reshape(B, T, S, DIM)
        x = layer_norm(input_feature, g1, b1)
        q = x @ Wq + bq
        k = x @ Wk + bk
        v = x @ Wv + bv
        out_f = local_attn(windows(q, False), windows(k, False), windows(v, False))[:, :, 1, :]
        out_r = local_attn(windows(q, True), windows(k, True), windows(v, True))[:, :, 1, :]
        out = jnp.concatenate([out_f, out_r], axis=2) @ Wfb + bfb
        out = layer_norm(out + x, g2, b2)
        return jax.nn.gelu(out @ Wo + bo, approximate=False)

    def _L0_xattn_ref(img_feat, comb_feat, Wq, bq, Wk, bk, Wv, bv, gamma, beta):
        import jax, jax.numpy as jnp
        import numpy as np
        EPS = 1e-05
        q = comb_feat @ Wq + bq
        k = img_feat @ Wk + bk
        v = img_feat @ Wv + bv
        scores = jnp.einsum('bqd,bkd->bqk', q, k)
        attn = jax.nn.softmax(scores, axis=-1)
        x = jnp.einsum('bqk,bkd->bqd', attn, v)
        h = comb_feat + x
        mu = jnp.mean(h, axis=-1, keepdims=True)
        var = jnp.mean(jnp.square(h - mu), axis=-1, keepdims=True)
        out = (h - mu) * jax.lax.rsqrt(var + EPS) * gamma + beta
        return out

    def _L0_ffn_ref(x, w_freq_real, w_freq_imag, bias):
        import jax, jax.numpy as jnp
        import numpy as np
        B, N, D = (4, 256, 128)
        SPARSITY = 0.01
        w = jax.lax.complex(w_freq_real, w_freq_imag)
        x_freq = jnp.fft.fft(x, axis=-1)
        y_freq = jnp.einsum('bnd,do->bno', x_freq, w)
        y = jnp.real(jnp.fft.ifft(y_freq, axis=-1))
        return y + bias

    def _L1_attn_ref(X, q_proj, k_proj, v_proj, o_proj):
        import jax, jax.numpy as jnp
        import numpy as np
        D_MODEL = 128
        NUM_HEADS = 16
        BATCH = 2
        SEQ = 256

        def _trunc_normal(key, shape, std):
            return jax.random.truncated_normal(key, -3.0, 3.0, shape, dtype=jnp.float32) * std
        B, S, D = X.shape
        H = NUM_HEADS
        d_k = D // H
        q_w = q_proj.reshape(H, d_k, D)
        k_w = k_proj.reshape(H, d_k, D)
        v_w = v_proj.reshape(H, d_k, D)
        o_w = o_proj.reshape(D, H, d_k).transpose(1, 0, 2)
        q = jnp.einsum('hkd,bsd->bhsk', q_w, X)
        k = jnp.einsum('hkd,bsd->bhsk', k_w, X)
        v = jnp.einsum('hkd,bsd->bhsk', v_w, X)
        scale = 1.0 / jnp.sqrt(jnp.asarray(d_k, dtype=X.dtype))
        scores = jnp.einsum('bhqk,bhsk->bhqs', q, k) * scale
        causal = jnp.tril(jnp.ones((S, S), dtype=bool))
        scores = jnp.where(causal, scores, jnp.asarray(-jnp.inf, dtype=scores.dtype))
        attn = jax.nn.softmax(scores, axis=-1)
        attn_out = jnp.einsum('bhqs,bhsk->bhqk', attn, v)
        return jnp.einsum('hdv,bhsv->bsd', o_w, attn_out)

    def _L1_xattn_ref(ix, iother, W, b):
        import jax, jax.numpy as jnp
        import numpy as np
        ex = jnp.einsum('bld,ed->ble', ix, W) + b
        eother = jnp.einsum('bld,ed->ble', iother, W) + b
        scores = jnp.einsum('bld,bmd->blm', ex, eother)
        attn = jax.nn.softmax(scores, axis=-1)
        aligned = jnp.einsum('blm,bmd->bld', attn, iother)
        return aligned

    def _L1_ffn_ref(x, W1, b1, W2, b2, gate_W, shared_W, shared_b, gamma, beta):
        import jax, jax.numpy as jnp
        import numpy as np
        B, S, D, E, H, DO = (4, 256, 128, 8, 512, 128)
        TOP_K = 2
        LN_EPS = 1e-05
        d = x.shape[-1]
        flat = x.reshape(-1, d)
        n_exp = gate_W.shape[-1]
        probs = jax.nn.softmax(flat @ gate_W, axis=-1)
        topk_w, topk_idx = jax.lax.top_k(probs, TOP_K)
        topk_w = topk_w / topk_w.sum(axis=-1, keepdims=True)
        combine = (jax.nn.one_hot(topk_idx, n_exp, dtype=flat.dtype) * topk_w[..., None]).sum(axis=1)
        out = 0.5 * jax.nn.gelu(flat @ shared_W + shared_b, approximate=False)
        for e in range(n_exp):
            h = jax.nn.gelu(flat @ W1[e] + b1[e], approximate=False)
            out = out + combine[:, e:e + 1] * (h @ W2[e] + b2[e])
        mean = out.mean(axis=-1, keepdims=True)
        var = ((out - mean) ** 2).mean(axis=-1, keepdims=True)
        out = (out - mean) * jax.lax.rsqrt(var + LN_EPS) * gamma + beta
        return out.reshape(*x.shape[:-1], out.shape[-1])
    x = x + _L0_attn_ref(_layernorm(x, axis=-1), L0_attn_Wq, L0_attn_bq, L0_attn_Wk, L0_attn_bk, L0_attn_Wv, L0_attn_bv, L0_attn_Wfb, L0_attn_bfb, L0_attn_Wo, L0_attn_bo, L0_attn_g1, L0_attn_b1, L0_attn_g2, L0_attn_b2)
    x = x + _L0_xattn_ref(ctx_1024, _layernorm(x, axis=-1), L0_xattn_Wq, L0_xattn_bq, L0_xattn_Wk, L0_xattn_bk, L0_xattn_Wv, L0_xattn_bv, L0_xattn_gamma, L0_xattn_beta)
    x = x + _L0_ffn_ref(_layernorm(x, axis=-1), L0_ffn_w_freq_real, L0_ffn_w_freq_imag, L0_ffn_bias)
    x = x + _L1_attn_ref(_layernorm(x, axis=-1), L1_attn_q_proj, L1_attn_k_proj, L1_attn_v_proj, L1_attn_o_proj)
    x = x + _L1_xattn_ref(_layernorm(x, axis=-1), ctx_1024, L1_xattn_W, L1_xattn_b)
    x = x + _L1_ffn_ref(_layernorm(x, axis=-1), L1_ffn_W1, L1_ffn_b1, L1_ffn_W2, L1_ffn_b2, L1_ffn_gate_W, L1_ffn_shared_W, L1_ffn_shared_b, L1_ffn_gamma, L1_ffn_beta)
    return x

_drawn_inputs = setup_inputs


def setup_inputs(seed=0):
    import zlib

    import numpy as np

    out = dict(_drawn_inputs(seed))
    spreads = {'L0_attn_bq': (0.0, 0.1),
     'L0_attn_bk': (0.0, 0.1),
     'L0_attn_bv': (0.0, 0.1),
     'L0_attn_bfb': (0.0, 0.1),
     'L0_attn_bo': (0.0, 0.1),
     'L0_attn_g1': (1.0, 0.2),
     'L0_attn_b1': (0.0, 0.1),
     'L0_attn_g2': (1.0, 0.2),
     'L0_attn_b2': (0.0, 0.1),
     'L0_xattn_bq': (0.0, 0.1),
     'L0_xattn_bk': (0.0, 0.1),
     'L0_xattn_bv': (0.0, 0.1),
     'L0_xattn_gamma': (1.0, 0.2),
     'L0_xattn_beta': (0.0, 0.1),
     'L1_ffn_b1': (0.0, 0.1),
     'L1_ffn_b2': (0.0, 0.1),
     'L1_ffn_shared_b': (0.0, 0.1),
     'L1_ffn_gamma': (1.0, 0.2),
     'L1_ffn_beta': (0.0, 0.1)}
    factors = {}
    for name, (base, spread) in spreads.items():
        noise = np.random.default_rng([zlib.crc32(name.encode()), seed]).standard_normal(out[name].shape)
        drawn = base * np.exp(spread * noise) if base else spread * noise
        out[name] = jnp.asarray(drawn.astype(out[name].dtype))
    for name, factor in factors.items():
        out[name] = (out[name] * factor).astype(out[name].dtype)
    return out
```

```python
from contextlib import ExitStack

import concourse.bass as bass
from concourse import mybir

ALU = mybir.AluOpType
ACT = mybir.ActivationFunctionType
AX = mybir.AxisListType
F32 = mybir.dt.float32
F16 = mybir.dt.float16
BF16 = mybir.dt.bfloat16

P = 128
TOKENS = 1024
TT = TOKENS // P
HALF = 512
HT = HALF // P
CTX = 6404
KT = CTX // P
TAIL = CTX - KT * P
HEADS, HD = 16, 8
GROUPS = 4
HPG = HEADS // GROUPS
STRIP = 32
EXPERTS, HIDDEN = 8, 512
HC = HIDDEN // P
RING = 5
STEP = 2 * RING
MASKED = -1.0e30


def decoder_kernel(nc, a, out):
    with ExitStack() as ctx:
        def sb(name, shape, dt=F32):
            return ctx.enter_context(nc.sbuf_tensor(name, shape, dt))

        def sem(name):
            return ctx.enter_context(nc.semaphore(name))

        PS = ctx.enter_context(nc.psum_tensor("PS", [P, 8, HALF], F32))
        X = sb("X", [P, TT, P])
        XN = sb("XN", [P, TT, P])
        XT = sb("XT", [P, TOKENS])
        NAT = sb("NAT", [P, TT, P])
        BIG = sb("BIG", [P, (KT + 1) * HALF])
        CTH = sb("CTH", [P, CTX], F16)
        CTL = sb("CTL", [P, CTX], F16)
        QH = sb("QH", [P, TOKENS], F16)
        QL = sb("QL", [P, TOKENS], F16)
        VR = sb("VR", [P, STEP, P])
        VTAIL = sb("VTAIL", [TAIL, P])
        RM = sb("RM", [P, 2, HALF])
        LS = sb("LS", [P, 2, HALF])
        OT = sb("OT", [P, TOKENS])
        DG = sb("DG", [P, HT, P])
        MX = sb("MX", [P, HT])
        MC = sb("MC", [P, HT])
        RL = sb("RL", [P, TT])
        ST = sb("ST", [P, TT, 6])
        MV = sb("MV", [P, TT, 2])
        VE = sb("VE", [P, TT])
        RS = sb("RS", [P, TT])
        NEGHALF = sb("NEGHALF", [P, TT])
        ONES = sb("ONES", [P, P])
        SQ = ["ident", "cos", "sin", "nsin", "blocks", "strip_sum", "L0_attn_Wq", "L0_attn_Wk", "L0_attn_Wv",
              "wfb_f", "wfb_r", "L0_attn_Wo", "L0_xattn_Wq", "xwk_t", "L0_xattn_Wv",
              "wr", "wi", "w1x_t", "L1_xattn_W", "L1_ffn_shared_W"]
        W = {n: sb("w_" + n, [P, P]) for n in SQ}
        SQ_SRC = {"wfb_f": a["L0_attn_Wfb"][0:P, :], "wfb_r": a["L0_attn_Wfb"][P:2 * P, :],
                  "wr": a["L0_ffn_w_freq_real"], "wi": a["L0_ffn_w_freq_imag"]}
        COLS = ["L0_attn_bq", "L0_attn_bk", "L0_attn_bv", "L0_attn_g1", "L0_attn_b1", "L0_attn_g2", "L0_attn_b2",
                "L0_xattn_bq", "L0_xattn_bk", "L1_xattn_b", "ones_row"]
        C = {n: sb("c_" + n, [P, 1]) for n in COLS}
        ROWS = ["L0_attn_bfb", "L0_attn_bo", "L0_xattn_bv", "L0_xattn_gamma", "L0_xattn_beta", "L0_ffn_bias",
                "L1_ffn_shared_b", "L1_ffn_gamma", "L1_ffn_beta"]
        R = {n: sb("r_" + n, [P, P]) for n in ROWS}
        MIX = sb("MIX", [P, P])
        AMT = sb("AMT", [P, 2, P])
        IDB = sb("IDB", [P, P], BF16)
        MASKN = sb("MASKN", [P, P], BF16)
        MASKT = sb("MASKT", [P, P], BF16)

        def work(at, *shape):
            n = 1
            for s in shape:
                n *= s
            v = BIG[:, at:at + n]
            if len(shape) == 2:
                return v.rearrange("p (a b) -> p a b", b=shape[1])
            if len(shape) == 3:
                return v.rearrange("p (a b c) -> p a b c", b=shape[1], c=shape[2])
            return v

        ident = W["ident"]

        s_x, s_sq, s_vec, s_mask, s_ctx, s_out = (sem(n) for n in (
            "x_loaded", "squares_loaded", "vectors_loaded", "masks_loaded", "context_loaded", "out_stored"))
        s_const = sem("constants_set")
        s_stats, s_aggr, s_var, s_rstd, s_normed, s_turned, s_xt = (sem(n) for n in (
            "norm_stats", "norm_aggregated", "norm_variance", "norm_rstd", "norm_applied", "norm_turned", "norm_xt"))
        s_ctx_turned, s_ctx_hi, s_ctx_lo = sem("context_turned"), sem("context_high"), sem("context_low")

        calls = {"norm": 0}

        def norm_stage(src, dst, eps, scale=1.0, bias=0.0, turn=True):
            n = calls["norm"]
            calls["norm"] += 1
            turns = calls.setdefault("turns", 0)
            if turn:
                calls["turns"] += 1
            with nc.Block() as block:
                @block.vector
                def _(dve):
                    for t in range(TT):
                        dve.bn_stats(ST[:, t, :], src[:, t, :]).then_inc(s_stats, 1)
                    for t in range(TT):
                        dve.wait_ge(s_stats, n * TT + t + 1)
                        dve.bn_aggr(MV[:, t, :], ST[:, t, :]).then_inc(s_aggr, 1)
                    dve.wait_ge(s_aggr, (n + 1) * TT)
                    dve.tensor_scalar(VE[:, :], MV[:, :, 1], eps, None, ALU.add).then_inc(s_var, 1)
                    dve.wait_ge(s_rstd, n + 1)
                    for t in range(TT):
                        dve.tensor_scalar(dst[:, t, :], src[:, t, :], MV[:, t, 0:1], RS[:, t:t + 1],
                                          ALU.subtract, ALU.mult).then_inc(s_normed, 1)

                @block.gpsimd
                def _(pool):
                    pool.wait_ge(s_var, n + 1)
                    pool.tensor_tensor(RS[:, :], VE[:, :], NEGHALF[:, :], ALU.pow).then_inc(s_rstd, 1)

                if turn:
                    @block.tensor
                    def _(pe):
                        for t in range(TT):
                            pe.wait_ge(s_normed, n * TT + t + 1)
                            pe.transpose(PS[:, t // HT, (t % HT) * P:(t % HT + 1) * P], dst[:, t, :],
                                         ident[:, :]).then_inc(s_turned, 1)

                    @block.scalar
                    def _(act):
                        for h in range(2):
                            act.wait_ge(s_turned, turns * TT + (h + 1) * HT)
                            act.activation(XT[:, h * HALF:(h + 1) * HALF], PS[:, h, :], ACT.Identity,
                                           bias=bias, scale=scale).then_inc(s_xt, 1)

        CN = work(0, KT, P)
        ctx_main = a["ctx_1024"][0, 0:KT * P, :].rearrange("(p t) d -> p t d", t=KT)
        ctx_tail = a["ctx_1024"][0, KT * P:CTX, :]

        with nc.Block() as block:
            @block.sync
            def _(sp):
                sp.dma_start(X[:, :, :], a["x"][0].rearrange("(t p) d -> p t d", p=P)).then_inc(s_x, 16)
                for n in SQ:
                    src = SQ_SRC.get(n, a.get(n))
                    sp.dma_start(W[n][:, :], src).then_inc(s_sq, 16)
                sp.dma_start(IDB[:, :], a["ident_b"]).then_inc(s_mask, 16)
                sp.dma_start(MASKN[:, :], a["mask_n"]).then_inc(s_mask, 16)
                sp.dma_start(MASKT[:, :], a["mask_t"]).then_inc(s_mask, 16)
                sp.wait_ge(s_x, 16)
                sp.wait_ge(s_sq, 16 * len(SQ))

            @block.scalar
            def _(act):
                for n in COLS:
                    act.dma_start(C[n][:, :], a[n].rearrange("(p o) -> p o", o=1)).then_inc(s_vec, 16)
                for n in ROWS:
                    act.dma_start(R[n][:, :], a[n].partition_broadcast(P)).then_inc(s_vec, 16)
                act.dma_start(CN, ctx_main).then_inc(s_ctx, 16)
                act.dma_start(VTAIL[:, :], ctx_tail).then_inc(s_ctx, 16)
                act.wait_ge(s_vec, 16 * (len(COLS) + len(ROWS)))

            @block.gpsimd
            def _(pool):
                pool.memset(NEGHALF[:, :], -0.5).then_inc(s_const, 1)
                pool.memset(ONES[:, :], 1.0).then_inc(s_const, 1)

        norm_stage(X, XN, 1e-5, turn=False)
        norm_stage(XN, XN, 1e-6, scale=C["L0_attn_g1"][:, 0:1], bias=C["L0_attn_b1"][:, 0:1])

        PADW = TOKENS + 4
        CW = (TOKENS + 2) // 3
        at = KT * P
        LQ, LK, LV = (work(at + i * PADW, PADW) for i in range(3))
        at += 3 * PADW
        PR = work(at, 3, TOKENS + 2)
        at += 3 * (TOKENS + 2)
        LM = work(at, TOKENS + 2)
        LA = work(at + TOKENS + 2, TOKENS + 2)
        s_lp, s_lq, s_pad, s_prod, s_lsc, s_lev, s_lch, s_lexp, s_la, s_lz, s_lzc = (sem(n) for n in (
            "local_projected", "local_qkv", "local_padded", "local_products", "local_scores", "local_evacuated",
            "local_chain", "local_exp", "local_out", "local_joined", "local_join_copied"))
        with nc.Block() as block:
            @block.tensor
            def _(pe):
                for i, w in enumerate(("L0_attn_Wq", "L0_attn_Wk", "L0_attn_Wv")):
                    for h in range(2):
                        pe.matmul(PS[:, 2 * i + h, :], W[w][:, :], XT[:, h * HALF:(h + 1) * HALF],
                                  start=True, stop=True).then_inc(s_lp, 1)
                for j in range(3):
                    pe.wait_ge(s_prod, j + 1)
                    for c in range(3):
                        n = 3 * j + c
                        pe.wait_ge(s_lq, 6)
                        if n >= 6:
                            pe.wait_ge(s_lev, n - 5)
                        pe.matmul(PS[:, n % 6, 0:CW], W["blocks"][:, :], PR[:, j, c * CW:(c + 1) * CW],
                                  start=True, stop=True).then_inc(s_lsc, 1)
                pe.wait_ge(s_la, 1)
                pe.wait_ge(s_lev, 9)
                for t in range(TT):
                    o = PS[:, t // HT, (t % HT) * P:(t % HT + 1) * P]
                    pe.matmul(o, LA[:, t * P:(t + 1) * P], W["wfb_f"][:, :], start=True, stop=False)
                    pe.matmul(o, LA[:, t * P + 2:(t + 1) * P + 2], W["wfb_r"][:, :], start=False, stop=False)
                    pe.matmul(o, XT[:, t * P:(t + 1) * P], ident[:, :], start=False, stop=True).then_inc(s_lz, 1)

            @block.gpsimd
            def _(pool):
                for v in (LQ, LK, LV):
                    pool.memset(v[:, 0:2], 0.0).then_inc(s_pad, 1)
                    pool.memset(v[:, PADW - 2:PADW], 0.0).then_inc(s_pad, 1)

            @block.scalar
            def _(act):
                for i, (v, b) in enumerate(((LQ, "L0_attn_bq"), (LK, "L0_attn_bk"), (LV, "L0_attn_bv"))):
                    for h in range(2):
                        act.wait_ge(s_lp, 2 * i + h + 1)
                        act.activation(v[:, 2 + h * HALF:2 + (h + 1) * HALF], PS[:, 2 * i + h, :], ACT.Identity,
                                       bias=C[b][:, 0:1]).then_inc(s_lq, 1)
                for n in range(9):
                    act.wait_ge(s_lsc, n + 1)
                    act.activation(PR[:, n // 3, (n % 3) * CW:(n % 3 + 1) * CW], PS[:, n % 6, 0:CW],
                                   ACT.Copy).then_inc(s_lev, 1)
                for j in range(3):
                    act.wait_ge(s_lch, 3 + j)
                    act.activation(PR[:, j, :], PR[:, j, :], ACT.Exp, scale=float(HD) ** -0.5).then_inc(s_lexp, 1)

            @block.vector
            def _(dve):
                dve.wait_ge(s_lq, 4)
                dve.wait_ge(s_pad, 4)
                for j in range(3):
                    dve.tensor_tensor(PR[:, j, :], LQ[:, 1:PADW - 1], LK[:, j:j + TOKENS + 2],
                                      ALU.mult).then_inc(s_prod, 1)
                dve.wait_ge(s_lev, 9)
                dve.tensor_tensor(LM, PR[:, 0, :], PR[:, 1, :], ALU.max).then_inc(s_lch, 1)
                dve.wait_ge(s_lch, 1)
                dve.tensor_tensor(LM, LM, PR[:, 2, :], ALU.max).then_inc(s_lch, 1)
                dve.wait_ge(s_lch, 2)
                for j in range(3):
                    dve.tensor_tensor(PR[:, j, :], PR[:, j, :], LM, ALU.subtract).then_inc(s_lch, 1)
                dve.wait_ge(s_lexp, 3)
                dve.wait_ge(s_lch, 5)
                dve.tensor_tensor(LM, PR[:, 0, :], PR[:, 1, :], ALU.add).then_inc(s_lch, 1)
                dve.wait_ge(s_lch, 6)
                dve.tensor_tensor(LM, LM, PR[:, 2, :], ALU.add).then_inc(s_lch, 1)
                dve.wait_ge(s_lq, 6)
                dve.wait_ge(s_pad, 6)
                dve.wait_ge(s_lch, 7)
                dve.reciprocal(LM, LM).then_inc(s_lch, 1)
                for j in range(3):
                    dve.tensor_tensor(PR[:, j, :], PR[:, j, :], LV[:, j:j + TOKENS + 2], ALU.mult).then_inc(s_lch, 1)
                dve.wait_ge(s_lch, 10)
                dve.tensor_tensor(LA, PR[:, 0, :], PR[:, 1, :], ALU.add).then_inc(s_lch, 1)
                dve.wait_ge(s_lch, 12)
                dve.tensor_tensor(LA, LA, PR[:, 2, :], ALU.add).then_inc(s_lch, 1)
                dve.wait_ge(s_lch, 13)
                dve.tensor_tensor(LA, LA, LM, ALU.mult).then_inc(s_la, 1)
                for h in range(2):
                    dve.wait_ge(s_lz, (h + 1) * HT)
                    dve.tensor_tensor(NAT[:, h * HT:(h + 1) * HT, :],
                                      PS[:, h, :].rearrange("p (t d) -> p t d", d=P),
                                      R["L0_attn_bfb"][:, :].unsqueeze(1).broadcast_to([P, HT, P]),
                                      ALU.add).then_inc(s_lzc, 1)

        norm_stage(NAT, NAT, 1e-6, scale=C["L0_attn_g2"][:, 0:1], bias=C["L0_attn_b2"][:, 0:1])

        lin = {"n": 0}
        s_lin, s_linb, s_ling, s_linx, s_lwait = (sem(n) for n in ("linear_done", "linear_biased", "linear_gelu", "linear_added", "linear_weights"))

        def linear_stage(weight, bias_row, gelu):
            n = lin["n"]
            g = lin.setdefault("g", 0)
            lin["n"] += 1
            lin["g"] += int(gelu)
            with nc.Block() as block:
                @block.tensor
                def _(pe):
                    for t in range(TT):
                        pe.matmul(PS[:, t // HT, (t % HT) * P:(t % HT + 1) * P], XT[:, t * P:(t + 1) * P],
                                  weight, start=True, stop=True).then_inc(s_lin, 1)

                @block.vector
                def _(dve):
                    for h in range(2):
                        dve.wait_ge(s_lin, n * TT + (h + 1) * HT)
                        dve.tensor_tensor(NAT[:, h * HT:(h + 1) * HT, :],
                                          PS[:, h, :].rearrange("p (t d) -> p t d", d=P),
                                          bias_row.unsqueeze(1).broadcast_to([P, HT, P]),
                                          ALU.add).then_inc(s_linb, 1)
                    for h in range(2):
                        if gelu:
                            dve.wait_ge(s_ling, 2 * g + h + 1)
                        else:
                            dve.wait_ge(s_linb, 2 * n + h + 1)
                        v = X[:, h * HT:(h + 1) * HT, :]
                        dve.tensor_tensor(v, v, NAT[:, h * HT:(h + 1) * HT, :], ALU.add).then_inc(s_linx, 1)

                if gelu:
                    @block.scalar
                    def _(act):
                        for h in range(2):
                            act.wait_ge(s_linb, 2 * n + h + 1)
                            v = NAT[:, h * HT:(h + 1) * HT, :]
                            act.activation(v, v, ACT.Gelu).then_inc(s_ling, 1)

        linear_stage(W["L0_attn_Wo"][:, :], R["L0_attn_bo"][:, :], True)

        LOTS = (KT + 3) // 4
        with nc.Block() as block:
            @block.tensor
            def _(pe):
                pe.wait_ge(s_ctx, 32)
                for b in range(LOTS):
                    if b >= 4:
                        pe.wait_ge(s_ctx_lo, b - 3)
                    for t in range(4 * b, min(4 * b + 4, KT)):
                        mm = pe.transpose(PS[:, b % 4, (t % 4) * P:(t % 4 + 1) * P], CN[:, t, :], ident[:, :])
                    mm.then_inc(s_ctx_turned, 1)
                pe.transpose(PS[:, 4, 0:TAIL], VTAIL[:, :], ident[0:TAIL, 0:TAIL]).then_inc(s_ctx_turned, 1)

            def part(b):
                if b < LOTS:
                    w = min(4 * P, KT * P - 4 * b * P)
                    return PS[:, b % 4, 0:w], slice(4 * b * P, 4 * b * P + w)
                return PS[:, 4, 0:TAIL], slice(KT * P, CTX)

            @block.scalar
            def _(act):
                for b in range(LOTS + 1):
                    src, cols = part(b)
                    act.wait_ge(s_ctx_turned, b + 1)
                    act.activation(CTH[:, cols], src, ACT.Copy).then_inc(s_ctx_hi, 1)

            @block.vector
            def _(dve):
                for b in range(LOTS + 1):
                    src, cols = part(b)
                    dve.wait_ge(s_ctx_hi, b + 1)
                    dve.tensor_tensor(CTL[:, cols], src, CTH[:, cols], ALU.subtract).then_inc(s_ctx_lo, 1)

        s_q, s_qs, s_qf, s_qh, s_ql, s_cb, s_cbs = (sem(n) for n in (
            "cross_q", "cross_q_biased", "cross_q_folded", "cross_q_high", "cross_q_low", "cross_key_bias", "cross_key_bias_kept"))
        s_sc, s_scc, s_mx, s_mxf, s_mt, s_mr, s_dg, s_mb = (sem(n) for n in (
            "cross_scores", "cross_scores_copied", "cross_max", "cross_max_joined", "cross_max_turned",
            "cross_max_rows", "cross_max_diagonal", "cross_max_spread"))
        s_sub, s_pr, s_pv, s_sv, s_sp, s_ot = (sem(n) for n in (
            "cross_shifted", "cross_probs", "cross_values", "cross_sum_vector", "cross_sum_pool", "cross_out_turned"))
        s_va, s_vb = sem("values_in_a"), sem("values_in_b")
        s_l, s_rl, s_on, s_of = sem("cross_sums"), sem("cross_sum_recip"), sem("cross_out"), sem("cross_finished")
        QF = work(KT * HALF - TOKENS, TOKENS)
        CB = sb("CB", [P, TT])
        xc = {"n": 0, "half": 0}

        def query_stage(w_query, query_bias, w_fold, key_bias):
            n = xc["n"]
            with nc.Block() as block:
                @block.tensor
                def _(pe):
                    for h in range(2):
                        pe.matmul(PS[:, h, :], w_query, XT[:, h * HALF:(h + 1) * HALF], start=True,
                                  stop=True).then_inc(s_q, 1)
                    for h in range(2):
                        pe.wait_ge(s_qs, 2 * n + h + 1)
                        pe.matmul(PS[:, 2 + h, :], w_fold, QF[:, h * HALF:(h + 1) * HALF], start=True,
                                  stop=True).then_inc(s_qf, 1)
                    for t in range(TT):
                        mm = pe.matmul(PS[:, 4, t:t + 1], QF[:, t * P:(t + 1) * P], key_bias, start=True, stop=True)
                    mm.then_inc(s_cb, 1)

                @block.scalar
                def _(act):
                    for h in range(2):
                        act.wait_ge(s_q, 2 * n + h + 1)
                        act.activation(QF[:, h * HALF:(h + 1) * HALF], PS[:, h, :], ACT.Identity,
                                       bias=query_bias).then_inc(s_qs, 1)
                    for h in range(2):
                        act.wait_ge(s_qf, 2 * n + h + 1)
                        act.activation(QH[:, h * HALF:(h + 1) * HALF], PS[:, 2 + h, :], ACT.Copy).then_inc(s_qh, 1)

                @block.vector
                def _(dve):
                    for h in range(2):
                        dve.wait_ge(s_qh, 2 * n + h + 1)
                        dve.tensor_tensor(QL[:, h * HALF:(h + 1) * HALF], PS[:, 2 + h, :],
                                          QH[:, h * HALF:(h + 1) * HALF], ALU.subtract).then_inc(s_ql, 1)
                    dve.wait_ge(s_cb, n + 1)
                    dve.tensor_copy(CB[:, :], PS[:, 4, 0:TT]).then_inc(s_cbs, 1)

        SCORE_BANKS = 5
        TILES = KT + 1
        DVE_SUMS = (1, 4, 6, 9)
        POOL_SUMS = tuple(u for u in range(STEP) if u not in DVE_SUMS)
        STEPS = KT // STEP

        def score_stage(h):
            n = xc["half"]
            base = n * TILES
            qh, ql = QH[:, h * HALF:(h + 1) * HALF], QL[:, h * HALF:(h + 1) * HALF]
            with nc.Block() as block:
                @block.tensor
                def _(pe):
                    def tile(i, u, first):
                        j = i * STEP + u
                        if not (first and u < SCORE_BANKS):
                            pe.wait_ge(s_scc, base + j - SCORE_BANKS + 1)
                        kh, kl = CTH[:, bass.ds(j * P, P)], CTL[:, bass.ds(j * P, P)]
                        o = PS[:, u % SCORE_BANKS, :]
                        pe.matmul(o, kh, qh, start=True, stop=False)
                        pe.matmul(o, kh, ql, start=False, stop=False)
                        pe.matmul(o, kl, qh, start=False, stop=True).then_inc(s_sc, 1)

                    for u in range(STEP):
                        tile(0, u, True)
                    with pe.Fori(1, STEPS) as i:
                        for u in range(STEP):
                            tile(i, u, False)
                    pe.wait_ge(s_scc, base + KT - SCORE_BANKS + 1)
                    o = PS[0:TAIL, 0, :]
                    pe.matmul(o, CTH[:, KT * P:CTX], qh, start=True, stop=False)
                    pe.matmul(o, CTH[:, KT * P:CTX], ql, start=False, stop=False)
                    pe.matmul(o, CTL[:, KT * P:CTX], qh, start=False, stop=True).then_inc(s_sc, 1)
                    pe.wait_ge(s_mxf, n + 1)
                    for k in range(HT):
                        mm = pe.transpose(PS[:, 7, k * P:(k + 1) * P], RM[:, 0, k * P:(k + 1) * P], ident[:, :])
                    mm.then_inc(s_mt, 1)
                    pe.wait_ge(s_dg, HT * (n + 1))
                    pe.matmul(PS[:, 6, :], ONES[:, :], DG[:, :, :].rearrange("p a b -> p (a b)"), start=True,
                              stop=True).then_inc(s_mb, 1)

                @block.scalar
                def _(act):
                    def tile(i, u):
                        j = i * STEP + u
                        act.wait_ge(s_sc, base + j + 1)
                        act.activation(BIG[:, bass.ds(j * HALF, HALF)], PS[:, u % SCORE_BANKS, :],
                                       ACT.Copy).then_inc(s_scc, 1)

                    with act.Fori(0, STEPS) as i:
                        for u in range(STEP):
                            tile(i, u)
                    act.wait_ge(s_sc, base + TILES)
                    act.activation(BIG[0:TAIL, KT * HALF:(KT + 1) * HALF], PS[0:TAIL, 0, :],
                                   ACT.Copy).then_inc(s_scc, 1)

                @block.vector
                def _(dve):
                    def tile(i, u, first):
                        j = i * STEP + u
                        r = RM[:, u % 2, :]
                        s = BIG[:, bass.ds(j * HALF, HALF)]
                        dve.wait_ge(s_scc, base + j + 1)
                        if first and u < 2:
                            dve.tensor_copy(r, s).then_inc(s_mx, 1)
                        else:
                            dve.wait_ge(s_mx, base + j - 1)
                            dve.tensor_tensor(r, s, r, ALU.max).then_inc(s_mx, 1)

                    for u in range(STEP):
                        tile(0, u, True)
                    with dve.Fori(1, STEPS) as i:
                        for u in range(STEP):
                            tile(i, u, False)
                    dve.wait_ge(s_scc, base + TILES)
                    dve.wait_ge(s_mx, base + KT - 1)
                    dve.tensor_tensor(RM[0:TAIL, 0, :], BIG[0:TAIL, KT * HALF:(KT + 1) * HALF], RM[0:TAIL, 0, :],
                                      ALU.max).then_inc(s_mx, 1)
                    dve.wait_ge(s_mx, base + TILES)
                    dve.tensor_tensor(RM[:, 0, :], RM[:, 0, :], RM[:, 1, :], ALU.max).then_inc(s_mxf, 1)
                    dve.wait_ge(s_mt, n + 1)
                    dve.tensor_reduce(MX[:, :], PS[:, 7, :].rearrange("p (k q) -> p k q", q=P), AX.X,
                                      ALU.max).then_inc(s_mr, 1)
                    cb = CB[:, h * HT:(h + 1) * HT]
                    dve.wait_ge(s_mr, 3 * n + 1)
                    dve.tensor_tensor(MC[:, :], MX[:, :], cb, ALU.add).then_inc(s_mr, 1)
                    dve.wait_ge(s_mr, 3 * n + 2)
                    dve.tensor_tensor(MX[:, :], MC[:, :], cb, ALU.subtract).then_inc(s_mr, 1)
                    dve.wait_ge(s_mr, 3 * n + 3)
                    for k in range(HT):
                        dve.tensor_scalar(DG[:, k, :], ident[:, :], MX[:, k:k + 1], None, ALU.mult).then_inc(s_dg, 1)

        def value_stage(h):
            n = xc["half"]
            base = n * TILES
            lots = n * 2 * STEPS
            with nc.Block() as block:
                @block.sync
                def _(sp):
                    def lot(i, k, first):
                        if not first:
                            sp.wait_ge(s_pv, base + (i - 1) * STEP + (k + 1) * RING)
                        src = ctx_main[:, bass.ds(i * STEP + k * RING, RING), :]
                        sp.dma_start(VR[:, k * RING:(k + 1) * RING, :], src).then_inc(s_va if k == 0 else s_vb, 16)

                    lot(0, 0, True)
                    lot(0, 1, True)
                    with sp.Fori(1, STEPS) as i:
                        lot(i, 0, False)
                        lot(i, 1, False)

                @block.vector
                def _(dve):
                    def shift(i, u):
                        s = BIG[:, bass.ds((i * STEP + u) * HALF, HALF)]
                        dve.tensor_tensor(s, s, PS[:, 6, :], ALU.subtract).then_inc(s_sub, 1)

                    def add(i, u, first):
                        k = DVE_SUMS.index(u)
                        j = i * STEP + u
                        before = (n * STEPS + i) * len(DVE_SUMS) + k
                        dve.wait_ge(s_pr, base + j + 1)
                        l, s = LS[:, 0, :], BIG[:, bass.ds(j * HALF, HALF)]
                        if first and k == 0:
                            dve.tensor_copy(l, s).then_inc(s_sv, 1)
                        else:
                            dve.wait_ge(s_sv, before)
                            dve.tensor_tensor(l, s, l, ALU.add).then_inc(s_sv, 1)

                    def step(i, first):
                        for u in range(STEP):
                            shift(i, u)
                            if u - 2 in DVE_SUMS:
                                add(i, u - 2, first)
                        for u in DVE_SUMS:
                            if u + 2 >= STEP:
                                add(i, u, first)

                    step(0, True)
                    with dve.Fori(1, STEPS) as i:
                        step(i, False)
                    s = BIG[0:TAIL, KT * HALF:(KT + 1) * HALF]
                    dve.tensor_tensor(s, s, PS[0:TAIL, 6, :], ALU.subtract).then_inc(s_sub, 1)
                    dve.wait_ge(s_pv, base + TILES)
                    dve.tensor_copy(OT[:, h * HALF:(h + 1) * HALF], PS[:, 5, :]).then_inc(s_ot, 1)
                    dve.wait_ge(s_l, n + 1)
                    dve.reciprocal(RL[:, h * HT:(h + 1) * HT], PS[:, 7, h * HT:(h + 1) * HT]).then_inc(s_rl, 1)

                @block.scalar
                def _(act):
                    with act.Fori(0, STEPS) as i:
                        for u in range(STEP):
                            j = i * STEP + u
                            act.wait_ge(s_sub, base + j + 1)
                            s = BIG[:, bass.ds(j * HALF, HALF)]
                            act.activation(s, s, ACT.Exp).then_inc(s_pr, 1)
                    act.wait_ge(s_sub, base + TILES)
                    s = BIG[0:TAIL, KT * HALF:(KT + 1) * HALF]
                    act.activation(s, s, ACT.Exp).then_inc(s_pr, 1)

                @block.gpsimd
                def _(pool):
                    sums = len(POOL_SUMS)
                    per = n * (STEPS * sums + 1)

                    def step(i, first):
                        for k, u in enumerate(POOL_SUMS):
                            j = i * STEP + u
                            l, s = LS[:, 1, :], BIG[:, bass.ds(j * HALF, HALF)]
                            pool.wait_ge(s_pr, base + j + 1)
                            if first and k == 0:
                                pool.tensor_copy(l, s).then_inc(s_sp, 1)
                            else:
                                pool.wait_ge(s_sp, per + i * sums + k)
                                pool.tensor_tensor(l, s, l, ALU.add).then_inc(s_sp, 1)

                    step(0, True)
                    with pool.Fori(1, STEPS) as i:
                        step(i, False)
                    pool.wait_ge(s_pr, base + TILES)
                    pool.wait_ge(s_sp, per + STEPS * sums)
                    l = LS[0:TAIL, 1, :]
                    pool.tensor_tensor(l, BIG[0:TAIL, KT * HALF:(KT + 1) * HALF], l, ALU.add).then_inc(s_sp, 1)

                @block.tensor
                def _(pe):
                    def step(i, first):
                        for u in range(STEP):
                            j = i * STEP + u
                            if u % RING == 0:
                                pe.wait_ge(s_va if u == 0 else s_vb, 16 * (lots // 2 + 1) + 16 * i)
                            pe.wait_ge(s_pr, base + j + 1)
                            pe.matmul(PS[:, 5, :], VR[:, u, :], BIG[:, bass.ds(j * HALF, HALF)],
                                      start=(first and u == 0), stop=False,
                                      skip_group_check=True).then_inc(s_pv, 1)

                    step(0, True)
                    with pe.Fori(1, STEPS) as i:
                        step(i, False)
                    pe.wait_ge(s_pr, base + TILES)
                    pe.matmul(PS[:, 5, :], VTAIL[:, :], BIG[0:TAIL, KT * HALF:(KT + 1) * HALF], start=False,
                              stop=True, skip_group_check=True).then_inc(s_pv, 1)
                    pe.wait_ge(s_sv, (n + 1) * STEPS * len(DVE_SUMS))
                    pe.wait_ge(s_sp, (n + 1) * (STEPS * len(POOL_SUMS) + 1))
                    for k in range(HT):
                        for e in range(2):
                            mm = pe.matmul(PS[:, 7, h * HT + k:h * HT + k + 1], LS[:, e, k * P:(k + 1) * P],
                                           ONES[:, 0:1], start=(e == 0), stop=(e == 1))
                    mm.then_inc(s_l, 1)
            xc["half"] += 1

        def mix_stage(w_value):
            n = xc["n"]
            with nc.Block() as block:
                @block.tensor
                def _(pe):
                    for t in range(TT):
                        pe.matmul(PS[:, t // HT, (t % HT) * P:(t % HT + 1) * P], OT[:, t * P:(t + 1) * P],
                                  w_value, start=True, stop=True).then_inc(s_on, 1)

                @block.vector
                def _(dve):
                    for t in range(TT):
                        dve.wait_ge(s_on, n * TT + (t // HT + 1) * HT)
                        dve.tensor_scalar(NAT[:, t, :], PS[:, t // HT, (t % HT) * P:(t % HT + 1) * P],
                                          RL[:, t:t + 1], None, ALU.mult).then_inc(s_of, 1)
            xc["n"] += 1

        norm_stage(X, XN, 1e-5)
        query_stage(W["L0_xattn_Wq"][:, :], C["L0_xattn_bq"][:, 0:1], W["xwk_t"][:, :], C["L0_xattn_bk"][:, 0:1])
        for h in range(2):
            score_stage(h)
            value_stage(h)
        mix_stage(W["L0_xattn_Wv"][:, :])

        s_ew = sem("elementwise_chain")
        ew = {"n": 0}

        def elementwise_stage(ops):
            with nc.Block() as block:
                @block.vector
                def _(dve):
                    for o, i0, i1, op in ops:
                        if ew["n"]:
                            dve.wait_ge(s_ew, ew["n"])
                        dve.tensor_tensor(o, i0, i1, op).then_inc(s_ew, 1)
                        ew["n"] += 1

        def over_tokens(row):
            return row[:, :].unsqueeze(1).broadcast_to([P, TT, P])

        N3, X3, XN3 = NAT[:, :, :], X[:, :, :], XN[:, :, :]
        elementwise_stage([(N3, N3, over_tokens(R["L0_xattn_bv"]), ALU.add), (N3, N3, XN3, ALU.add)])
        norm_stage(NAT, NAT, 1e-5, turn=False)
        elementwise_stage([(N3, N3, over_tokens(R["L0_xattn_gamma"]), ALU.mult),
                           (N3, N3, over_tokens(R["L0_xattn_beta"]), ALU.add), (X3, X3, N3, ALU.add)])

        s_fa, s_fac, s_fm, s_fmc = (sem(n) for n in ("mix_parts", "mix_parts_copied", "mix_matrix", "mix_matrix_copied"))
        with nc.Block() as block:
            @block.tensor
            def _(pe):
                pe.matmul(PS[:, 0, 0:P], W["wr"][:, :], W["cos"][:, :], start=True, stop=False)
                pe.matmul(PS[:, 0, 0:P], W["wi"][:, :], W["sin"][:, :], start=False, stop=True).then_inc(s_fa, 1)
                pe.matmul(PS[:, 1, 0:P], W["wi"][:, :], W["cos"][:, :], start=True, stop=False)
                pe.matmul(PS[:, 1, 0:P], W["wr"][:, :], W["nsin"][:, :], start=False, stop=True).then_inc(s_fa, 1)
                pe.wait_ge(s_fac, 2)
                pe.matmul(PS[:, 2, 0:P], AMT[:, 0, :], W["cos"][:, :], start=True, stop=False)
                pe.matmul(PS[:, 2, 0:P], AMT[:, 1, :], W["nsin"][:, :], start=False, stop=True).then_inc(s_fm, 1)

            @block.scalar
            def _(act):
                for k in range(2):
                    act.wait_ge(s_fa, k + 1)
                    act.activation(AMT[:, k, :], PS[:, k, 0:P], ACT.Copy).then_inc(s_fac, 1)
                act.wait_ge(s_fm, 1)
                act.activation(MIX[:, :], PS[:, 2, 0:P], ACT.Copy, scale=1.0 / P).then_inc(s_fmc, 1)

        norm_stage(X, XN, 1e-5)
        linear_stage(MIX[:, :], R["L0_ffn_bias"][:, :], False)

        norm_stage(X, XN, 1e-5)
        QT = work(0, GROUPS, TOKENS)
        KTT = work(4096, GROUPS, TOKENS)
        VA = work(8192, TT, HALF)
        NM = work(12288, TT, GROUPS, P)
        AT = work(16384, GROUPS, TOKENS)
        PB = sb("PB", [P, 4, 2, HALF])
        WS = work(20480, 3, HALF)
        WOG = work(20480 + 3 * HALF, GROUPS, P)
        VONE = work(20480 + 4 * HALF, HALF)
        MXC = sb("MXC", [P, TT * HEADS, 2])
        MXR = sb("MXR", [P, TT * HEADS])
        s_cw, s_cp, s_cpc, s_nmz = (sem(n) for n in ("causal_weights", "causal_projected", "causal_kept", "causal_cleared"))
        with nc.Block() as block:
            @block.sync
            def _(sp):
                sp.dma_start(WS, a["causal_qkv"]).then_inc(s_cw, 16)
                sp.dma_start(WOG, a["causal_o"]).then_inc(s_cw, 16)
                sp.dma_start(VONE, a["v_one"].partition_broadcast(P)).then_inc(s_cw, 16)
                sp.wait_ge(s_cw, 48)

            @block.gpsimd
            def _(pool):
                pool.memset(NM, 0.0).then_inc(s_nmz, 1)
                pool.memset(MXC[:, :, :], MASKED).then_inc(s_nmz, 1)

            def units():
                for k in range(2):
                    for g in range(GROUPS):
                        for h in range(2):
                            yield k, g, h
                for t in range(TT):
                    yield 2, t, 0

            UNITS = list(units())

            @block.tensor
            def _(pe):
                pe.wait_ge(s_cw, 48)
                for u, (k, g, h) in enumerate(UNITS):
                    if u >= 8:
                        pe.wait_ge(s_cpc, u - 7)
                    if k < 2:
                        pe.matmul(PS[:, u % 8, :], WS[:, k, g * P:(g + 1) * P], XT[:, h * HALF:(h + 1) * HALF],
                                  start=True, stop=True).then_inc(s_cp, 1)
                    else:
                        pe.matmul(PS[:, u % 8, :], XT[:, g * P:(g + 1) * P], WS[:, 2, :], start=True,
                                  stop=True).then_inc(s_cp, 1)

            @block.scalar
            def _(act):
                for u, (k, g, h) in enumerate(UNITS):
                    if k == 2:
                        continue
                    act.wait_ge(s_cp, u + 1)
                    dst = (QT if k == 0 else KTT)[:, g, h * HALF:(h + 1) * HALF]
                    act.activation(dst, PS[:, u % 8, :], ACT.Identity,
                                   bias=0.0 if k == 0 else C["ones_row"][:, 0:1]).then_inc(s_cpc, 1)

            @block.vector
            def _(dve):
                dve.wait_ge(s_cw, 48)
                for u, (k, g, h) in enumerate(UNITS):
                    if k < 2:
                        continue
                    dve.wait_ge(s_cp, u + 1)
                    dve.wait_ge(s_cpc, u)
                    dve.tensor_tensor(VA[:, g, :], PS[:, u % 8, :], VONE, ALU.add).then_inc(s_cpc, 1)

        s_c1, s_c1m, s_c1r, s_c1n, s_c1t, s_c1q = (sem(n) for n in (
            "causal_rows", "causal_row_max", "causal_row_max_joined", "causal_negative_max", "causal_max_turned",
            "causal_q_with_max"))
        PASS1 = [(g, t, c) for g in range(GROUPS) for t in range(TT) for c in range(t // HT + 1)]
        with nc.Block() as block:
            @block.tensor
            def _(pe):
                for u, (g, t, c) in enumerate(PASS1):
                    n = min(HALF, (t + 1) * P - c * HALF)
                    diagonal = c == t // HT
                    if u >= 2:
                        pe.wait_ge(s_c1m, u - 1)
                    b = 4 * (u % 2)
                    if diagonal:
                        for i in range(HPG):
                            pe.matmul(PS[:, b + i, n - P:n], IDB[:, :], MASKN[:, :], start=True, stop=False,
                                      skip_group_check=True)
                    for i in range(HPG):
                        rows = slice(STRIP * i, STRIP * (i + 1))
                        mm = pe.matmul(PS[:, b + i, 0:n], QT[rows, g, t * P:(t + 1) * P],
                                       KTT[rows, g, c * HALF:c * HALF + n], start=not diagonal, stop=True,
                                       skip_group_check=True)
                    mm.then_inc(s_c1, 1)
                for g in range(GROUPS):
                    for t in range(TT):
                        if g == 0 and t == 0:
                            pe.wait_ge(s_c1n, 1)
                        mm = pe.transpose(PS[:, 2 * g + t // HT, (t % HT) * P:(t % HT + 1) * P], NM[:, t, g, :],
                                          ident[:, :])
                        if t % HT == HT - 1:
                            mm.then_inc(s_c1t, 1)

            @block.vector
            def _(dve):
                for u, (g, t, c) in enumerate(PASS1):
                    n = min(HALF, (t + 1) * P - c * HALF)
                    k = t * HEADS + g * HPG
                    dve.wait_ge(s_c1, u + 1)
                    b = 4 * (u % 2)
                    dve.tensor_reduce(MXC[:, k:k + HPG, c], PS[:, b:b + HPG, 0:n], AX.X, ALU.max).then_inc(s_c1m, 1)
                dve.wait_ge(s_c1m, len(PASS1))
                dve.tensor_reduce(MXR[:, :], MXC[:, :, :], AX.X, ALU.max).then_inc(s_c1r, 1)
                dve.wait_ge(s_c1r, 1)
                dve.tensor_scalar(NM.rearrange("p t g (i s) -> p (t g i) s", s=STRIP)[:, :, HD], MXR[:, :], -1.0,
                                  None, ALU.mult).then_inc(s_c1n, 1)
                for g in range(GROUPS):
                    for h in range(2):
                        dve.wait_ge(s_c1t, 2 * g + h + 1)
                        q = QT[:, g, h * HALF:(h + 1) * HALF]
                        dve.tensor_tensor(q, PS[:, 2 * g + h, :], q, ALU.add).then_inc(s_c1q, 1)

        s_c2, s_c2e, s_c2v, s_c2a = (sem(n) for n in ("causal_scores", "causal_probs", "causal_mixed", "causal_mix_kept"))
        PASS2 = []
        for g in range(GROUPS):
            for h in range(2):
                for k in range((h + 1) * HT):
                    for pair in range(2):
                        PASS2.append((g, h, k, pair))
        LAG = 2
        with nc.Block() as block:
            def columns(h, k):
                first = max(0, k * P - h * HALF)
                return first, HALF - first

            @block.tensor
            def _(pe):
                for u in range(len(PASS2) + LAG):
                    if u < len(PASS2):
                        g, h, k, pair = PASS2[u]
                        first, n = columns(h, k)
                        diagonal = k * P >= h * HALF
                        if u >= 3:
                            pe.wait_ge(s_c2e, u - 2)
                        b = 2 * (u % 3)
                        if diagonal:
                            for i in range(2):
                                pe.matmul(PS[:, b + i, 0:P], IDB[:, :], MASKT[:, :], start=True, stop=False,
                                          skip_group_check=True)
                        for i in range(2):
                            rows = slice(STRIP * (2 * pair + i), STRIP * (2 * pair + i + 1))
                            mm = pe.matmul(PS[:, b + i, 0:n], KTT[rows, g, k * P:(k + 1) * P],
                                           QT[rows, g, h * HALF + first:(h + 1) * HALF], start=not diagonal,
                                           stop=True, skip_group_check=True)
                        mm.then_inc(s_c2, 1)
                    v = u - LAG
                    if v >= 0:
                        g, h, k, pair = PASS2[v]
                        first, n = columns(h, k)
                        gh = 2 * g + h
                        if k == 0 and pair == 0 and gh >= 2:
                            pe.wait_ge(s_c2a, gh - 1)
                        pe.wait_ge(s_c2e, v + 1)
                        for i in range(2):
                            j = 2 * pair + i
                            head = g * HPG + j
                            mm = pe.matmul(PS[STRIP * j:STRIP * (j + 1), 6 + gh % 2, first:HALF],
                                           VA[:, k, head * STRIP:(head + 1) * STRIP], PB[:, v % 4, i, 0:n],
                                           start=(k == 0), stop=(k == (h + 1) * HT - 1), skip_group_check=True)
                        mm.then_inc(s_c2v, 1)

            @block.scalar
            def _(act):
                for u, (g, h, k, pair) in enumerate(PASS2):
                    first, n = columns(h, k)
                    act.wait_ge(s_c2, u + 1)
                    if u >= 4:
                        act.wait_ge(s_c2v, u - 3)
                    b = 2 * (u % 3)
                    act.activation(PB[:, u % 4, :, 0:n], PS[:, b:b + 2, 0:n], ACT.Exp,
                                   scale=float(HD) ** -0.5).then_inc(s_c2e, 1)

            @block.vector
            def _(dve):
                done = 0
                for gh in range(2 * GROUPS):
                    done += 2 * (gh % 2 + 1) * HT
                    dve.wait_ge(s_c2v, done)
                    dve.tensor_copy(AT[:, gh // 2, (gh % 2) * HALF:(gh % 2 + 1) * HALF],
                                    PS[:, 6 + gh % 2, :]).then_inc(s_c2a, 1)

        s_cs, s_cr, s_ca, s_co, s_cx = (sem(n) for n in (
            "causal_sums_spread", "causal_recip", "causal_divided", "causal_out", "causal_added"))
        RB = work(0, 2, HALF)
        with nc.Block() as block:
            @block.tensor
            def _(pe):
                for u in range(2 * GROUPS):
                    pe.matmul(PS[:, u, :], W["strip_sum"][:, :], AT[:, u // 2, (u % 2) * HALF:(u % 2 + 1) * HALF],
                              start=True, stop=True).then_inc(s_cs, 1)
                pe.wait_ge(s_ca, 2 * GROUPS)
                for t in range(TT):
                    for g in range(GROUPS):
                        mm = pe.matmul(PS[:, t // HT, (t % HT) * P:(t % HT + 1) * P], AT[:, g, t * P:(t + 1) * P],
                                       WOG[:, g, :], start=(g == 0), stop=(g == GROUPS - 1))
                    mm.then_inc(s_co, 1)

            @block.vector
            def _(dve):
                for u in range(2 * GROUPS):
                    dve.wait_ge(s_cs, u + 1)
                    if u >= 2:
                        dve.wait_ge(s_ca, u - 1)
                    dve.reciprocal(RB[:, u % 2, :], PS[:, u, :]).then_inc(s_cr, 1)
                    dve.wait_ge(s_cr, u + 1)
                    v = AT[:, u // 2, (u % 2) * HALF:(u % 2 + 1) * HALF]
                    dve.tensor_tensor(v, v, RB[:, u % 2, :], ALU.mult).then_inc(s_ca, 1)
                for h in range(2):
                    dve.wait_ge(s_co, (h + 1) * HT)
                    v = X[:, h * HT:(h + 1) * HT, :]
                    dve.tensor_tensor(v, PS[:, h, :].rearrange("p (t d) -> p t d", d=P), v, ALU.add).then_inc(s_cx, 1)

        norm_stage(X, XN, 1e-5)
        query_stage(W["w1x_t"][:, :], C["L1_xattn_b"][:, 0:1], W["L1_xattn_W"][:, :], C["L1_xattn_b"][:, 0:1])
        for h in range(2):
            score_stage(h)
            value_stage(h)
        mix_stage(ident[:, :])
        elementwise_stage([(X3, X3, N3, ALU.add)])

        norm_stage(X, XN, 1e-5)
        ACC = work(0, TT, P)
        HID = work(1024, 2, HC, HALF)
        W1S = work(5120, 2, HIDDEN)
        W2S = work(6144, 2, HC, P)
        B1S = work(7168, 2, HC)
        B2 = work(7232, P)
        GW = work(7360, EXPERTS)
        LG = work(7424, TT, EXPERTS)
        G1 = work(7488, TT, EXPERTS, EXPERTS)
        G2 = work(8000, TT, EXPERTS, EXPERTS)
        LOW = work(8512, EXPERTS, EXPERTS)
        RK = work(8576, TT, EXPERTS)
        S8 = work(8640, TT)
        CMB = work(8704, TT, EXPERTS)
        CMT = work(8768, TOKENS)
        s_gw, s_gl, s_gc, s_ge, s_ct, s_ctc, s_sg, s_b2 = (sem(n) for n in (
            "gate_loaded", "gate_logits", "gate_chain", "gate_exp", "combine_turned", "combine_kept",
            "shared_gelu", "bias_mixed"))
        with nc.Block() as block:
            @block.sync
            def _(sp):
                sp.dma_start(B2[0:EXPERTS, :], a["L1_ffn_b2"]).then_inc(s_gw, 16)
                sp.dma_start(GW, a["L1_ffn_gate_W"]).then_inc(s_gw, 16)
                sp.dma_start(LOW.rearrange("p a b -> p (a b)"), a["lower"].partition_broadcast(P)).then_inc(s_gw, 16)
                sp.wait_ge(s_gw, 48)

            @block.tensor
            def _(pe):
                pe.wait_ge(s_gw, 48)
                for t in range(TT):
                    mm = pe.matmul(PS[:, 0, t * EXPERTS:(t + 1) * EXPERTS], XT[:, t * P:(t + 1) * P], GW,
                                   start=True, stop=True)
                mm.then_inc(s_gl, 1)
                for t in range(TT):
                    mm = pe.matmul(PS[:, 1 + t // HT, (t % HT) * P:(t % HT + 1) * P], XT[:, t * P:(t + 1) * P],
                                   W["L1_ffn_shared_W"][:, :], start=True, stop=True)
                mm.then_inc(s_gl, 1)
                pe.wait_ge(s_gc, 14)
                for t in range(TT):
                    mm = pe.transpose(PS[0:EXPERTS, 3 + t // HT, (t % HT) * P:(t % HT + 1) * P], CMB[:, t, :],
                                      ident[:, :])
                mm.then_inc(s_ct, 1)
                pe.wait_ge(s_ctc, 1)
                for t in range(TT):
                    mm = pe.matmul(PS[:, 5 + t // HT, (t % HT) * P:(t % HT + 1) * P],
                                   CMT[0:EXPERTS, t * P:(t + 1) * P], B2[0:EXPERTS, :], start=True, stop=True)
                mm.then_inc(s_b2, 1)

            @block.vector
            def _(dve):
                steps = [0]

                def chained(instruction):
                    instruction.then_inc(s_gc, 1)
                    steps[0] += 1

                def across(v):
                    return v.unsqueeze(2).broadcast_to([P, TT, EXPERTS])

                dve.wait_ge(s_gl, 1)
                dve.tensor_reduce(S8, PS[:, 0, 0:TT * EXPERTS].rearrange("p (t e) -> p t e", e=EXPERTS), AX.X,
                                  ALU.max).then_inc(s_gc, 1)
                dve.wait_ge(s_gc, 1)
                dve.tensor_tensor(LG, PS[:, 0, 0:TT * EXPERTS].rearrange("p (t e) -> p t e", e=EXPERTS),
                                  across(S8), ALU.subtract).then_inc(s_gc, 1)
                dve.wait_ge(s_ge, 1)
                dve.tensor_reduce(S8, LG, AX.X, ALU.add).then_inc(s_gc, 1)
                dve.wait_ge(s_gc, 3)
                dve.reciprocal(S8, S8).then_inc(s_gc, 1)
                dve.wait_ge(s_gc, 4)
                dve.tensor_tensor(LG, LG, across(S8), ALU.mult).then_inc(s_gc, 1)
                dve.wait_ge(s_gc, 5)
                mine = LG.unsqueeze(3).broadcast_to([P, TT, EXPERTS, EXPERTS])
                other = LG.unsqueeze(2).broadcast_to([P, TT, EXPERTS, EXPERTS])
                dve.tensor_tensor(G1, other, mine, ALU.is_gt).then_inc(s_gc, 1)
                dve.tensor_tensor(G2, other, mine, ALU.is_equal).then_inc(s_gc, 1)
                dve.wait_ge(s_gc, 7)
                dve.wait_ge(s_gw, 48)
                dve.tensor_tensor(G2, G2, LOW.unsqueeze(1).broadcast_to([P, TT, EXPERTS, EXPERTS]),
                                  ALU.mult).then_inc(s_gc, 1)
                dve.wait_ge(s_gc, 8)
                dve.tensor_tensor(G1, G1, G2, ALU.add).then_inc(s_gc, 1)
                dve.wait_ge(s_gc, 9)
                dve.tensor_reduce(RK, G1, AX.X, ALU.add).then_inc(s_gc, 1)
                dve.wait_ge(s_gc, 10)
                dve.scalar_tensor_tensor(out=CMB, in0=RK, scalar=1.5, in1=LG, op0=ALU.is_lt,
                                         op1=ALU.mult).then_inc(s_gc, 1)
                dve.wait_ge(s_gc, 11)
                dve.tensor_reduce(S8, CMB, AX.X, ALU.add).then_inc(s_gc, 1)
                dve.wait_ge(s_gc, 12)
                dve.reciprocal(S8, S8).then_inc(s_gc, 1)
                dve.wait_ge(s_gc, 13)
                dve.tensor_tensor(CMB, CMB, across(S8), ALU.mult).then_inc(s_gc, 1)
                dve.wait_ge(s_ct, 1)
                dve.tensor_copy(CMT[0:EXPERTS, :].rearrange("p (h q) -> p h q", h=2),
                                PS[0:EXPERTS, 3:5, :]).then_inc(s_ctc, 1)
                dve.wait_ge(s_gl, 2)
                dve.tensor_tensor(NAT[:, :, :].rearrange("p (h t) d -> p h t d", h=2),
                                  PS[:, 1:3, :].rearrange("p h (t d) -> p h t d", d=P),
                                  R["L1_ffn_shared_b"][:, :].unsqueeze(1).unsqueeze(1).broadcast_to([P, 2, HT, P]),
                                  ALU.add).then_inc(s_gc, 1)
                dve.wait_ge(s_sg, 1)
                dve.wait_ge(s_b2, 1)
                dve.scalar_tensor_tensor(out=ACC.rearrange("p t d -> p (t d)").rearrange("p (h q) -> p h q", h=2),
                                         in0=NAT[:, :, :].rearrange("p t d -> p (t d)").rearrange(
                                             "p (h q) -> p h q", h=2),
                                         scalar=0.5, in1=PS[:, 5:7, :], op0=ALU.mult, op1=ALU.add).then_inc(s_gc, 1)

            @block.scalar
            def _(act):
                act.wait_ge(s_gc, 2)
                act.activation(LG, LG, ACT.Exp).then_inc(s_ge, 1)
                act.wait_ge(s_gc, 15)
                act.activation(NAT[:, :, :], NAT[:, :, :], ACT.Gelu).then_inc(s_sg, 1)

        s_wa, s_wb, s_h, s_hg, s_y, s_acc = (sem(n) for n in (
            "expert_weights_a", "expert_weights_b", "expert_hidden", "expert_gelu", "expert_out", "expert_added"))
        PAIRS = EXPERTS // 2
        UPP = 4
        with nc.Block() as block:
            @block.sync
            def _(sp):
                def load(i, k, first):
                    if not first:
                        sp.wait_ge(s_y, HT * (UPP * (i - 1) + 2 * k + 2))
                    e = i * 2 + k
                    s = s_wa if k == 0 else s_wb
                    sp.dma_start(W1S[:, k, :], a["L1_ffn_W1"][bass.ds(e, 1), :, :].rearrange("e d h -> d (e h)")
                                 ).then_inc(s, 16)
                    sp.dma_start(W2S[:, k, :, :], a["L1_ffn_W2"][bass.ds(e, 1), :, :].rearrange(
                        "e (c p) d -> p (e c) d", p=P)).then_inc(s, 16)
                    sp.dma_start(B1S[:, k, :], a["b1_cols"][:, bass.ds(e * HC, HC)]).then_inc(s, 16)

                load(0, 0, True)
                load(0, 1, True)
                with sp.Fori(1, PAIRS) as i:
                    load(i, 0, False)
                    load(i, 1, False)

            @block.tensor
            def _(pe):
                def hidden(i, k, first):
                    slot, h = k // 2, k % 2
                    if h == 0:
                        pe.wait_ge(s_wa if slot == 0 else s_wb, 48 * i + 48)
                    for c in range(HC):
                        if not (first and k == 0):
                            pe.wait_ge(s_hg, (i * UPP + k - 1) * HC + c + 1)
                        pe.matmul(PS[:, c, :], W1S[:, slot, c * P:(c + 1) * P], XT[:, h * HALF:(h + 1) * HALF],
                                  start=True, stop=True).then_inc(s_h, 1)

                def output(i, k, early):
                    slot, h = k // 2, k % 2
                    pe.wait_ge(s_hg, (i * UPP + k + 1) * HC)
                    if not early:
                        pe.wait_ge(s_acc, (i * UPP + k - 1) * HT)
                    for t in range(HT):
                        for c in range(HC):
                            mm = pe.matmul(PS[:, 4 + k % 2, t * P:(t + 1) * P], HID[:, h, c, t * P:(t + 1) * P],
                                           W2S[:, slot, c, :], start=(c == 0), stop=(c == HC - 1))
                        mm.then_inc(s_y, 1)

                def step(i, first):
                    for k in range(UPP):
                        hidden(i, k, first)
                        if k > 0:
                            output(i, k - 1, first and k - 1 < 2)
                        elif not first:
                            output(i - 1, UPP - 1, False)

                step(0, True)
                with pe.Fori(1, PAIRS) as i:
                    step(i, False)
                output(PAIRS - 1, UPP - 1, False)

            @block.scalar
            def _(act):
                def step(i, first):
                    for k in range(UPP):
                        slot, h = k // 2, k % 2
                        if not (first and k < 2):
                            act.wait_ge(s_y, (i * UPP + k - 1) * HT)
                        for c in range(HC):
                            act.wait_ge(s_h, (i * UPP + k) * HC + c + 1)
                            act.activation(HID[:, h, c, :], PS[:, c, :], ACT.Gelu,
                                           bias=B1S[:, slot, c:c + 1]).then_inc(s_hg, 1)

                step(0, True)
                with act.Fori(1, PAIRS) as i:
                    step(i, False)

            @block.vector
            def _(dve):
                with dve.Fori(0, PAIRS) as i:
                    for k in range(UPP):
                        slot, h = k // 2, k % 2
                        dve.wait_ge(s_y, (i * UPP + k + 1) * HT)
                        for t in range(HT):
                            v = ACC[:, h * HT + t, :]
                            dve.scalar_tensor_tensor(out=v, in0=PS[:, 4 + k % 2, t * P:(t + 1) * P],
                                                     scalar=CMB[:, h * HT + t, bass.ds(i * 2 + slot, 1)], in1=v,
                                                     op0=ALU.mult, op1=ALU.add).then_inc(s_acc, 1)

        norm_stage(ACC, NAT, 1e-5, turn=False)
        elementwise_stage([(N3, N3, over_tokens(R["L1_ffn_gamma"]), ALU.mult),
                           (N3, N3, over_tokens(R["L1_ffn_beta"]), ALU.add), (X3, X3, N3, ALU.add)])
        with nc.Block() as block:
            @block.sync
            def _(sp):
                sp.dma_start(out[0].rearrange("(t p) d -> p t d", p=P), X[:, :, :]).then_inc(s_out, 16)
                sp.wait_ge(s_out, 16)


def kernel(**inputs):
    import ml_dtypes
    import numpy as np
    import concourse.bacc as bacc
    from concourse.bass_utils import run_bass_kernel_spmd

    f = {k: np.ascontiguousarray(v) for k, v in inputs.items()}
    bf16 = ml_dtypes.bfloat16

    f["xwk_t"] = f["L0_xattn_Wk"].T
    f["w1x_t"] = f["L1_xattn_W"].T
    strips = np.zeros((P, 3, HEADS, STRIP), np.float32)
    for n, w in enumerate(("L1_attn_q_proj", "L1_attn_k_proj", "L1_attn_v_proj")):
        strips[:, n, :, 0:HD] = f[w].T.reshape(P, HEADS, HD)
    f["causal_qkv"] = strips.reshape(P, 3, HEADS * STRIP)
    rows = np.zeros((HPG, STRIP, GROUPS, P), np.float32)
    rows[:, 0:HD] = f["L1_attn_o_proj"].T.reshape(GROUPS, HPG, HD, P).transpose(1, 2, 0, 3)
    f["causal_o"] = rows.reshape(P, GROUPS, P)
    f["b1_cols"] = f["L1_ffn_b1"].reshape(EXPERTS * HC, P).T

    k = np.arange(P)
    turn = 2.0 * np.pi * (np.outer(k, k) % P) / P
    f["ident"] = np.eye(P, dtype=np.float32)
    f["cos"] = np.cos(turn).astype(np.float32)
    f["sin"] = np.sin(turn).astype(np.float32)
    f["nsin"] = -f["sin"]
    f["blocks"] = np.kron(np.eye(HEADS), np.ones((HD, HD))).astype(np.float32)
    spread = np.zeros((P, P), np.float32)
    spread[(k // STRIP) * STRIP + HD, k] = 1.0
    f["strip_sum"] = spread
    f["ones_row"] = (k % STRIP == HD).astype(np.float32)
    f["v_one"] = (np.arange(HALF) % STRIP == HD).astype(np.float32)
    f["ident_b"] = np.eye(P).astype(bf16)
    f["mask_n"] = np.where(k[None, :] > k[:, None], MASKED, 0.0).astype(bf16)
    f["mask_t"] = np.where(k[:, None] > k[None, :], MASKED, 0.0).astype(bf16)
    e = np.arange(EXPERTS)
    f["lower"] = (e[None, :] < e[:, None]).astype(np.float32).reshape(-1)

    unused = ("L0_xattn_Wk", "L1_attn_q_proj", "L1_attn_k_proj", "L1_attn_v_proj", "L1_attn_o_proj", "L1_ffn_b1")
    nc = bacc.Bacc("TRN2", target_bir_lowering=False, num_devices=1)
    arrays, aps = {}, {}
    for name, v in f.items():
        if name in unused:
            continue
        v = np.ascontiguousarray(v)
        arrays[f"in_{name}"] = v
        aps[name] = nc.dram_tensor(f"in_{name}", v.shape, mybir.dt.from_np(v.dtype), kind="ExternalInput").ap()
    out = nc.dram_tensor("out_0", (1, TOKENS, P), F32, kind="ExternalOutput").ap()
    decoder_kernel(nc, aps, out)
    r = run_bass_kernel_spmd(nc, [arrays], core_ids=[0])
    return r.results[0]["out_0"]
```

```python
from contextlib import ExitStack

import concourse.bass as bass
from concourse import mybir

ALU = mybir.AluOpType
ACT = mybir.ActivationFunctionType
AX = mybir.AxisListType
F32 = mybir.dt.float32
F16 = mybir.dt.float16
BF16 = mybir.dt.bfloat16

P = 128
TOKENS = 1024
TT = TOKENS // P
HALF = 512
HT = HALF // P
CTX = 6404
KT = CTX // P
TAIL = CTX - KT * P
HEADS, HD = 16, 8
GROUPS = 4
HPG = HEADS // GROUPS
STRIP = 32
EXPERTS, HIDDEN = 8, 512
HC = HIDDEN // P
RING = 5
STEP = 2 * RING
MASKED = -1.0e30


def decoder_kernel(nc, a, out):
    with ExitStack() as ctx:
        def sb(name, shape, dt=F32):
            return ctx.enter_context(nc.sbuf_tensor(name, shape, dt))

        def sem(name):
            return ctx.enter_context(nc.semaphore(name))

        PS = ctx.enter_context(nc.psum_tensor("PS", [P, 8, HALF], F32))
        X = sb("X", [P, TT, P])
        XN = sb("XN", [P, TT, P])
        XT = sb("XT", [P, TOKENS])
        NAT = sb("NAT", [P, TT, P])
        BIG = sb("BIG", [P, (KT + 1) * HALF])
        CTH = sb("CTH", [P, CTX], F16)
        CTL = sb("CTL", [P, CTX], F16)
        QH = sb("QH", [P, TOKENS], F16)
        QL = sb("QL", [P, TOKENS], F16)
        VR = sb("VR", [P, STEP, P])
        VTAIL = sb("VTAIL", [TAIL, P])
        RM = sb("RM", [P, 2, HALF])
        LS = sb("LS", [P, 2, HALF])
        OT = sb("OT", [P, TOKENS])
        DG = sb("DG", [P, HT, P])
        MX = sb("MX", [P, HT])
        MC = sb("MC", [P, HT])
        RL = sb("RL", [P, TT])
        ST = sb("ST", [P, TT, 6])
        MV = sb("MV", [P, TT, 2])
        VE = sb("VE", [P, TT])
        RS = sb("RS", [P, TT])
        NEGHALF = sb("NEGHALF", [P, TT])
        ONES = sb("ONES", [P, P])
        SQ = ["ident", "cos", "sin", "nsin", "blocks", "wqc_t", "wkc_t", "wvc_t", "woc_t", "L0_attn_Wq", "L0_attn_Wk", "L0_attn_Wv",
              "wfb_f", "wfb_r", "L0_attn_Wo", "L0_xattn_Wq", "xwk_t", "L0_xattn_Wv",
              "wr", "wi", "w1x_t", "L1_xattn_W", "L1_ffn_shared_W"]
        W = {n: sb("w_" + n, [P, P]) for n in SQ}
        SQ_SRC = {"wfb_f": a["L0_attn_Wfb"][0:P, :], "wfb_r": a["L0_attn_Wfb"][P:2 * P, :],
                  "wr": a["L0_ffn_w_freq_real"], "wi": a["L0_ffn_w_freq_imag"]}
        COLS = ["L0_attn_bq", "L0_attn_bk", "L0_attn_bv", "L0_attn_g1", "L0_attn_b1", "L0_attn_g2", "L0_attn_b2",
                "L0_xattn_bq", "L0_xattn_bk", "L1_xattn_b"]
        C = {n: sb("c_" + n, [P, 1]) for n in COLS}
        ROWS = ["L0_attn_bfb", "L0_attn_bo", "L0_xattn_bv", "L0_xattn_gamma", "L0_xattn_beta", "L0_ffn_bias",
                "L1_ffn_shared_b", "L1_ffn_gamma", "L1_ffn_beta"]
        R = {n: sb("r_" + n, [P, P]) for n in ROWS}
        MIX = sb("MIX", [P, P])
        AMT = sb("AMT", [P, 2, P])
        IDB = sb("IDB", [P, P], BF16)
        MASKN = sb("MASKN", [P, P], BF16)
        MASKT = sb("MASKT", [P, P], BF16)

        def work(at, *shape):
            n = 1
            for s in shape:
                n *= s
            v = BIG[:, at:at + n]
            if len(shape) == 2:
                return v.rearrange("p (a b) -> p a b", b=shape[1])
            if len(shape) == 3:
                return v.rearrange("p (a b c) -> p a b c", b=shape[1], c=shape[2])
            return v

        ident = W["ident"]

        s_x, s_sq, s_vec, s_mask, s_ctx, s_out = (sem(n) for n in (
            "x_loaded", "squares_loaded", "vectors_loaded", "masks_loaded", "context_loaded", "out_stored"))
        s_const = sem("constants_set")
        s_stats, s_aggr, s_var, s_rstd, s_normed, s_turned, s_xt = (sem(n) for n in (
            "norm_stats", "norm_aggregated", "norm_variance", "norm_rstd", "norm_applied", "norm_turned", "norm_xt"))
        s_ctx_turned, s_ctx_hi, s_ctx_lo = sem("context_turned"), sem("context_high"), sem("context_low")

        calls = {"norm": 0}

        def norm_stage(src, dst, eps, scale=1.0, bias=0.0, turn=True):
            n = calls["norm"]
            calls["norm"] += 1
            turns = calls.setdefault("turns", 0)
            if turn:
                calls["turns"] += 1
            with nc.Block() as block:
                @block.vector
                def _(dve):
                    for t in range(TT):
                        dve.bn_stats(ST[:, t, :], src[:, t, :]).then_inc(s_stats, 1)
                    for t in range(TT):
                        dve.wait_ge(s_stats, n * TT + t + 1)
                        dve.bn_aggr(MV[:, t, :], ST[:, t, :]).then_inc(s_aggr, 1)
                    dve.wait_ge(s_aggr, (n + 1) * TT)
                    dve.tensor_scalar(VE[:, :], MV[:, :, 1], eps, None, ALU.add).then_inc(s_var, 1)
                    dve.wait_ge(s_rstd, n + 1)
                    for t in range(TT):
                        dve.tensor_scalar(dst[:, t, :], src[:, t, :], MV[:, t, 0:1], RS[:, t:t + 1],
                                          ALU.subtract, ALU.mult).then_inc(s_normed, 1)

                @block.gpsimd
                def _(pool):
                    pool.wait_ge(s_var, n + 1)
                    pool.tensor_tensor(RS[:, :], VE[:, :], NEGHALF[:, :], ALU.pow).then_inc(s_rstd, 1)

                if turn:
                    @block.tensor
                    def _(pe):
                        for t in range(TT):
                            pe.wait_ge(s_normed, n * TT + t + 1)
                            pe.transpose(PS[:, t // HT, (t % HT) * P:(t % HT + 1) * P], dst[:, t, :],
                                         ident[:, :]).then_inc(s_turned, 1)

                    @block.scalar
                    def _(act):
                        for h in range(2):
                            act.wait_ge(s_turned, turns * TT + (h + 1) * HT)
                            act.activation(XT[:, h * HALF:(h + 1) * HALF], PS[:, h, :], ACT.Identity,
                                           bias=bias, scale=scale).then_inc(s_xt, 1)

        CN = work(0, KT, P)
        ctx_main = a["ctx_1024"][0, 0:KT * P, :].rearrange("(p t) d -> p t d", t=KT)
        ctx_tail = a["ctx_1024"][0, KT * P:CTX, :]

        with nc.Block() as block:
            @block.sync
            def _(sp):
                sp.dma_start(X[:, :, :], a["x"][0].rearrange("(t p) d -> p t d", p=P)).then_inc(s_x, 16)
                for n in SQ:
                    src = SQ_SRC.get(n, a.get(n))
                    sp.dma_start(W[n][:, :], src).then_inc(s_sq, 16)
                sp.dma_start(IDB[:, :], a["ident_b"]).then_inc(s_mask, 16)
                sp.dma_start(MASKN[:, :], a["mask_n"]).then_inc(s_mask, 16)
                sp.dma_start(MASKT[:, :], a["mask_t"]).then_inc(s_mask, 16)
                sp.wait_ge(s_x, 16)
                sp.wait_ge(s_sq, 16 * len(SQ))

            @block.scalar
            def _(act):
                for n in COLS:
                    act.dma_start(C[n][:, :], a[n].rearrange("(p o) -> p o", o=1)).then_inc(s_vec, 16)
                for n in ROWS:
                    act.dma_start(R[n][:, :], a[n].partition_broadcast(P)).then_inc(s_vec, 16)
                act.dma_start(CN, ctx_main).then_inc(s_ctx, 16)
                act.dma_start(VTAIL[:, :], ctx_tail).then_inc(s_ctx, 16)
                act.wait_ge(s_vec, 16 * (len(COLS) + len(ROWS)))

            @block.gpsimd
            def _(pool):
                pool.memset(NEGHALF[:, :], -0.5).then_inc(s_const, 1)
                pool.memset(ONES[:, :], 1.0).then_inc(s_const, 1)

        norm_stage(X, XN, 1e-5, turn=False)
        norm_stage(XN, XN, 1e-6, scale=C["L0_attn_g1"][:, 0:1], bias=C["L0_attn_b1"][:, 0:1])

        PADW = TOKENS + 4
        CW = (TOKENS + 2) // 3
        at = KT * P
        LQ, LK, LV = (work(at + i * PADW, PADW) for i in range(3))
        at += 3 * PADW
        PR = work(at, 3, TOKENS + 2)
        at += 3 * (TOKENS + 2)
        LM = work(at, TOKENS + 2)
        LA = work(at + TOKENS + 2, TOKENS + 2)
        s_lp, s_lq, s_pad, s_prod, s_lsc, s_lev, s_lch, s_lexp, s_la, s_lz, s_lzc = (sem(n) for n in (
            "local_projected", "local_qkv", "local_padded", "local_products", "local_scores", "local_evacuated",
            "local_chain", "local_exp", "local_out", "local_joined", "local_join_copied"))
        with nc.Block() as block:
            @block.tensor
            def _(pe):
                for i, w in enumerate(("L0_attn_Wq", "L0_attn_Wk", "L0_attn_Wv")):
                    for h in range(2):
                        pe.matmul(PS[:, 2 * i + h, :], W[w][:, :], XT[:, h * HALF:(h + 1) * HALF],
                                  start=True, stop=True).then_inc(s_lp, 1)
                for j in range(3):
                    pe.wait_ge(s_prod, j + 1)
                    for c in range(3):
                        n = 3 * j + c
                        pe.wait_ge(s_lq, 6)
                        if n >= 6:
                            pe.wait_ge(s_lev, n - 5)
                        pe.matmul(PS[:, n % 6, 0:CW], W["blocks"][:, :], PR[:, j, c * CW:(c + 1) * CW],
                                  start=True, stop=True).then_inc(s_lsc, 1)
                pe.wait_ge(s_la, 1)
                pe.wait_ge(s_lev, 9)
                for t in range(TT):
                    o = PS[:, t // HT, (t % HT) * P:(t % HT + 1) * P]
                    pe.matmul(o, LA[:, t * P:(t + 1) * P], W["wfb_f"][:, :], start=True, stop=False)
                    pe.matmul(o, LA[:, t * P + 2:(t + 1) * P + 2], W["wfb_r"][:, :], start=False, stop=False)
                    pe.matmul(o, XT[:, t * P:(t + 1) * P], ident[:, :], start=False, stop=True).then_inc(s_lz, 1)

            @block.gpsimd
            def _(pool):
                for v in (LQ, LK, LV):
                    pool.memset(v[:, 0:2], 0.0).then_inc(s_pad, 1)
                    pool.memset(v[:, PADW - 2:PADW], 0.0).then_inc(s_pad, 1)

            @block.scalar
            def _(act):
                for i, (v, b) in enumerate(((LQ, "L0_attn_bq"), (LK, "L0_attn_bk"), (LV, "L0_attn_bv"))):
                    for h in range(2):
                        act.wait_ge(s_lp, 2 * i + h + 1)
                        act.activation(v[:, 2 + h * HALF:2 + (h + 1) * HALF], PS[:, 2 * i + h, :], ACT.Identity,
                                       bias=C[b][:, 0:1]).then_inc(s_lq, 1)
                for n in range(9):
                    act.wait_ge(s_lsc, n + 1)
                    act.activation(PR[:, n // 3, (n % 3) * CW:(n % 3 + 1) * CW], PS[:, n % 6, 0:CW],
                                   ACT.Copy).then_inc(s_lev, 1)
                for j in range(3):
                    act.wait_ge(s_lch, 3 + j)
                    act.activation(PR[:, j, :], PR[:, j, :], ACT.Exp, scale=float(HD) ** -0.5).then_inc(s_lexp, 1)

            @block.vector
            def _(dve):
                dve.wait_ge(s_lq, 4)
                dve.wait_ge(s_pad, 4)
                for j in range(3):
                    dve.tensor_tensor(PR[:, j, :], LQ[:, 1:PADW - 1], LK[:, j:j + TOKENS + 2],
                                      ALU.mult).then_inc(s_prod, 1)
                dve.wait_ge(s_lev, 9)
                dve.tensor_tensor(LM, PR[:, 0, :], PR[:, 1, :], ALU.max).then_inc(s_lch, 1)
                dve.wait_ge(s_lch, 1)
                dve.tensor_tensor(LM, LM, PR[:, 2, :], ALU.max).then_inc(s_lch, 1)
                dve.wait_ge(s_lch, 2)
                for j in range(3):
                    dve.tensor_tensor(PR[:, j, :], PR[:, j, :], LM, ALU.subtract).then_inc(s_lch, 1)
                dve.wait_ge(s_lexp, 3)
                dve.wait_ge(s_lch, 5)
                dve.tensor_tensor(LM, PR[:, 0, :], PR[:, 1, :], ALU.add).then_inc(s_lch, 1)
                dve.wait_ge(s_lch, 6)
                dve.tensor_tensor(LM, LM, PR[:, 2, :], ALU.add).then_inc(s_lch, 1)
                dve.wait_ge(s_lq, 6)
                dve.wait_ge(s_pad, 6)
                dve.wait_ge(s_lch, 7)
                dve.reciprocal(LM, LM).then_inc(s_lch, 1)
                for j in range(3):
                    dve.tensor_tensor(PR[:, j, :], PR[:, j, :], LV[:, j:j + TOKENS + 2], ALU.mult).then_inc(s_lch, 1)
                dve.wait_ge(s_lch, 10)
                dve.tensor_tensor(LA, PR[:, 0, :], PR[:, 1, :], ALU.add).then_inc(s_lch, 1)
                dve.wait_ge(s_lch, 12)
                dve.tensor_tensor(LA, LA, PR[:, 2, :], ALU.add).then_inc(s_lch, 1)
                dve.wait_ge(s_lch, 13)
                dve.tensor_tensor(LA, LA, LM, ALU.mult).then_inc(s_la, 1)
                for h in range(2):
                    dve.wait_ge(s_lz, (h + 1) * HT)
                    dve.tensor_tensor(NAT[:, h * HT:(h + 1) * HT, :],
                                      PS[:, h, :].rearrange("p (t d) -> p t d", d=P),
                                      R["L0_attn_bfb"][:, :].unsqueeze(1).broadcast_to([P, HT, P]),
                                      ALU.add).then_inc(s_lzc, 1)

        norm_stage(NAT, NAT, 1e-6, scale=C["L0_attn_g2"][:, 0:1], bias=C["L0_attn_b2"][:, 0:1])

        lin = {"n": 0}
        s_lin, s_linb, s_ling, s_linx, s_lwait = (sem(n) for n in ("linear_done", "linear_biased", "linear_gelu", "linear_added", "linear_weights"))

        def linear_stage(weight, bias_row, gelu):
            n = lin["n"]
            g = lin.setdefault("g", 0)
            lin["n"] += 1
            lin["g"] += int(gelu)
            with nc.Block() as block:
                @block.tensor
                def _(pe):
                    for t in range(TT):
                        pe.matmul(PS[:, t // HT, (t % HT) * P:(t % HT + 1) * P], XT[:, t * P:(t + 1) * P],
                                  weight, start=True, stop=True).then_inc(s_lin, 1)

                @block.vector
                def _(dve):
                    for h in range(2):
                        dve.wait_ge(s_lin, n * TT + (h + 1) * HT)
                        dve.tensor_tensor(NAT[:, h * HT:(h + 1) * HT, :],
                                          PS[:, h, :].rearrange("p (t d) -> p t d", d=P),
                                          bias_row.unsqueeze(1).broadcast_to([P, HT, P]),
                                          ALU.add).then_inc(s_linb, 1)
                    for h in range(2):
                        if gelu:
                            dve.wait_ge(s_ling, 2 * g + h + 1)
                        else:
                            dve.wait_ge(s_linb, 2 * n + h + 1)
                        v = X[:, h * HT:(h + 1) * HT, :]
                        dve.tensor_tensor(v, v, NAT[:, h * HT:(h + 1) * HT, :], ALU.add).then_inc(s_linx, 1)

                if gelu:
                    @block.scalar
                    def _(act):
                        for h in range(2):
                            act.wait_ge(s_linb, 2 * n + h + 1)
                            v = NAT[:, h * HT:(h + 1) * HT, :]
                            act.activation(v, v, ACT.Gelu).then_inc(s_ling, 1)

        linear_stage(W["L0_attn_Wo"][:, :], R["L0_attn_bo"][:, :], True)

        LOTS = (KT + 3) // 4
        with nc.Block() as block:
            @block.tensor
            def _(pe):
                pe.wait_ge(s_ctx, 32)
                for b in range(LOTS):
                    if b >= 4:
                        pe.wait_ge(s_ctx_lo, b - 3)
                    for t in range(4 * b, min(4 * b + 4, KT)):
                        mm = pe.transpose(PS[:, b % 4, (t % 4) * P:(t % 4 + 1) * P], CN[:, t, :], ident[:, :])
                    mm.then_inc(s_ctx_turned, 1)
                pe.transpose(PS[:, 4, 0:TAIL], VTAIL[:, :], ident[0:TAIL, 0:TAIL]).then_inc(s_ctx_turned, 1)

            def part(b):
                if b < LOTS:
                    w = min(4 * P, KT * P - 4 * b * P)
                    return PS[:, b % 4, 0:w], slice(4 * b * P, 4 * b * P + w)
                return PS[:, 4, 0:TAIL], slice(KT * P, CTX)

            @block.scalar
            def _(act):
                for b in range(LOTS + 1):
                    src, cols = part(b)
                    act.wait_ge(s_ctx_turned, b + 1)
                    act.activation(CTH[:, cols], src, ACT.Copy).then_inc(s_ctx_hi, 1)

            @block.vector
            def _(dve):
                for b in range(LOTS + 1):
                    src, cols = part(b)
                    dve.wait_ge(s_ctx_hi, b + 1)
                    dve.tensor_tensor(CTL[:, cols], src, CTH[:, cols], ALU.subtract).then_inc(s_ctx_lo, 1)

        s_q, s_qs, s_qf, s_qh, s_ql, s_cb, s_cbs = (sem(n) for n in (
            "cross_q", "cross_q_biased", "cross_q_folded", "cross_q_high", "cross_q_low", "cross_key_bias", "cross_key_bias_kept"))
        s_sc, s_scc, s_mx, s_mxf, s_mt, s_mr, s_dg, s_mb = (sem(n) for n in (
            "cross_scores", "cross_scores_copied", "cross_max", "cross_max_joined", "cross_max_turned",
            "cross_max_rows", "cross_max_diagonal", "cross_max_spread"))
        s_sub, s_pr, s_pv, s_sv, s_sp, s_ot = (sem(n) for n in (
            "cross_shifted", "cross_probs", "cross_values", "cross_sum_vector", "cross_sum_pool", "cross_out_turned"))
        s_va, s_vb = sem("values_in_a"), sem("values_in_b")
        s_l, s_rl, s_on, s_of = sem("cross_sums"), sem("cross_sum_recip"), sem("cross_out"), sem("cross_finished")
        QF = work(KT * HALF - TOKENS, TOKENS)
        CB = sb("CB", [P, TT])
        xc = {"n": 0, "half": 0}

        def query_stage(w_query, query_bias, w_fold, key_bias):
            n = xc["n"]
            with nc.Block() as block:
                @block.tensor
                def _(pe):
                    for h in range(2):
                        pe.matmul(PS[:, h, :], w_query, XT[:, h * HALF:(h + 1) * HALF], start=True,
                                  stop=True).then_inc(s_q, 1)
                    for h in range(2):
                        pe.wait_ge(s_qs, 2 * n + h + 1)
                        pe.matmul(PS[:, 2 + h, :], w_fold, QF[:, h * HALF:(h + 1) * HALF], start=True,
                                  stop=True).then_inc(s_qf, 1)
                    for t in range(TT):
                        mm = pe.matmul(PS[:, 4, t:t + 1], QF[:, t * P:(t + 1) * P], key_bias, start=True, stop=True)
                    mm.then_inc(s_cb, 1)

                @block.scalar
                def _(act):
                    for h in range(2):
                        act.wait_ge(s_q, 2 * n + h + 1)
                        act.activation(QF[:, h * HALF:(h + 1) * HALF], PS[:, h, :], ACT.Identity,
                                       bias=query_bias).then_inc(s_qs, 1)
                    for h in range(2):
                        act.wait_ge(s_qf, 2 * n + h + 1)
                        act.activation(QH[:, h * HALF:(h + 1) * HALF], PS[:, 2 + h, :], ACT.Copy).then_inc(s_qh, 1)

                @block.vector
                def _(dve):
                    for h in range(2):
                        dve.wait_ge(s_qh, 2 * n + h + 1)
                        dve.tensor_tensor(QL[:, h * HALF:(h + 1) * HALF], PS[:, 2 + h, :],
                                          QH[:, h * HALF:(h + 1) * HALF], ALU.subtract).then_inc(s_ql, 1)
                    dve.wait_ge(s_cb, n + 1)
                    dve.tensor_copy(CB[:, :], PS[:, 4, 0:TT]).then_inc(s_cbs, 1)

        SCORE_BANKS = 5
        TILES = KT + 1
        DVE_SUMS = (1, 4, 6, 9)
        POOL_SUMS = tuple(u for u in range(STEP) if u not in DVE_SUMS)
        STEPS = KT // STEP

        def score_stage(h):
            n = xc["half"]
            base = n * TILES
            qh, ql = QH[:, h * HALF:(h + 1) * HALF], QL[:, h * HALF:(h + 1) * HALF]
            with nc.Block() as block:
                @block.tensor
                def _(pe):
                    def tile(i, u, first):
                        j = i * STEP + u
                        if not (first and u < SCORE_BANKS):
                            pe.wait_ge(s_scc, base + j - SCORE_BANKS + 1)
                        kh, kl = CTH[:, bass.ds(j * P, P)], CTL[:, bass.ds(j * P, P)]
                        o = PS[:, u % SCORE_BANKS, :]
                        pe.matmul(o, kh, qh, start=True, stop=False)
                        pe.matmul(o, kh, ql, start=False, stop=False)
                        pe.matmul(o, kl, qh, start=False, stop=True).then_inc(s_sc, 1)

                    for u in range(STEP):
                        tile(0, u, True)
                    with pe.Fori(1, STEPS) as i:
                        for u in range(STEP):
                            tile(i, u, False)
                    pe.wait_ge(s_scc, base + KT - SCORE_BANKS + 1)
                    o = PS[0:TAIL, 0, :]
                    pe.matmul(o, CTH[:, KT * P:CTX], qh, start=True, stop=False)
                    pe.matmul(o, CTH[:, KT * P:CTX], ql, start=False, stop=False)
                    pe.matmul(o, CTL[:, KT * P:CTX], qh, start=False, stop=True).then_inc(s_sc, 1)
                    pe.wait_ge(s_mxf, n + 1)
                    for k in range(HT):
                        mm = pe.transpose(PS[:, 7, k * P:(k + 1) * P], RM[:, 0, k * P:(k + 1) * P], ident[:, :])
                    mm.then_inc(s_mt, 1)
                    pe.wait_ge(s_dg, HT * (n + 1))
                    pe.matmul(PS[:, 6, :], ONES[:, :], DG[:, :, :].rearrange("p a b -> p (a b)"), start=True,
                              stop=True).then_inc(s_mb, 1)

                @block.scalar
                def _(act):
                    def tile(i, u):
                        j = i * STEP + u
                        act.wait_ge(s_sc, base + j + 1)
                        act.activation(BIG[:, bass.ds(j * HALF, HALF)], PS[:, u % SCORE_BANKS, :],
                                       ACT.Copy).then_inc(s_scc, 1)

                    with act.Fori(0, STEPS) as i:
                        for u in range(STEP):
                            tile(i, u)
                    act.wait_ge(s_sc, base + TILES)
                    act.activation(BIG[0:TAIL, KT * HALF:(KT + 1) * HALF], PS[0:TAIL, 0, :],
                                   ACT.Copy).then_inc(s_scc, 1)

                @block.vector
                def _(dve):
                    def tile(i, u, first):
                        j = i * STEP + u
                        r = RM[:, u % 2, :]
                        s = BIG[:, bass.ds(j * HALF, HALF)]
                        dve.wait_ge(s_scc, base + j + 1)
                        if first and u < 2:
                            dve.tensor_copy(r, s).then_inc(s_mx, 1)
                        else:
                            dve.wait_ge(s_mx, base + j - 1)
                            dve.tensor_tensor(r, s, r, ALU.max).then_inc(s_mx, 1)

                    for u in range(STEP):
                        tile(0, u, True)
                    with dve.Fori(1, STEPS) as i:
                        for u in range(STEP):
                            tile(i, u, False)
                    dve.wait_ge(s_scc, base + TILES)
                    dve.wait_ge(s_mx, base + KT - 1)
                    dve.tensor_tensor(RM[0:TAIL, 0, :], BIG[0:TAIL, KT * HALF:(KT + 1) * HALF], RM[0:TAIL, 0, :],
                                      ALU.max).then_inc(s_mx, 1)
                    dve.wait_ge(s_mx, base + TILES)
                    dve.tensor_tensor(RM[:, 0, :], RM[:, 0, :], RM[:, 1, :], ALU.max).then_inc(s_mxf, 1)
                    dve.wait_ge(s_mt, n + 1)
                    dve.tensor_reduce(MX[:, :], PS[:, 7, :].rearrange("p (k q) -> p k q", q=P), AX.X,
                                      ALU.max).then_inc(s_mr, 1)
                    cb = CB[:, h * HT:(h + 1) * HT]
                    dve.wait_ge(s_mr, 3 * n + 1)
                    dve.tensor_tensor(MC[:, :], MX[:, :], cb, ALU.add).then_inc(s_mr, 1)
                    dve.wait_ge(s_mr, 3 * n + 2)
                    dve.tensor_tensor(MX[:, :], MC[:, :], cb, ALU.subtract).then_inc(s_mr, 1)
                    dve.wait_ge(s_mr, 3 * n + 3)
                    for k in range(HT):
                        dve.tensor_scalar(DG[:, k, :], ident[:, :], MX[:, k:k + 1], None, ALU.mult).then_inc(s_dg, 1)

        def value_stage(h):
            n = xc["half"]
            base = n * TILES
            lots = n * 2 * STEPS
            with nc.Block() as block:
                @block.sync
                def _(sp):
                    def lot(i, k, first):
                        if not first:
                            sp.wait_ge(s_pv, base + (i - 1) * STEP + (k + 1) * RING)
                        src = ctx_main[:, bass.ds(i * STEP + k * RING, RING), :]
                        sp.dma_start(VR[:, k * RING:(k + 1) * RING, :], src).then_inc(s_va if k == 0 else s_vb, 16)

                    lot(0, 0, True)
                    lot(0, 1, True)
                    with sp.Fori(1, STEPS) as i:
                        lot(i, 0, False)
                        lot(i, 1, False)

                @block.vector
                def _(dve):
                    def shift(i, u):
                        s = BIG[:, bass.ds((i * STEP + u) * HALF, HALF)]
                        dve.tensor_tensor(s, s, PS[:, 6, :], ALU.subtract).then_inc(s_sub, 1)

                    def add(i, u, first):
                        k = DVE_SUMS.index(u)
                        j = i * STEP + u
                        before = (n * STEPS + i) * len(DVE_SUMS) + k
                        dve.wait_ge(s_pr, base + j + 1)
                        l, s = LS[:, 0, :], BIG[:, bass.ds(j * HALF, HALF)]
                        if first and k == 0:
                            dve.tensor_copy(l, s).then_inc(s_sv, 1)
                        else:
                            dve.wait_ge(s_sv, before)
                            dve.tensor_tensor(l, s, l, ALU.add).then_inc(s_sv, 1)

                    def step(i, first):
                        for u in range(STEP):
                            shift(i, u)
                            if u - 2 in DVE_SUMS:
                                add(i, u - 2, first)
                        for u in DVE_SUMS:
                            if u + 2 >= STEP:
                                add(i, u, first)

                    step(0, True)
                    with dve.Fori(1, STEPS) as i:
                        step(i, False)
                    s = BIG[0:TAIL, KT * HALF:(KT + 1) * HALF]
                    dve.tensor_tensor(s, s, PS[0:TAIL, 6, :], ALU.subtract).then_inc(s_sub, 1)
                    dve.wait_ge(s_pv, base + TILES)
                    dve.tensor_copy(OT[:, h * HALF:(h + 1) * HALF], PS[:, 5, :]).then_inc(s_ot, 1)
                    dve.wait_ge(s_l, n + 1)
                    dve.reciprocal(RL[:, h * HT:(h + 1) * HT], PS[:, 7, h * HT:(h + 1) * HT]).then_inc(s_rl, 1)

                @block.scalar
                def _(act):
                    with act.Fori(0, STEPS) as i:
                        for u in range(STEP):
                            j = i * STEP + u
                            act.wait_ge(s_sub, base + j + 1)
                            s = BIG[:, bass.ds(j * HALF, HALF)]
                            act.activation(s, s, ACT.Exp).then_inc(s_pr, 1)
                    act.wait_ge(s_sub, base + TILES)
                    s = BIG[0:TAIL, KT * HALF:(KT + 1) * HALF]
                    act.activation(s, s, ACT.Exp).then_inc(s_pr, 1)

                @block.gpsimd
                def _(pool):
                    sums = len(POOL_SUMS)
                    per = n * (STEPS * sums + 1)

                    def step(i, first):
                        for k, u in enumerate(POOL_SUMS):
                            j = i * STEP + u
                            l, s = LS[:, 1, :], BIG[:, bass.ds(j * HALF, HALF)]
                            pool.wait_ge(s_pr, base + j + 1)
                            if first and k == 0:
                                pool.tensor_copy(l, s).then_inc(s_sp, 1)
                            else:
                                pool.wait_ge(s_sp, per + i * sums + k)
                                pool.tensor_tensor(l, s, l, ALU.add).then_inc(s_sp, 1)

                    step(0, True)
                    with pool.Fori(1, STEPS) as i:
                        step(i, False)
                    pool.wait_ge(s_pr, base + TILES)
                    pool.wait_ge(s_sp, per + STEPS * sums)
                    l = LS[0:TAIL, 1, :]
                    pool.tensor_tensor(l, BIG[0:TAIL, KT * HALF:(KT + 1) * HALF], l, ALU.add).then_inc(s_sp, 1)

                @block.tensor
                def _(pe):
                    def step(i, first):
                        for u in range(STEP):
                            j = i * STEP + u
                            if u % RING == 0:
                                pe.wait_ge(s_va if u == 0 else s_vb, 16 * (lots // 2 + 1) + 16 * i)
                            pe.wait_ge(s_pr, base + j + 1)
                            pe.matmul(PS[:, 5, :], VR[:, u, :], BIG[:, bass.ds(j * HALF, HALF)],
                                      start=(first and u == 0), stop=False,
                                      skip_group_check=True).then_inc(s_pv, 1)

                    step(0, True)
                    with pe.Fori(1, STEPS) as i:
                        step(i, False)
                    pe.wait_ge(s_pr, base + TILES)
                    pe.matmul(PS[:, 5, :], VTAIL[:, :], BIG[0:TAIL, KT * HALF:(KT + 1) * HALF], start=False,
                              stop=True, skip_group_check=True).then_inc(s_pv, 1)
                    pe.wait_ge(s_sv, (n + 1) * STEPS * len(DVE_SUMS))
                    pe.wait_ge(s_sp, (n + 1) * (STEPS * len(POOL_SUMS) + 1))
                    for k in range(HT):
                        for e in range(2):
                            mm = pe.matmul(PS[:, 7, h * HT + k:h * HT + k + 1], LS[:, e, k * P:(k + 1) * P],
                                           ONES[:, 0:1], start=(e == 0), stop=(e == 1))
                    mm.then_inc(s_l, 1)
            xc["half"] += 1

        def mix_stage(w_value):
            n = xc["n"]
            with nc.Block() as block:
                @block.tensor
                def _(pe):
                    for t in range(TT):
                        pe.matmul(PS[:, t // HT, (t % HT) * P:(t % HT + 1) * P], OT[:, t * P:(t + 1) * P],
                                  w_value, start=True, stop=True).then_inc(s_on, 1)

                @block.vector
                def _(dve):
                    for t in range(TT):
                        dve.wait_ge(s_on, n * TT + (t // HT + 1) * HT)
                        dve.tensor_scalar(NAT[:, t, :], PS[:, t // HT, (t % HT) * P:(t % HT + 1) * P],
                                          RL[:, t:t + 1], None, ALU.mult).then_inc(s_of, 1)
            xc["n"] += 1

        norm_stage(X, XN, 1e-5)
        query_stage(W["L0_xattn_Wq"][:, :], C["L0_xattn_bq"][:, 0:1], W["xwk_t"][:, :], C["L0_xattn_bk"][:, 0:1])
        for h in range(2):
            score_stage(h)
            value_stage(h)
        mix_stage(W["L0_xattn_Wv"][:, :])

        s_ew = sem("elementwise_chain")
        ew = {"n": 0}

        def elementwise_stage(ops):
            with nc.Block() as block:
                @block.vector
                def _(dve):
                    for o, i0, i1, op in ops:
                        if ew["n"]:
                            dve.wait_ge(s_ew, ew["n"])
                        dve.tensor_tensor(o, i0, i1, op).then_inc(s_ew, 1)
                        ew["n"] += 1

        def over_tokens(row):
            return row[:, :].unsqueeze(1).broadcast_to([P, TT, P])

        N3, X3, XN3 = NAT[:, :, :], X[:, :, :], XN[:, :, :]
        elementwise_stage([(N3, N3, over_tokens(R["L0_xattn_bv"]), ALU.add), (N3, N3, XN3, ALU.add)])
        norm_stage(NAT, NAT, 1e-5, turn=False)
        elementwise_stage([(N3, N3, over_tokens(R["L0_xattn_gamma"]), ALU.mult),
                           (N3, N3, over_tokens(R["L0_xattn_beta"]), ALU.add), (X3, X3, N3, ALU.add)])

        s_fa, s_fac, s_fm, s_fmc = (sem(n) for n in ("mix_parts", "mix_parts_copied", "mix_matrix", "mix_matrix_copied"))
        with nc.Block() as block:
            @block.tensor
            def _(pe):
                pe.matmul(PS[:, 0, 0:P], W["wr"][:, :], W["cos"][:, :], start=True, stop=False)
                pe.matmul(PS[:, 0, 0:P], W["wi"][:, :], W["sin"][:, :], start=False, stop=True).then_inc(s_fa, 1)
                pe.matmul(PS[:, 1, 0:P], W["wi"][:, :], W["cos"][:, :], start=True, stop=False)
                pe.matmul(PS[:, 1, 0:P], W["wr"][:, :], W["nsin"][:, :], start=False, stop=True).then_inc(s_fa, 1)
                pe.wait_ge(s_fac, 2)
                pe.matmul(PS[:, 2, 0:P], AMT[:, 0, :], W["cos"][:, :], start=True, stop=False)
                pe.matmul(PS[:, 2, 0:P], AMT[:, 1, :], W["nsin"][:, :], start=False, stop=True).then_inc(s_fm, 1)

            @block.scalar
            def _(act):
                for k in range(2):
                    act.wait_ge(s_fa, k + 1)
                    act.activation(AMT[:, k, :], PS[:, k, 0:P], ACT.Copy).then_inc(s_fac, 1)
                act.wait_ge(s_fm, 1)
                act.activation(MIX[:, :], PS[:, 2, 0:P], ACT.Copy, scale=1.0 / P).then_inc(s_fmc, 1)

        norm_stage(X, XN, 1e-5)
        linear_stage(MIX[:, :], R["L0_ffn_bias"][:, :], False)

        norm_stage(X, XN, 1e-5)
        ROLES = ((0, 0), (0, 1), (1, 0), (0, 2), (2, 0), (1, 1))
        PAIRS_ALL = HEADS // 2
        HROWS = P // 2
        MAXROW = HD * len(ROLES)

        def work16(at, *shape):
            v = BIG[:, at:at + shape[0] * shape[1] // 2].bitcast(BF16)
            return v.rearrange("p (a b) -> p a b", b=shape[1])

        QS = work16(0, HEADS, TOKENS)
        KS = work16(8192, PAIRS_ALL, TOKENS)
        VA = work(12288, TT, HEADS, STRIP)
        PB = work(16384, 3 * HPG, HALF).rearrange("p (s i) q -> p s i q", i=HPG)
        QP = work16(16384, 3, TOKENS)
        KP = work16(17920, 3, TOKENS)
        AT3 = work(22528, GROUPS - 1, TOKENS)
        AT = [AT3[:, g, :] for g in range(GROUPS - 1)] + [OT[:, :]]
        RST = sb("RST", [P, 2, HALF])
        MXC = sb("MXC", [P, GROUPS, HT, 2 * HPG, 2])
        MXR = sb("MXR", [P, GROUPS, HT, 2 * HPG])
        MRS = sb("MRS", [2 * HPG, HALF])
        MP = sb("MP", [2 * HPG, 3, HALF], BF16)
        s_cp, s_ch, s_cr1, s_cm, s_cl, s_cv, s_cset, s_cst, s_cset2 = (sem(n) for n in (
            "causal_projected", "causal_high", "causal_rest", "causal_middle", "causal_low", "causal_values",
            "causal_cleared", "causal_stacked", "causal_value_ones"))
        with nc.Block() as block:
            @block.gpsimd
            def _(pool):
                pool.memset(QS.bitcast(F32), 0.0).then_inc(s_cset, 1)
                for k, r in enumerate((STRIP, HROWS + STRIP)):
                    pool.wait_ge(s_cset, k + 1)
                    pool.memset(KS[r:r + STRIP, :, :], 1.0).then_inc(s_cset, 1)
                pool.wait_ge(s_cset, 3)
                pool.memset(VA, 0.0).then_inc(s_cset2, 1)
                pool.wait_ge(s_cset2, 1)
                pool.memset(VA[:, :, :, HD:HD + 1], 1.0).then_inc(s_cset2, 1)
                pool.wait_ge(s_cset2, 2)
                pool.memset(MXC[:, :, :, :, :], MASKED).then_inc(s_cset2, 1)

            @block.tensor
            def _(pe):
                for u in range(4):
                    w = W["wqc_t"] if u < 2 else W["wkc_t"]
                    pe.matmul(PS[:, u, :], w[:, :], XT[:, (u % 2) * HALF:(u % 2 + 1) * HALF], start=True,
                              stop=True).then_inc(s_cp, 1)
                for t in range(TT):
                    pe.matmul(PS[:, 4 + t // HT, (t % HT) * P:(t % HT + 1) * P], XT[:, t * P:(t + 1) * P],
                              W["wvc_t"][:, :], start=True, stop=True).then_inc(s_cp, 1)

            def parts(u):
                cols = slice((u % 2) * HALF, (u % 2 + 1) * HALF)
                return [(QP if u < 2 else KP)[:, k, cols] for k in range(3)]

            @block.scalar
            def _(act):
                for u in range(4):
                    act.wait_ge(s_cp, u + 1)
                    act.activation(parts(u)[0], PS[:, u, :], ACT.Copy).then_inc(s_ch, 1)
                for u in range(4):
                    act.wait_ge(s_cr1, u + 1)
                    act.activation(parts(u)[1], RST[:, u % 2, :], ACT.Copy).then_inc(s_cm, 1)

            @block.vector
            def _(dve):
                def rest(u):
                    dve.wait_ge(s_ch, u + 1)
                    if u >= 2:
                        dve.wait_ge(s_cl, u - 1)
                    dve.tensor_tensor(RST[:, u % 2, :], PS[:, u, :], parts(u)[0], ALU.subtract).then_inc(s_cr1, 1)

                def low(u):
                    dve.wait_ge(s_cm, u + 1)
                    dve.tensor_tensor(parts(u)[2], RST[:, u % 2, :], parts(u)[1], ALU.subtract).then_inc(s_cl, 1)

                rest(0)
                rest(1)
                low(0)
                rest(2)
                low(1)
                rest(3)
                low(2)
                low(3)
                dve.wait_ge(s_cset2, 2)
                for h in range(2):
                    dve.wait_ge(s_cp, 4 + (h + 1) * HT)
                    dve.tensor_copy(VA[:, h * HT:(h + 1) * HT, :, 0:HD],
                                    PS[:, 4 + h, :].rearrange("p (t h d) -> p t h d", h=HEADS, d=HD)
                                    ).then_inc(s_cv, 1)

            def stack(eng, dst, src, side, roles, done):
                eng.wait_ge(s_cset, 3)
                for r in roles:
                    part = ROLES[r][side]
                    eng.wait_ge(done[part][0], done[part][1])
                    for a in range(2):
                        row = HROWS * a + HD * r
                        to = dst[row:row + HD, :, :] if side else dst[row:row + HD, a:HEADS:2, :]
                        eng.dma_start(to, src[HROWS * a:HROWS * (a + 1), part, :]
                                      ).then_inc(s_cst, 16)

            @block.sync
            def _(sp):
                stack(sp, QS, QP, 0, (0, 1, 3, 2, 5, 4), ((s_ch, 2), (s_cm, 2), (s_cl, 2)))
                stack(sp, KS, KP, 1, (0, 2, 4, 1, 5, 3), ((s_ch, 4), (s_cm, 4), (s_cl, 4)))
                sp.wait_ge(s_cst, 16 * 4 * len(ROLES))

        s_c1, s_c1m, s_c1r, s_c1t, s_c1p, s_c1q = (sem(n) for n in (
            "causal_rows", "causal_row_max", "causal_row_max_joined", "causal_max_turned", "causal_max_parts",
            "causal_q_with_max"))
        s_c2, s_c2e, s_c2v, s_c2a = (sem(n) for n in ("causal_scores", "causal_probs", "causal_mixed", "causal_mix_kept"))
        SUBS = [(g, t, c, i) for g in range(GROUPS) for t in range(TT) for c in range(t // HT + 1) for i in range(HPG)]
        STEPS2 = [(h, k) for h in range(2) for k in range((h + 1) * HT)]
        NS, N2 = len(SUBS) // GROUPS, len(STEPS2)
        AHEAD = 10
        FIRST_SUBS = NS + AHEAD

        def subs_with(n):
            return range(min(FIRST_SUBS + HPG * n, len(SUBS)), min(FIRST_SUBS + HPG * (n + 1), len(SUBS)))

        def turned_with(n):
            for g in range(1, GROUPS):
                if n >= 1 and (g + 1) * NS - 1 in subs_with(n - 1):
                    return g
            return None

        def bank1(m):
            return m % 6 if m < FIRST_SUBS else 4 + m % 2

        def columns(h, k):
            first = max(0, k * P - h * HALF)
            return first, HALF - first

        with nc.Block() as block:
            @block.tensor
            def _(pe):
                def rows(m):
                    g, t, c, i = SUBS[m]
                    width = min(HALF, (t + 1) * P - c * HALF)
                    diagonal = c == t // HT
                    held = 6 if m < FIRST_SUBS else 2
                    if m >= held:
                        pe.wait_ge(s_c1m, m - held + 1)
                    if diagonal:
                        pe.matmul(PS[:, bank1(m), width - P:width], IDB[:, :], MASKN[:, :], start=True, stop=False,
                                  skip_group_check=True)
                    pe.matmul(PS[:, bank1(m), 0:width], QS[:, g * HPG + i, t * P:(t + 1) * P],
                              KS[:, 2 * g + i // 2, c * HALF:c * HALF + width], start=not diagonal, stop=True,
                              skip_group_check=True).then_inc(s_c1, 1)

                def turn_max(g):
                    pe.wait_ge(s_c1r, g + 1)
                    if g >= 1:
                        pe.wait_ge(s_c1p, 4 * g)
                    for t in range(HT):
                        mm = pe.transpose(PS[0:2 * HPG, 7, t * P:(t + 1) * P], MXR[:, g, t, :], ident[:, :])
                    mm.then_inc(s_c1t, 1)

                def scores(g, s, pair):
                    h, k = STEPS2[s]
                    first, width = columns(h, k)
                    diagonal = k * P >= h * HALF
                    u = (g * N2 + s) * 2 + pair
                    if u >= 2:
                        pe.wait_ge(s_c2e, u - 1)
                    b = 2 * pair
                    if diagonal:
                        for a in range(2):
                            pe.matmul(PS[:, b + a, 0:P], IDB[:, :], MASKT[:, :], start=True, stop=False,
                                      skip_group_check=True)
                    for a in range(2):
                        mm = pe.matmul(PS[:, b + a, 0:width], KS[:, 2 * g + pair, k * P:(k + 1) * P],
                                       QS[:, g * HPG + 2 * pair + a, h * HALF + first:(h + 1) * HALF],
                                       start=not diagonal, stop=True, skip_group_check=True)
                    mm.then_inc(s_c2, 1)

                def values(g, s):
                    h, k = STEPS2[s]
                    first, width = columns(h, k)
                    if k == 0 and 2 * g + h >= 1:
                        pe.wait_ge(s_c2a, 2 * g + h)
                    pe.wait_ge(s_c2e, (g * N2 + s + 1) * 2)
                    for i in range(HPG):
                        mm = pe.matmul(PS[STRIP * i:STRIP * (i + 1), 6, first:HALF], VA[:, k, g * HPG + i, :],
                                       PB[:, (g * N2 + s) % 3, i, 0:width], start=(k == 0),
                                       stop=(k == (h + 1) * HT - 1), skip_group_check=True)
                    mm.then_inc(s_c2v, 1)

                for m in range(FIRST_SUBS):
                    rows(m)
                turn_max(0)
                pe.wait_ge(s_c1m, FIRST_SUBS)
                for n in range(GROUPS * N2):
                    g, s = n // N2, n % N2
                    if s == 0:
                        pe.wait_ge(s_c1q, 128 * (g + 1))
                    scores(g, s, 0)
                    scores(g, s, 1)
                    for m in subs_with(n):
                        rows(m)
                    if n >= 1:
                        values((n - 1) // N2, (n - 1) % N2)
                    if turned_with(n) is not None:
                        turn_max(turned_with(n))
                values(GROUPS - 1, N2 - 1)

            @block.scalar
            def _(act):
                def keep(gh):
                    act.wait_ge(s_c2v, (gh // 2) * N2 + (HT if gh % 2 == 0 else N2))
                    act.activation(AT[gh // 2][:, (gh % 2) * HALF:(gh % 2 + 1) * HALF], PS[:, 6, :],
                                   ACT.Copy).then_inc(s_c2a, 1)

                for u in range(GROUPS * N2 * 2):
                    g, s, pair = u // (2 * N2), u // 2 % N2, u % 2
                    first, width = columns(*STEPS2[s])
                    n = g * N2 + s
                    act.wait_ge(s_c2, u + 1)
                    if n >= 3:
                        act.wait_ge(s_c2v, n - 2)
                    act.activation(PB[:, n % 3, 2 * pair:2 * pair + 2, 0:width], PS[:, 2 * pair:2 * pair + 2, 0:width],
                                   ACT.Exp, scale=float(HD) ** -0.5).then_inc(s_c2e, 1)
                    if pair == 1 and s == HT:
                        keep(2 * g)
                    if pair == 1 and s == 0 and g >= 1:
                        keep(2 * g - 1)
                keep(2 * GROUPS - 1)

            @block.vector
            def _(dve):
                def row_max(m):
                    g, t, c, i = SUBS[m]
                    width = min(HALF, (t + 1) * P - c * HALF)
                    k = (t // HT) * HPG + i
                    dve.wait_ge(s_c1, m + 1)
                    dve.tensor_reduce(MXC[:, g, t % HT, k:k + 1, c], PS[:, bank1(m), 0:width], AX.X,
                                      ALU.max).then_inc(s_c1m, 1)
                    if (m + 1) % NS == 0:
                        dve.wait_ge(s_c1m, m + 1)
                        dve.tensor_reduce(MXR[:, g, :, :], MXC[:, g, :, :, :], AX.X, ALU.max).then_inc(s_c1r, 1)

                def max_parts(g):
                    if g >= 1:
                        dve.wait_ge(s_c1q, 128 * g)
                    m = PS[0:2 * HPG, 7, :]
                    dve.wait_ge(s_c1t, g + 1)
                    dve.tensor_scalar(MP[:, 0, :], m, -1.0, None, ALU.mult).then_inc(s_c1p, 1)
                    dve.wait_ge(s_c1p, 4 * g + 1)
                    dve.scalar_tensor_tensor(out=MRS[:, :], in0=m, scalar=-1.0, in1=MP[:, 0, :], op0=ALU.mult,
                                             op1=ALU.subtract).then_inc(s_c1p, 1)
                    dve.wait_ge(s_c1p, 4 * g + 2)
                    dve.tensor_copy(MP[:, 1, :], MRS[:, :]).then_inc(s_c1p, 1)
                    dve.wait_ge(s_c1p, 4 * g + 3)
                    dve.tensor_tensor(MP[:, 2, :], MRS[:, :], MP[:, 1, :], ALU.subtract).then_inc(s_c1p, 1)

                for m in range(FIRST_SUBS):
                    row_max(m)
                max_parts(0)
                for n in range(GROUPS * N2):
                    for m in subs_with(n):
                        row_max(m)
                    if turned_with(n) is not None:
                        max_parts(turned_with(n))

            @block.sync
            def _(sp):
                for g in range(GROUPS):
                    sp.wait_ge(s_c1p, 4 * (g + 1))
                    for a in range(2):
                        row = HROWS * a + MAXROW
                        for k in range(2):
                            for h in range(2):
                                m = h * HPG + 2 * k + a
                                sp.dma_start(QS[row:row + 3, g * HPG + 2 * k + a, h * HALF:(h + 1) * HALF],
                                             MP[m:m + 1, :, :]).then_inc(s_c1q, 16)

        s_ct1, s_cr, s_ca, s_ct2, s_ca2, s_co, s_cx = (sem(n) for n in (
            "causal_turned", "causal_recip", "causal_divided", "causal_turned_back", "causal_turned_kept",
            "causal_out", "causal_added"))
        RN = sb("RN", [P, TT, HEADS])
        AN = work(16384, TT, P)
        ANT = work(17408, TOKENS)
        with nc.Block() as block:
            @block.tensor
            def _(pe):
                for t in range(TT):
                    if t >= 4:
                        pe.wait_ge(s_ca, t - 3)
                    for g in range(GROUPS):
                        mm = pe.transpose(PS[:, t % 4, g * P:(g + 1) * P], AT[g][:, t * P:(t + 1) * P], ident[:, :])
                    mm.then_inc(s_ct1, 1)
                for t in range(TT):
                    pe.wait_ge(s_ca, t + 1)
                    pe.transpose(PS[:, 4 + t // HT, (t % HT) * P:(t % HT + 1) * P], AN[:, t, :],
                                 ident[:, :]).then_inc(s_ct2, 1)
                for t in range(TT):
                    pe.wait_ge(s_ca2, t // HT + 1)
                    pe.matmul(PS[:, 6 + t // HT, (t % HT) * P:(t % HT + 1) * P], ANT[:, t * P:(t + 1) * P],
                              W["woc_t"][:, :], start=True, stop=True).then_inc(s_co, 1)

            @block.scalar
            def _(act):
                for h in range(2):
                    act.wait_ge(s_ct2, (h + 1) * HT)
                    act.activation(ANT[:, h * HALF:(h + 1) * HALF], PS[:, 4 + h, :], ACT.Copy).then_inc(s_ca2, 1)

            @block.vector
            def _(dve):
                for t in range(TT):
                    src = PS[:, t % 4, :].rearrange("p (h s) -> p h s", s=STRIP)
                    dve.wait_ge(s_ct1, t + 1)
                    dve.reciprocal(RN[:, t, :], src[:, :, HD]).then_inc(s_cr, 1)
                    dve.wait_ge(s_cr, t + 1)
                    dve.tensor_tensor(AN[:, t, :].rearrange("p (h d) -> p h d", d=HD), src[:, :, 0:HD],
                                      RN[:, t, :].unsqueeze(2).broadcast_to([P, HEADS, HD]),
                                      ALU.mult).then_inc(s_ca, 1)
                for h in range(2):
                    dve.wait_ge(s_co, (h + 1) * HT)
                    v = X[:, h * HT:(h + 1) * HT, :]
                    dve.tensor_tensor(v, PS[:, 6 + h, :].rearrange("p (t d) -> p t d", d=P), v, ALU.add).then_inc(s_cx, 1)

        norm_stage(X, XN, 1e-5)
        query_stage(W["w1x_t"][:, :], C["L1_xattn_b"][:, 0:1], W["L1_xattn_W"][:, :], C["L1_xattn_b"][:, 0:1])
        for h in range(2):
            score_stage(h)
            value_stage(h)
        mix_stage(ident[:, :])
        elementwise_stage([(X3, X3, N3, ALU.add)])

        norm_stage(X, XN, 1e-5)
        ACC = work(0, TT, P)
        HID = work(1024, 2, HC, HALF)
        W1S = work(5120, 2, HIDDEN)
        W2S = work(6144, 2, HC, P)
        B1S = work(7168, 2, HC)
        B2 = work(7232, P)
        GW = work(7360, EXPERTS)
        LG = work(7424, TT, EXPERTS)
        G1 = work(7488, TT, EXPERTS, EXPERTS)
        G2 = work(8000, TT, EXPERTS, EXPERTS)
        LOW = work(8512, EXPERTS, EXPERTS)
        RK = work(8576, TT, EXPERTS)
        S8 = work(8640, TT)
        CMB = work(8704, TT, EXPERTS)
        CMT = work(8768, TOKENS)
        s_gw, s_gl, s_gc, s_ge, s_ct, s_ctc, s_sg, s_b2 = (sem(n) for n in (
            "gate_loaded", "gate_logits", "gate_chain", "gate_exp", "combine_turned", "combine_kept",
            "shared_gelu", "bias_mixed"))
        with nc.Block() as block:
            @block.sync
            def _(sp):
                sp.dma_start(B2[0:EXPERTS, :], a["L1_ffn_b2"]).then_inc(s_gw, 16)
                sp.dma_start(GW, a["L1_ffn_gate_W"]).then_inc(s_gw, 16)
                sp.dma_start(LOW.rearrange("p a b -> p (a b)"), a["lower"].partition_broadcast(P)).then_inc(s_gw, 16)
                sp.wait_ge(s_gw, 48)

            @block.tensor
            def _(pe):
                pe.wait_ge(s_gw, 48)
                for t in range(TT):
                    mm = pe.matmul(PS[:, 0, t * EXPERTS:(t + 1) * EXPERTS], XT[:, t * P:(t + 1) * P], GW,
                                   start=True, stop=True)
                mm.then_inc(s_gl, 1)
                for t in range(TT):
                    mm = pe.matmul(PS[:, 1 + t // HT, (t % HT) * P:(t % HT + 1) * P], XT[:, t * P:(t + 1) * P],
                                   W["L1_ffn_shared_W"][:, :], start=True, stop=True)
                mm.then_inc(s_gl, 1)
                pe.wait_ge(s_gc, 14)
                for t in range(TT):
                    mm = pe.transpose(PS[0:EXPERTS, 3 + t // HT, (t % HT) * P:(t % HT + 1) * P], CMB[:, t, :],
                                      ident[:, :])
                mm.then_inc(s_ct, 1)
                pe.wait_ge(s_ctc, 1)
                for t in range(TT):
                    mm = pe.matmul(PS[:, 5 + t // HT, (t % HT) * P:(t % HT + 1) * P],
                                   CMT[0:EXPERTS, t * P:(t + 1) * P], B2[0:EXPERTS, :], start=True, stop=True)
                mm.then_inc(s_b2, 1)

            @block.vector
            def _(dve):
                steps = [0]

                def chained(instruction):
                    instruction.then_inc(s_gc, 1)
                    steps[0] += 1

                def across(v):
                    return v.unsqueeze(2).broadcast_to([P, TT, EXPERTS])

                dve.wait_ge(s_gl, 1)
                dve.tensor_reduce(S8, PS[:, 0, 0:TT * EXPERTS].rearrange("p (t e) -> p t e", e=EXPERTS), AX.X,
                                  ALU.max).then_inc(s_gc, 1)
                dve.wait_ge(s_gc, 1)
                dve.tensor_tensor(LG, PS[:, 0, 0:TT * EXPERTS].rearrange("p (t e) -> p t e", e=EXPERTS),
                                  across(S8), ALU.subtract).then_inc(s_gc, 1)
                dve.wait_ge(s_ge, 1)
                dve.tensor_reduce(S8, LG, AX.X, ALU.add).then_inc(s_gc, 1)
                dve.wait_ge(s_gc, 3)
                dve.reciprocal(S8, S8).then_inc(s_gc, 1)
                dve.wait_ge(s_gc, 4)
                dve.tensor_tensor(LG, LG, across(S8), ALU.mult).then_inc(s_gc, 1)
                dve.wait_ge(s_gc, 5)
                mine = LG.unsqueeze(3).broadcast_to([P, TT, EXPERTS, EXPERTS])
                other = LG.unsqueeze(2).broadcast_to([P, TT, EXPERTS, EXPERTS])
                dve.tensor_tensor(G1, other, mine, ALU.is_gt).then_inc(s_gc, 1)
                dve.tensor_tensor(G2, other, mine, ALU.is_equal).then_inc(s_gc, 1)
                dve.wait_ge(s_gc, 7)
                dve.wait_ge(s_gw, 48)
                dve.tensor_tensor(G2, G2, LOW.unsqueeze(1).broadcast_to([P, TT, EXPERTS, EXPERTS]),
                                  ALU.mult).then_inc(s_gc, 1)
                dve.wait_ge(s_gc, 8)
                dve.tensor_tensor(G1, G1, G2, ALU.add).then_inc(s_gc, 1)
                dve.wait_ge(s_gc, 9)
                dve.tensor_reduce(RK, G1, AX.X, ALU.add).then_inc(s_gc, 1)
                dve.wait_ge(s_gc, 10)
                dve.scalar_tensor_tensor(out=CMB, in0=RK, scalar=1.5, in1=LG, op0=ALU.is_lt,
                                         op1=ALU.mult).then_inc(s_gc, 1)
                dve.wait_ge(s_gc, 11)
                dve.tensor_reduce(S8, CMB, AX.X, ALU.add).then_inc(s_gc, 1)
                dve.wait_ge(s_gc, 12)
                dve.reciprocal(S8, S8).then_inc(s_gc, 1)
                dve.wait_ge(s_gc, 13)
                dve.tensor_tensor(CMB, CMB, across(S8), ALU.mult).then_inc(s_gc, 1)
                dve.wait_ge(s_ct, 1)
                dve.tensor_copy(CMT[0:EXPERTS, :].rearrange("p (h q) -> p h q", h=2),
                                PS[0:EXPERTS, 3:5, :]).then_inc(s_ctc, 1)
                dve.wait_ge(s_gl, 2)
                dve.tensor_tensor(NAT[:, :, :].rearrange("p (h t) d -> p h t d", h=2),
                                  PS[:, 1:3, :].rearrange("p h (t d) -> p h t d", d=P),
                                  R["L1_ffn_shared_b"][:, :].unsqueeze(1).unsqueeze(1).broadcast_to([P, 2, HT, P]),
                                  ALU.add).then_inc(s_gc, 1)
                dve.wait_ge(s_sg, 1)
                dve.wait_ge(s_b2, 1)
                dve.scalar_tensor_tensor(out=ACC.rearrange("p t d -> p (t d)").rearrange("p (h q) -> p h q", h=2),
                                         in0=NAT[:, :, :].rearrange("p t d -> p (t d)").rearrange(
                                             "p (h q) -> p h q", h=2),
                                         scalar=0.5, in1=PS[:, 5:7, :], op0=ALU.mult, op1=ALU.add).then_inc(s_gc, 1)

            @block.scalar
            def _(act):
                act.wait_ge(s_gc, 2)
                act.activation(LG, LG, ACT.Exp).then_inc(s_ge, 1)
                act.wait_ge(s_gc, 15)
                act.activation(NAT[:, :, :], NAT[:, :, :], ACT.Gelu).then_inc(s_sg, 1)

        s_wa, s_wb, s_h, s_hg, s_y, s_acc = (sem(n) for n in (
            "expert_weights_a", "expert_weights_b", "expert_hidden", "expert_gelu", "expert_out", "expert_added"))
        PAIRS = EXPERTS // 2
        UPP = 4
        with nc.Block() as block:
            @block.sync
            def _(sp):
                def load(i, k, first):
                    if not first:
                        sp.wait_ge(s_y, HT * (UPP * (i - 1) + 2 * k + 2))
                    e = i * 2 + k
                    s = s_wa if k == 0 else s_wb
                    sp.dma_start(W1S[:, k, :], a["L1_ffn_W1"][bass.ds(e, 1), :, :].rearrange("e d h -> d (e h)")
                                 ).then_inc(s, 16)
                    sp.dma_start(W2S[:, k, :, :], a["L1_ffn_W2"][bass.ds(e, 1), :, :].rearrange(
                        "e (c p) d -> p (e c) d", p=P)).then_inc(s, 16)
                    sp.dma_start(B1S[:, k, :], a["b1_cols"][:, bass.ds(e * HC, HC)]).then_inc(s, 16)

                load(0, 0, True)
                load(0, 1, True)
                with sp.Fori(1, PAIRS) as i:
                    load(i, 0, False)
                    load(i, 1, False)

            @block.tensor
            def _(pe):
                def hidden(i, k, first):
                    slot, h = k // 2, k % 2
                    if h == 0:
                        pe.wait_ge(s_wa if slot == 0 else s_wb, 48 * i + 48)
                    for c in range(HC):
                        if not (first and k == 0):
                            pe.wait_ge(s_hg, (i * UPP + k - 1) * HC + c + 1)
                        pe.matmul(PS[:, c, :], W1S[:, slot, c * P:(c + 1) * P], XT[:, h * HALF:(h + 1) * HALF],
                                  start=True, stop=True).then_inc(s_h, 1)

                def output(i, k, early):
                    slot, h = k // 2, k % 2
                    pe.wait_ge(s_hg, (i * UPP + k + 1) * HC)
                    if not early:
                        pe.wait_ge(s_acc, (i * UPP + k - 1) * HT)
                    for t in range(HT):
                        for c in range(HC):
                            mm = pe.matmul(PS[:, 4 + k % 2, t * P:(t + 1) * P], HID[:, h, c, t * P:(t + 1) * P],
                                           W2S[:, slot, c, :], start=(c == 0), stop=(c == HC - 1))
                        mm.then_inc(s_y, 1)

                def step(i, first):
                    for k in range(UPP):
                        hidden(i, k, first)
                        if k > 0:
                            output(i, k - 1, first and k - 1 < 2)
                        elif not first:
                            output(i - 1, UPP - 1, False)

                step(0, True)
                with pe.Fori(1, PAIRS) as i:
                    step(i, False)
                output(PAIRS - 1, UPP - 1, False)

            @block.scalar
            def _(act):
                def step(i, first):
                    for k in range(UPP):
                        slot, h = k // 2, k % 2
                        if not (first and k < 2):
                            act.wait_ge(s_y, (i * UPP + k - 1) * HT)
                        for c in range(HC):
                            act.wait_ge(s_h, (i * UPP + k) * HC + c + 1)
                            act.activation(HID[:, h, c, :], PS[:, c, :], ACT.Gelu,
                                           bias=B1S[:, slot, c:c + 1]).then_inc(s_hg, 1)

                step(0, True)
                with act.Fori(1, PAIRS) as i:
                    step(i, False)

            @block.vector
            def _(dve):
                with dve.Fori(0, PAIRS) as i:
                    for k in range(UPP):
                        slot, h = k // 2, k % 2
                        dve.wait_ge(s_y, (i * UPP + k + 1) * HT)
                        for t in range(HT):
                            v = ACC[:, h * HT + t, :]
                            dve.scalar_tensor_tensor(out=v, in0=PS[:, 4 + k % 2, t * P:(t + 1) * P],
                                                     scalar=CMB[:, h * HT + t, bass.ds(i * 2 + slot, 1)], in1=v,
                                                     op0=ALU.mult, op1=ALU.add).then_inc(s_acc, 1)

        norm_stage(ACC, NAT, 1e-5, turn=False)
        elementwise_stage([(N3, N3, over_tokens(R["L1_ffn_gamma"]), ALU.mult),
                           (N3, N3, over_tokens(R["L1_ffn_beta"]), ALU.add), (X3, X3, N3, ALU.add)])
        with nc.Block() as block:
            @block.sync
            def _(sp):
                sp.dma_start(out[0].rearrange("(t p) d -> p t d", p=P), X[:, :, :]).then_inc(s_out, 16)
                sp.wait_ge(s_out, 16)


def kernel(**inputs):
    import ml_dtypes
    import numpy as np
    import concourse.bacc as bacc
    from concourse.bass_utils import run_bass_kernel_spmd

    f = {k: np.ascontiguousarray(v) for k, v in inputs.items()}
    bf16 = ml_dtypes.bfloat16

    f["xwk_t"] = f["L0_xattn_Wk"].T
    f["w1x_t"] = f["L1_xattn_W"].T
    for name, w in (("wqc_t", "L1_attn_q_proj"), ("wkc_t", "L1_attn_k_proj")):
        f[name] = f[w].reshape(HEADS // 2, 2, HD, P).transpose(1, 2, 0, 3).reshape(P, P).T
    f["wvc_t"] = f["L1_attn_v_proj"].T
    f["woc_t"] = f["L1_attn_o_proj"].T
    f["b1_cols"] = f["L1_ffn_b1"].reshape(EXPERTS * HC, P).T

    k = np.arange(P)
    turn = 2.0 * np.pi * (np.outer(k, k) % P) / P
    f["ident"] = np.eye(P, dtype=np.float32)
    f["cos"] = np.cos(turn).astype(np.float32)
    f["sin"] = np.sin(turn).astype(np.float32)
    f["nsin"] = -f["sin"]
    f["blocks"] = np.kron(np.eye(HEADS), np.ones((HD, HD))).astype(np.float32)
    f["ident_b"] = np.eye(P).astype(bf16)
    f["mask_n"] = np.where(k[None, :] > k[:, None], MASKED, 0.0).astype(bf16)
    f["mask_t"] = np.where(k[:, None] > k[None, :], MASKED, 0.0).astype(bf16)
    e = np.arange(EXPERTS)
    f["lower"] = (e[None, :] < e[:, None]).astype(np.float32).reshape(-1)

    unused = ("L0_xattn_Wk", "L1_attn_q_proj", "L1_attn_k_proj", "L1_attn_v_proj", "L1_attn_o_proj", "L1_ffn_b1")
    nc = bacc.Bacc("TRN2", target_bir_lowering=False, num_devices=1)
    arrays, aps = {}, {}
    for name, v in f.items():
        if name in unused:
            continue
        v = np.ascontiguousarray(v)
        arrays[f"in_{name}"] = v
        aps[name] = nc.dram_tensor(f"in_{name}", v.shape, mybir.dt.from_np(v.dtype), kind="ExternalInput").ap()
    out = nc.dram_tensor("out_0", (1, TOKENS, P), F32, kind="ExternalOutput").ap()
    decoder_kernel(nc, aps, out)
    r = run_bass_kernel_spmd(nc, [arrays], core_ids=[0])
    return r.results[0]["out_0"]
```

```python
from contextlib import ExitStack

import concourse.bass as bass
from concourse import mybir

ALU = mybir.AluOpType
ACT = mybir.ActivationFunctionType
AX = mybir.AxisListType
F32 = mybir.dt.float32
F16 = mybir.dt.float16
BF16 = mybir.dt.bfloat16

P = 128
TOKENS = 1024
TT = TOKENS // P
HALF = 512
HT = HALF // P
CTX = 6404
KT = CTX // P
TAIL = CTX - KT * P
HEADS, HD = 16, 8
GROUPS = 4
HPG = HEADS // GROUPS
STRIP = 32
EXPERTS, HIDDEN = 8, 512
HC = HIDDEN // P
RING = 5
STEP = 2 * RING
MASKED = -1.0e30
SQ = ["ident", "L0_attn_Wq", "L0_attn_Wk", "L0_attn_Wv", "blocks", "wfb_f", "wfb_r", "L0_attn_Wo", "L0_xattn_Wq",
      "xwk_t", "L0_xattn_Wv", "wr", "wi", "cos", "sin", "nsin", "wqc_t", "wkc_t", "wvc_t", "woc_t", "w1x_t",
      "L1_xattn_W", "L1_ffn_shared_W"]
COLS = ["L0_attn_bq", "L0_attn_bk", "L0_attn_bv", "L0_attn_g1", "L0_attn_b1", "L0_attn_g2", "L0_attn_b2",
        "L0_xattn_bq", "L0_xattn_bk", "L1_xattn_b"]
ROWS = ["L0_attn_bfb", "L0_attn_bo", "L0_xattn_bv", "L0_xattn_gamma", "L0_xattn_beta", "L0_ffn_bias",
        "L1_ffn_shared_b", "L1_ffn_gamma", "L1_ffn_beta"]
WSCALE = 64.0


def decoder_kernel(nc, a, out):
    with ExitStack() as ctx:
        def sb(name, shape, dt=F32):
            return ctx.enter_context(nc.sbuf_tensor(name, shape, dt))

        def sem(name):
            return ctx.enter_context(nc.semaphore(name))

        PS = ctx.enter_context(nc.psum_tensor("PS", [P, 8, HALF], F32))
        X = sb("X", [P, TT, P])
        XN = sb("XN", [P, TT, P])
        XT = sb("XT", [P, TOKENS])
        NAT = sb("NAT", [P, TT, P])
        BIG = sb("BIG", [P, (KT + 1) * HALF])
        CTH = sb("CTH", [P, CTX], F16)
        CTL = sb("CTL", [P, CTX], F16)
        QH = sb("QH", [P, TOKENS], F16)
        QL = sb("QL", [P, TOKENS], F16)
        VR = sb("VR", [P, STEP, P])
        VTAIL = sb("VTAIL", [TAIL, P])
        RM = sb("RM", [P, 2, HALF])
        LS = sb("LS", [P, 2, HALF])
        OT = sb("OT", [P, TOKENS])
        DG = sb("DG", [P, HT, P])
        MX = sb("MX", [P, HT])
        MC = sb("MC", [P, HT])
        RL = sb("RL", [P, TT])
        ST = sb("ST", [P, TT, 6])
        MV = sb("MV", [P, TT, 2])
        VE = sb("VE", [P, TT])
        RS = sb("RS", [P, TT])
        NEGHALF = sb("NEGHALF", [P, TT])
        ONES = sb("ONES", [P, P])
        EARLY = SQ.index("L0_xattn_Wq")
        SQUARES = sb("SQUARES", [P, len(SQ), P])
        W = {n: SQUARES[:, k, :] for k, n in enumerate(SQ)}
        COLUMNS = sb("COLUMNS", [P, len(COLS)])
        C = {n: COLUMNS[:, k:k + 1] for k, n in enumerate(COLS)}
        ROWS_ALL = sb("ROWS_ALL", [P, len(ROWS), P])
        R = {n: ROWS_ALL[:, k, :] for k, n in enumerate(ROWS)}
        MIX = sb("MIX", [P, P])
        AMT = sb("AMT", [P, 2, P])
        BF_ALL = sb("BF_ALL", [P, 3, P], BF16)
        IDB, MASKN, MASKT = (BF_ALL[:, k, :] for k in range(3))

        def work(at, *shape):
            n = 1
            for s in shape:
                n *= s
            v = BIG[:, at:at + n]
            if len(shape) == 2:
                return v.rearrange("p (a b) -> p a b", b=shape[1])
            if len(shape) == 3:
                return v.rearrange("p (a b c) -> p a b c", b=shape[1], c=shape[2])
            return v

        ident = W["ident"]

        s_x, s_sq, s_late, s_vec, s_mask, s_ctx, s_out = (sem(n) for n in (
            "x_loaded", "early_squares_loaded", "late_squares_loaded", "vectors_loaded", "masks_loaded", "context_loaded", "out_stored"))
        s_const = sem("constants_set")
        s_stats, s_aggr, s_var, s_rstd, s_normed, s_turned, s_xt = (sem(n) for n in (
            "norm_stats", "norm_aggregated", "norm_variance", "norm_rstd", "norm_applied", "norm_turned", "norm_xt"))
        s_gained, s_gain_added = sem("norm_gained"), sem("norm_gain_added")
        s_ctx_turned, s_ctx_hi, s_ctx_lo = sem("context_turned"), sem("context_high"), sem("context_low")

        calls = {"norm": 0}

        def norm_stage(src, dst, eps, scale=1.0, bias=0.0, turn=True, loaded=None, alongside=None,
                       with_pe=None, with_act=None, pool_after=None, gain=None, store=False):
            n = calls["norm"]
            calls["norm"] += 1
            turns = calls.setdefault("turns", 0)
            gains = calls.setdefault("gains", 0)
            if gain is not None:
                calls["gains"] += 1
            if turn:
                calls["turns"] += 1
            with nc.Block() as block:
                @block.vector
                def _(dve):
                    if loaded is not None:
                        dve.wait_ge(loaded, 16)

                    def statistics(h):
                        for t in range(h * HT, (h + 1) * HT):
                            dve.bn_stats(ST[:, t, :], src[:, t, :]).then_inc(s_stats, 1)
                        for t in range(h * HT, (h + 1) * HT):
                            dve.wait_ge(s_stats, n * TT + t + 1)
                            dve.bn_aggr(MV[:, t, :], ST[:, t, :]).then_inc(s_aggr, 1)
                        dve.wait_ge(s_aggr, n * TT + (h + 1) * HT)
                        own = slice(h * HT, (h + 1) * HT)
                        dve.tensor_scalar(VE[:, own], MV[:, own, 1], eps, None, ALU.add).then_inc(s_var, 1)

                    def apply(h):
                        dve.wait_ge(s_rstd, 2 * n + h + 1)
                        for t in range(h * HT, (h + 1) * HT):
                            dve.tensor_scalar(dst[:, t, :], src[:, t, :], MV[:, t, 0:1], RS[:, t:t + 1],
                                              ALU.subtract, ALU.mult).then_inc(s_normed, 1)
                        if gain is not None:
                            own = slice(h * HT, (h + 1) * HT)
                            dve.wait_ge(s_normed, n * TT + (h + 1) * HT)
                            dve.tensor_tensor(dst[:, own, :], dst[:, own, :],
                                              gain.unsqueeze(1).broadcast_to([P, HT, P]), ALU.mult
                                              ).then_inc(s_gained, 1)
                            dve.wait_ge(s_gained, 2 * gains + h + 1)
                            dve.tensor_tensor(X[:, own, :], X[:, own, :], dst[:, own, :], ALU.add
                                              ).then_inc(s_gain_added, 1)

                    statistics(0)
                    statistics(1)
                    apply(0)
                    apply(1)

                @block.gpsimd
                def _(pool):
                    for h in range(2):
                        own = slice(h * HT, (h + 1) * HT)
                        pool.wait_ge(s_var, 2 * n + h + 1)
                        pool.tensor_tensor(RS[:, own], VE[:, own], NEGHALF[:, own], ALU.pow).then_inc(s_rstd, 1)
                    if pool_after is not None:
                        pool_after(pool)

                if alongside is not None:
                    block.sync(alongside)

                if store:
                    @block.sync
                    def _(sp):
                        to = out[0].rearrange("(t p) d -> p t d", p=P)
                        for h in range(2):
                            sp.wait_ge(s_gain_added, 2 * gains + h + 1)
                            own = slice(h * HT, (h + 1) * HT)
                            sp.dma_start(to[:, own, :], X[:, own, :]).then_inc(s_out, 16)
                        sp.wait_ge(s_out, 32)

                if not turn and with_pe is not None:
                    block.tensor(with_pe)
                    block.scalar(with_act)

                if turn:
                    @block.tensor
                    def _(pe):
                        if with_pe is not None:
                            with_pe(pe)
                        for t in range(TT):
                            pe.wait_ge(s_normed, n * TT + t + 1)
                            pe.transpose(PS[:, t // HT, (t % HT) * P:(t % HT + 1) * P], dst[:, t, :],
                                         ident[:, :]).then_inc(s_turned, 1)

                    @block.scalar
                    def _(act):
                        if with_act is not None:
                            with_act(act)
                        for h in range(2):
                            act.wait_ge(s_turned, turns * TT + (h + 1) * HT)
                            act.activation(XT[:, h * HALF:(h + 1) * HALF], PS[:, h, :], ACT.Identity,
                                           bias=bias, scale=scale).then_inc(s_xt, 1)

        CN = work(0, KT, P)
        ctx_main = a["ctx_1024"][0, 0:KT * P, :].rearrange("(p t) d -> p t d", t=KT)
        ctx_tail = a["ctx_1024"][0, KT * P:CTX, :]

        with nc.Block() as block:
            @block.sync
            def _(sp):
                sp.dma_start(X[:, :, :], a["x"][0].rearrange("(t p) d -> p t d", p=P)).then_inc(s_x, 16)
                sp.dma_start(SQUARES[:, 0:EARLY, :], a["squares"][:, 0:EARLY, :]).then_inc(s_sq, 16)
                sp.dma_start(CN, ctx_main).then_inc(s_ctx, 16)
                sp.dma_start(VTAIL[:, :], ctx_tail).then_inc(s_ctx, 16)
                sp.dma_start(SQUARES[:, EARLY:, :], a["squares"][:, EARLY:, :]).then_inc(s_late, 16)
                sp.dma_start(BF_ALL[:, :, :], a["bf_squares"]).then_inc(s_mask, 16)

            @block.scalar
            def _(act):
                act.dma_start(COLUMNS[:, :], a["columns"]).then_inc(s_vec, 16)
                act.dma_start(ROWS_ALL[:, :, :].rearrange("p k d -> p (k d)"), a["rows"].partition_broadcast(P)
                              ).then_inc(s_vec, 16)

            @block.gpsimd
            def _(pool):
                pool.memset(NEGHALF[:, :], -0.5).then_inc(s_const, 1)
                pool.memset(ONES[:, :], 1.0).then_inc(s_const, 1)

        def early_loads(sp):
            sp.wait_ge(s_sq, 16)
            sp.wait_ge(s_vec, 32)

        def late_loads(sp):
            sp.wait_ge(s_late, 16)
            sp.wait_ge(s_mask, 16)

        norm_stage(X, XN, 1e-5, turn=False, loaded=s_x, alongside=early_loads)
        norm_stage(XN, XN, 1e-6, scale=C["L0_attn_g1"][:, 0:1], bias=C["L0_attn_b1"][:, 0:1])

        PADW = TOKENS + 4
        CHUNKS = 3
        CW = (TOKENS + 2) // CHUNKS
        TW = CW // 3
        at = KT * P
        LQ, LK, LV = (work(at + i * PADW, PADW) for i in range(3))
        at += 3 * PADW
        PR = work(at, 3, TOKENS + 2)
        PV = work(at + 3 * (TOKENS + 2), 3, TOKENS + 2)
        at += 6 * (TOKENS + 2)
        LM = work(at, TOKENS + 2)
        LA = work(at + TOKENS + 2, TOKENS + 2)
        LRN = sb("LRN", [TW, CHUNKS, 3, HEADS])
        LRW = sb("LRW", [TW, CHUNKS, 3 * HEADS, HD])
        s_lrw, s_lp, s_lq, s_pad, s_prod, s_lsc, s_lmx, s_lsub, s_lexp, s_lsum, s_lst, s_lrc, s_lex, s_lpv, s_lpa, s_la, s_lz, s_lzc = (
            sem(n) for n in (
                "local_recip_repeated", "local_projected", "local_qkv", "local_padded", "local_products", "local_scores", "local_max",
                "local_shifted", "local_exp", "local_sums", "local_sums_turned", "local_recip", "local_recip_spread",
                "local_values", "local_values_added", "local_out", "local_joined", "local_join_copied"))
        HALVES = [(0, 0), (1, 0), (0, 1), (1, 1), (2, 0), (2, 1)]
        CENTRES = [slice(c * CW, (c + 1) * CW) for c in range(CHUNKS)]
        TURN_BANK = (6, 7, 1)
        SPREAD_BANK = (6, 7, 0)
        MIX_BANK = (4, 5)
        TILES_AT = [[t for t in range(TT) if c * CW < (t + 1) * P + 2 <= (c + 1) * CW] for c in range(CHUNKS)]
        with nc.Block() as block:
            @block.tensor
            def _(pe):
                for k, (i, h) in enumerate(HALVES):
                    w = ("L0_attn_Wq", "L0_attn_Wk", "L0_attn_Wv")[i]
                    pe.matmul(PS[:, k, :], W[w], XT[:, h * HALF:(h + 1) * HALF], start=True,
                              stop=True).then_inc(s_lp, 1)

                def scores(c):
                    pe.wait_ge(s_lq, 3 if c == 0 else 6)
                    if c == 2:
                        pe.wait_ge(s_lsub, 1)
                    for j in range(3):
                        pe.wait_ge(s_prod, 3 * c + j + 1)
                        mm = pe.matmul(PS[:, 3 * (c % 2) + j, 0:CW], W["blocks"], PR[:, j, CENTRES[c]], start=True,
                                       stop=True)
                    mm.then_inc(s_lsc, 1)

                def turn_sums(c):
                    pe.wait_ge(s_lsum, 2 * c + 2)
                    for k in range(3):
                        mm = pe.matmul(PS[0:TW, TURN_BANK[c], k * HEADS:(k + 1) * HEADS],
                                       LM[:, c * CW + k * TW:c * CW + (k + 1) * TW], ident[:, 0:P:HD], start=True,
                                       stop=True)
                    mm.then_inc(s_lst, 1)

                def spread(c):
                    pe.wait_ge(s_lrw, c + 1)
                    for k in range(3):
                        mm = pe.matmul(PS[:, SPREAD_BANK[c], k * TW:(k + 1) * TW],
                                       LRW[:, c, k * HEADS:(k + 1) * HEADS, :].rearrange("p h d -> p (h d)"),
                                       ident[0:TW, 0:TW], start=True, stop=True)
                    mm.then_inc(s_lex, 1)

                def join(c):
                    pe.wait_ge(s_la, c + 1)
                    pe.wait_ge(s_lsub, 3)
                    for t in TILES_AT[c]:
                        o = PS[:, MIX_BANK[t // HT], (t % HT) * P:(t % HT + 1) * P]
                        pe.matmul(o, LA[:, t * P:(t + 1) * P], W["wfb_f"], start=True, stop=False)
                        pe.matmul(o, LA[:, t * P + 2:(t + 1) * P + 2], W["wfb_r"], start=False, stop=False)
                        pe.matmul(o, XT[:, t * P:(t + 1) * P], ident, start=False, stop=True).then_inc(s_lz, 1)

                scores(0)
                scores(1)
                scores(2)
                turn_sums(0)
                turn_sums(1)
                spread(0)
                turn_sums(2)
                spread(1)
                join(0)
                spread(2)
                join(1)
                join(2)

            @block.scalar
            def _(act):
                for k, (i, h) in enumerate(HALVES):
                    v, b = ((LQ, "L0_attn_bq"), (LK, "L0_attn_bk"), (LV, "L0_attn_bv"))[i]
                    act.wait_ge(s_lp, k + 1)
                    act.activation(v[:, 2 + h * HALF:2 + (h + 1) * HALF], PS[:, k, :], ACT.Identity,
                                   bias=C[b]).then_inc(s_lq, 1)
                for c in range(CHUNKS):
                    act.wait_ge(s_lsub, c + 1)
                    act.activation(PR[:, :, CENTRES[c]], PR[:, :, CENTRES[c]], ACT.Exp,
                                   scale=float(HD) ** -0.5).then_inc(s_lexp, 1)
                for c in range(CHUNKS):
                    act.wait_ge(s_lrc, c + 1)
                    act.activation(LRW[:, c, :, :], LRN[:, c, :, :].rearrange("p k h -> p (k h)").unsqueeze(2)
                                   .broadcast_to([TW, 3 * HEADS, HD]), ACT.Copy).then_inc(s_lrw, 1)

            @block.gpsimd
            def _(pool):
                for v in (LQ, LK, LV):
                    pool.memset(v[:, 0:2], 0.0).then_inc(s_pad, 1)
                    pool.memset(v[:, PADW - 2:PADW], 0.0).then_inc(s_pad, 1)
                pool.wait_ge(s_pad, 6)
                pool.wait_ge(s_lq, 6)
                for c in range(CHUNKS):
                    pool.wait_ge(s_lexp, c + 1)
                    for j in range(3):
                        pool.tensor_tensor(PV[:, j, CENTRES[c]], PR[:, j, CENTRES[c]],
                                           LV[:, c * CW + j:(c + 1) * CW + j], ALU.mult).then_inc(s_lpv, 1)

            @block.vector
            def _(dve):
                def products(c):
                    dve.wait_ge(s_lq, 2 if c == 0 else 4)
                    for j in range(3):
                        dve.tensor_tensor(PR[:, j, CENTRES[c]], LQ[:, c * CW + 1:(c + 1) * CW + 1],
                                          LK[:, c * CW + j:(c + 1) * CW + j], ALU.mult).then_inc(s_prod, 1)

                def shift(c):
                    b = 3 * (c % 2)
                    s = PS[:, b:b + 3, 0:CW]
                    dve.wait_ge(s_lsc, c + 1)
                    dve.tensor_reduce(LM[:, CENTRES[c]], s.rearrange("p j q -> p q j"), AX.X,
                                      ALU.max).then_inc(s_lmx, 1)
                    dve.wait_ge(s_lmx, c + 1)
                    dve.tensor_tensor(PR[:, :, CENTRES[c]], s, LM[:, CENTRES[c]].unsqueeze(1).broadcast_to([P, 3, CW]),
                                      ALU.subtract).then_inc(s_lsub, 1)

                def add_up(c):
                    dve.wait_ge(s_lexp, c + 1)
                    dve.tensor_tensor(LM[:, CENTRES[c]], PR[:, 0, CENTRES[c]], PR[:, 1, CENTRES[c]],
                                      ALU.add).then_inc(s_lsum, 1)
                    dve.wait_ge(s_lsum, 2 * c + 1)
                    dve.tensor_tensor(LM[:, CENTRES[c]], LM[:, CENTRES[c]], PR[:, 2, CENTRES[c]],
                                      ALU.add).then_inc(s_lsum, 1)

                def invert(c):
                    dve.wait_ge(s_lst, c + 1)
                    dve.reciprocal(LRN[:, c, :, :], PS[0:TW, TURN_BANK[c], 0:3 * HEADS].rearrange(
                        "p (k h) -> p k h", h=HEADS)).then_inc(s_lrc, 1)

                def add_values(c):
                    dve.wait_ge(s_lpv, 3 * c + 3)
                    dve.tensor_tensor(LA[:, CENTRES[c]], PV[:, 0, CENTRES[c]], PV[:, 1, CENTRES[c]],
                                      ALU.add).then_inc(s_lpa, 1)
                    dve.wait_ge(s_lpa, 2 * c + 1)
                    dve.tensor_tensor(LA[:, CENTRES[c]], LA[:, CENTRES[c]], PV[:, 2, CENTRES[c]],
                                      ALU.add).then_inc(s_lpa, 1)

                def divide(c):
                    dve.wait_ge(s_lex, c + 1)
                    dve.wait_ge(s_lpa, 2 * c + 2)
                    dve.tensor_tensor(LA[:, CENTRES[c]], LA[:, CENTRES[c]], PS[:, SPREAD_BANK[c], 0:CW],
                                      ALU.mult).then_inc(s_la, 1)

                dve.wait_ge(s_pad, 4)
                products(0)
                products(1)
                products(2)
                shift(0)
                shift(1)
                add_up(0)
                shift(2)
                add_up(1)
                invert(0)
                add_up(2)
                invert(1)
                add_values(0)
                divide(0)
                invert(2)
                add_values(1)
                divide(1)
                add_values(2)
                divide(2)
                for h in range(2):
                    dve.wait_ge(s_lz, (h + 1) * HT)
                    dve.tensor_tensor(NAT[:, h * HT:(h + 1) * HT, :],
                                      PS[:, MIX_BANK[h], :].rearrange("p (t d) -> p t d", d=P),
                                      R["L0_attn_bfb"].unsqueeze(1).broadcast_to([P, HT, P]),
                                      ALU.add).then_inc(s_lzc, 1)

        s_fa, s_fac, s_fm, s_fmc = (sem(n) for n in ("mix_parts", "mix_parts_copied", "mix_matrix", "mix_matrix_copied"))

        def mixing_products(pe):
            pe.wait_ge(s_late, 16)
            pe.matmul(PS[:, 2, 0:P], W["wr"], W["cos"], start=True, stop=False)
            pe.matmul(PS[:, 2, 0:P], W["wi"], W["sin"], start=False, stop=True).then_inc(s_fa, 1)
            pe.matmul(PS[:, 3, 0:P], W["wi"], W["cos"], start=True, stop=False)
            pe.matmul(PS[:, 3, 0:P], W["wr"], W["nsin"], start=False, stop=True).then_inc(s_fa, 1)
            pe.wait_ge(s_fac, 2)
            pe.matmul(PS[:, 2, 0:P], AMT[:, 0, :], W["cos"], start=True, stop=False)
            pe.matmul(PS[:, 2, 0:P], AMT[:, 1, :], W["nsin"], start=False, stop=True).then_inc(s_fm, 1)

        def mixing_copies(act):
            for k in range(2):
                act.wait_ge(s_fa, k + 1)
                act.activation(AMT[:, k, :], PS[:, 2 + k, 0:P], ACT.Copy).then_inc(s_fac, 1)
            act.wait_ge(s_fm, 1)
            act.activation(MIX[:, :], PS[:, 2, 0:P], ACT.Copy, scale=1.0 / P).then_inc(s_fmc, 1)

        norm_stage(NAT, NAT, 1e-6, scale=C["L0_attn_g2"][:, 0:1], bias=C["L0_attn_b2"][:, 0:1], alongside=late_loads,
                   with_pe=mixing_products, with_act=mixing_copies)

        lin = {"n": 0}
        s_lin, s_linb, s_ling, s_linx, s_lwait = (sem(n) for n in ("linear_done", "linear_biased", "linear_gelu", "linear_added", "linear_weights"))

        def linear_stage(weight, bias_row, gelu, meanwhile=None):
            n = lin["n"]
            g = lin.setdefault("g", 0)
            lin["n"] += 1
            lin["g"] += int(gelu)
            with nc.Block() as block:
                if meanwhile is not None:
                    block.gpsimd(meanwhile)

                @block.tensor
                def _(pe):
                    for t in range(TT):
                        pe.matmul(PS[:, t // HT, (t % HT) * P:(t % HT + 1) * P], XT[:, t * P:(t + 1) * P],
                                  weight, start=True, stop=True).then_inc(s_lin, 1)

                @block.vector
                def _(dve):
                    for h in range(2):
                        dve.wait_ge(s_lin, n * TT + (h + 1) * HT)
                        dve.tensor_tensor(NAT[:, h * HT:(h + 1) * HT, :],
                                          PS[:, h, :].rearrange("p (t d) -> p t d", d=P),
                                          bias_row.unsqueeze(1).broadcast_to([P, HT, P]),
                                          ALU.add).then_inc(s_linb, 1)
                    for h in range(2):
                        if gelu:
                            dve.wait_ge(s_ling, 2 * g + h + 1)
                        else:
                            dve.wait_ge(s_linb, 2 * n + h + 1)
                        v = X[:, h * HT:(h + 1) * HT, :]
                        dve.tensor_tensor(v, v, NAT[:, h * HT:(h + 1) * HT, :], ALU.add).then_inc(s_linx, 1)

                if gelu:
                    @block.scalar
                    def _(act):
                        for h in range(2):
                            act.wait_ge(s_linb, 2 * n + h + 1)
                            v = NAT[:, h * HT:(h + 1) * HT, :]
                            act.activation(v, v, ACT.Gelu).then_inc(s_ling, 1)

        linear_stage(W["L0_attn_Wo"][:, :], R["L0_attn_bo"][:, :], True)

        LOTS = (KT + 3) // 4
        with nc.Block() as block:
            @block.tensor
            def _(pe):
                pe.wait_ge(s_ctx, 32)
                for b in range(LOTS):
                    if b >= 4:
                        pe.wait_ge(s_ctx_lo, b - 3)
                    for t in range(4 * b, min(4 * b + 4, KT)):
                        mm = pe.transpose(PS[:, b % 4, (t % 4) * P:(t % 4 + 1) * P], CN[:, t, :], ident[:, :])
                    mm.then_inc(s_ctx_turned, 1)
                pe.transpose(PS[:, 4, 0:TAIL], VTAIL[:, :], ident[0:TAIL, 0:TAIL]).then_inc(s_ctx_turned, 1)

            def part(b):
                if b < LOTS:
                    w = min(4 * P, KT * P - 4 * b * P)
                    return PS[:, b % 4, 0:w], slice(4 * b * P, 4 * b * P + w)
                return PS[:, 4, 0:TAIL], slice(KT * P, CTX)

            @block.scalar
            def _(act):
                for b in range(LOTS + 1):
                    src, cols = part(b)
                    act.wait_ge(s_ctx_turned, b + 1)
                    act.activation(CTH[:, cols], src, ACT.Copy).then_inc(s_ctx_hi, 1)

            @block.vector
            def _(dve):
                for b in range(LOTS + 1):
                    src, cols = part(b)
                    dve.wait_ge(s_ctx_hi, b + 1)
                    dve.tensor_tensor(CTL[:, cols], src, CTH[:, cols], ALU.subtract).then_inc(s_ctx_lo, 1)

        s_q, s_qs, s_qf, s_qh, s_ql, s_cb, s_cbs = (sem(n) for n in (
            "cross_q", "cross_q_biased", "cross_q_folded", "cross_q_high", "cross_q_low", "cross_key_bias", "cross_key_bias_kept"))
        s_sc, s_scc, s_mx, s_mxf, s_mt, s_mr, s_dg, s_mb = (sem(n) for n in (
            "cross_scores", "cross_scores_copied", "cross_max", "cross_max_joined", "cross_max_turned",
            "cross_max_rows", "cross_max_diagonal", "cross_max_spread"))
        s_sub, s_pr, s_pv, s_sv, s_sp, s_ot = (sem(n) for n in (
            "cross_shifted", "cross_probs", "cross_values", "cross_sum_vector", "cross_sum_pool", "cross_out_turned"))
        s_va, s_vb = sem("values_in_a"), sem("values_in_b")
        s_l, s_rl, s_on, s_of = sem("cross_sums"), sem("cross_sum_recip"), sem("cross_out"), sem("cross_finished")
        QF = work(KT * HALF - TOKENS, TOKENS)
        CB = sb("CB", [P, TT])
        xc = {"n": 0}

        def query_stage(w_query, query_bias, w_fold, key_bias):
            n = xc["n"]
            with nc.Block() as block:
                @block.tensor
                def _(pe):
                    for h in range(2):
                        pe.matmul(PS[:, h, :], w_query, XT[:, h * HALF:(h + 1) * HALF], start=True,
                                  stop=True).then_inc(s_q, 1)
                    for h in range(2):
                        pe.wait_ge(s_qs, 2 * n + h + 1)
                        pe.matmul(PS[:, 2 + h, :], w_fold, QF[:, h * HALF:(h + 1) * HALF], start=True,
                                  stop=True).then_inc(s_qf, 1)
                    for t in range(TT):
                        mm = pe.matmul(PS[:, 4, t:t + 1], QF[:, t * P:(t + 1) * P], key_bias, start=True, stop=True)
                    mm.then_inc(s_cb, 1)

                @block.scalar
                def _(act):
                    for h in range(2):
                        act.wait_ge(s_q, 2 * n + h + 1)
                        act.activation(QF[:, h * HALF:(h + 1) * HALF], PS[:, h, :], ACT.Identity,
                                       bias=query_bias).then_inc(s_qs, 1)
                    for h in range(2):
                        act.wait_ge(s_qf, 2 * n + h + 1)
                        act.activation(QH[:, h * HALF:(h + 1) * HALF], PS[:, 2 + h, :], ACT.Copy).then_inc(s_qh, 1)

                @block.vector
                def _(dve):
                    for h in range(2):
                        dve.wait_ge(s_qh, 2 * n + h + 1)
                        dve.tensor_tensor(QL[:, h * HALF:(h + 1) * HALF], PS[:, 2 + h, :],
                                          QH[:, h * HALF:(h + 1) * HALF], ALU.subtract).then_inc(s_ql, 1)
                    dve.wait_ge(s_cb, n + 1)
                    dve.tensor_copy(CB[:, :], PS[:, 4, 0:TT]).then_inc(s_cbs, 1)

        SCORE_BANKS = 5
        TILES = KT + 1
        STEPS = KT // STEP
        DVE_SUMS = ((), (1, 4, 6, 9))
        POOL_SUMS = tuple(tuple(u for u in range(STEP) if u not in d) for d in DVE_SUMS)

        def sums_before(n, mine, tail):
            return sum(STEPS * len(mine[m % 2]) + tail for m in range(n))

        def attend_stage(values_of, scores_of, meanwhile=None):
            v, s = values_of, scores_of
            n = xc["n"]
            nv = 2 * n + v if v is not None else None
            ns = 2 * n + s if s is not None else None
            vbase = nv * TILES if v is not None else 0
            sbase = ns * TILES if s is not None else 0
            both = v is not None and s is not None
            copy_lag, max_lag = (2, 3) if both else (0, 0)
            if v is not None:
                dsums, psums = DVE_SUMS[v], POOL_SUMS[v]
                dbase, pbase = sums_before(nv, DVE_SUMS, 0), sums_before(nv, POOL_SUMS, 1)
            if s is not None:
                qh, ql = QH[:, s * HALF:(s + 1) * HALF], QL[:, s * HALF:(s + 1) * HALF]

            def slot(j):
                return BIG[:, bass.ds(j * HALF, HALF)]

            tail_slot = BIG[0:TAIL, KT * HALF:(KT + 1) * HALF]

            def in_steps(eng, part):
                for u in range(STEP):
                    part(0, u, True)
                with eng.Fori(1, STEPS) as i:
                    for u in range(STEP):
                        part(i, u, False)

            with nc.Block() as block:
                if meanwhile is not None:
                    block.gpsimd(meanwhile)

                if v is not None:
                    @block.sync
                    def _(sp):
                        lots = nv * 2 * STEPS

                        def lot(i, k, first):
                            if not first:
                                sp.wait_ge(s_pv, vbase + (i - 1) * STEP + (k + 1) * RING)
                            src = ctx_main[:, bass.ds(i * STEP + k * RING, RING), :]
                            sp.dma_start(VR[:, k * RING:(k + 1) * RING, :], src
                                         ).then_inc(s_va if k == 0 else s_vb, 16)

                        lot(0, 0, True)
                        lot(0, 1, True)
                        with sp.Fori(1, STEPS) as i:
                            lot(i, 0, False)
                            lot(i, 1, False)

                @block.tensor
                def _(pe):
                    def score(i, u, first):
                        j = i * STEP + u
                        if not (first and u < SCORE_BANKS):
                            pe.wait_ge(s_scc, sbase + j - SCORE_BANKS + 1)
                        kh, kl = CTH[:, bass.ds(j * P, P)], CTL[:, bass.ds(j * P, P)]
                        o = PS[:, u % SCORE_BANKS, :]
                        pe.matmul(o, kh, qh, start=True, stop=False)
                        pe.matmul(o, kh, ql, start=False, stop=False)
                        pe.matmul(o, kl, qh, start=False, stop=True).then_inc(s_sc, 1)

                    def mix(i, u, first):
                        j = i * STEP + u
                        if u % RING == 0:
                            pe.wait_ge(s_va if u == 0 else s_vb, 16 * (nv * STEPS + 1) + 16 * i)
                        pe.wait_ge(s_pr, vbase + j + 1)
                        pe.matmul(PS[:, 5, :], VR[:, u, :], slot(j), start=(first and u == 0), stop=False,
                                  skip_group_check=True).then_inc(s_pv, 1)

                    def part(i, u, first):
                        if s is not None:
                            score(i, u, first)
                        if v is not None:
                            mix(i, u, first)

                    in_steps(pe, part)
                    if s is not None:
                        pe.wait_ge(s_scc, sbase + KT - SCORE_BANKS + 1)
                        o = PS[0:TAIL, 0, :]
                        pe.matmul(o, CTH[:, KT * P:CTX], qh, start=True, stop=False)
                        pe.matmul(o, CTH[:, KT * P:CTX], ql, start=False, stop=False)
                        pe.matmul(o, CTL[:, KT * P:CTX], qh, start=False, stop=True).then_inc(s_sc, 1)
                    if v is not None:
                        pe.wait_ge(s_pr, vbase + TILES)
                        pe.matmul(PS[:, 5, :], VTAIL[:, :], tail_slot, start=False, stop=True,
                                  skip_group_check=True).then_inc(s_pv, 1)
                        summed = [e for e in range(2) if (dsums, psums)[e]]
                        if dsums:
                            pe.wait_ge(s_sv, dbase + STEPS * len(dsums))
                        pe.wait_ge(s_sp, pbase + STEPS * len(psums) + 1)
                        for k in range(HT):
                            for e in summed:
                                mm = pe.matmul(PS[:, 7, v * HT + k:v * HT + k + 1], LS[:, e, k * P:(k + 1) * P],
                                               ONES[:, 0:1], start=(e == summed[0]), stop=(e == 1))
                        mm.then_inc(s_l, 1)
                    if s is not None:
                        if v is not None:
                            pe.wait_ge(s_rl, nv + 1)
                            pe.wait_ge(s_sub, vbase + TILES)
                        pe.wait_ge(s_mxf, ns + 1)
                        for k in range(HT):
                            mm = pe.transpose(PS[:, 7, k * P:(k + 1) * P], RM[:, 0, k * P:(k + 1) * P], ident[:, :])
                        mm.then_inc(s_mt, 1)
                        pe.wait_ge(s_dg, HT * (ns + 1))
                        pe.matmul(PS[:, 6, :], ONES[:, :], DG[:, :, :].rearrange("p a b -> p (a b)"), start=True,
                                  stop=True).then_inc(s_mb, 1)

                @block.scalar
                def _(act):
                    def exp(i, u):
                        j = i * STEP + u
                        act.wait_ge(s_sub, vbase + j + 1)
                        act.activation(slot(j), slot(j), ACT.Exp).then_inc(s_pr, 1)

                    def keep(i, u):
                        j = i * STEP + u
                        if v is not None:
                            act.wait_ge(s_pv, vbase + j + 1)
                            act.wait_ge(s_sp, pbase + j + 1)
                        act.wait_ge(s_sc, sbase + j + 1)
                        to = BIG[:, bass.ds(i * (STEP * HALF) + u * HALF, HALF)]
                        act.activation(to, PS[:, u % SCORE_BANKS, :], ACT.Copy).then_inc(s_scc, 1)

                    def part(i, u, first):
                        if v is not None:
                            exp(i, u)
                        if s is not None and not (first and u < copy_lag):
                            keep(i, u - copy_lag)

                    in_steps(act, part)
                    if v is not None:
                        act.wait_ge(s_sub, vbase + TILES)
                        act.activation(tail_slot, tail_slot, ACT.Exp).then_inc(s_pr, 1)
                    if s is not None:
                        for u in range(copy_lag):
                            keep(STEPS, u - copy_lag)
                        if v is not None:
                            act.wait_ge(s_pv, vbase + TILES)
                            act.wait_ge(s_sp, pbase + TILES)
                        act.wait_ge(s_sc, sbase + TILES)
                        act.activation(tail_slot, PS[0:TAIL, 0, :], ACT.Copy).then_inc(s_scc, 1)

                def keep_mix(dve):
                    dve.wait_ge(s_pv, vbase + TILES)
                    dve.tensor_copy(OT[:, v * HALF:(v + 1) * HALF], PS[:, 5, :]).then_inc(s_ot, 1)

                @block.vector
                def _(dve):
                    def shift(i, u):
                        j = i * STEP + u
                        dve.tensor_tensor(slot(j), slot(j), PS[:, 6, :], ALU.subtract).then_inc(s_sub, 1)

                    def add(i, u, first):
                        k = dsums.index(u)
                        j = i * STEP + u
                        dve.wait_ge(s_pr, vbase + j + 1)
                        if first and k == 0:
                            dve.tensor_copy(LS[:, 0, :], slot(j)).then_inc(s_sv, 1)
                        else:
                            dve.wait_ge(s_sv, dbase + i * len(dsums) + k)
                            dve.tensor_tensor(LS[:, 0, :], slot(j), LS[:, 0, :], ALU.add).then_inc(s_sv, 1)

                    def maximum(i, u, first):
                        j = i * STEP + u
                        r = RM[:, u % 2, :]
                        dve.wait_ge(s_scc, sbase + j + 1)
                        if first and u < 2:
                            dve.tensor_copy(r, slot(j)).then_inc(s_mx, 1)
                        else:
                            dve.wait_ge(s_mx, sbase + j - 1)
                            dve.tensor_tensor(r, slot(j), r, ALU.max).then_inc(s_mx, 1)

                    def part(i, u, first):
                        if v is not None:
                            shift(i, u)
                            if u - 2 in dsums:
                                add(i, u - 2, first)
                            if u == STEP - 1:
                                for w in dsums:
                                    if w + 2 >= STEP:
                                        add(i, w, first)
                        if s is not None and not (first and u < max_lag):
                            maximum(i, u - max_lag, first)

                    in_steps(dve, part)
                    if v is not None:
                        dve.tensor_tensor(tail_slot, tail_slot, PS[0:TAIL, 6, :], ALU.subtract).then_inc(s_sub, 1)
                    if s is not None:
                        for u in range(max_lag):
                            maximum(STEPS, u - max_lag, False)
                        dve.wait_ge(s_scc, sbase + TILES)
                        dve.wait_ge(s_mx, sbase + KT - 1)
                        dve.tensor_tensor(RM[0:TAIL, 0, :], tail_slot, RM[0:TAIL, 0, :], ALU.max).then_inc(s_mx, 1)
                        dve.wait_ge(s_mx, sbase + TILES)
                        dve.tensor_tensor(RM[:, 0, :], RM[:, 0, :], RM[:, 1, :], ALU.max).then_inc(s_mxf, 1)
                    if v is not None:
                        dve.wait_ge(s_l, nv + 1)
                        dve.reciprocal(RL[:, v * HT:(v + 1) * HT], PS[:, 7, v * HT:(v + 1) * HT]).then_inc(s_rl, 1)
                        if s is None:
                            keep_mix(dve)
                    if s is not None:
                        dve.wait_ge(s_mt, ns + 1)
                        dve.tensor_reduce(MX[:, :], PS[:, 7, :].rearrange("p (k q) -> p k q", q=P), AX.X,
                                          ALU.max).then_inc(s_mr, 1)
                        cb = CB[:, s * HT:(s + 1) * HT]
                        dve.wait_ge(s_mr, 3 * ns + 1)
                        dve.tensor_tensor(MC[:, :], MX[:, :], cb, ALU.add).then_inc(s_mr, 1)
                        dve.wait_ge(s_mr, 3 * ns + 2)
                        dve.tensor_tensor(MX[:, :], MC[:, :], cb, ALU.subtract).then_inc(s_mr, 1)
                        dve.wait_ge(s_mr, 3 * ns + 3)
                        for k in range(HT):
                            dve.tensor_scalar(DG[:, k, :], ident[:, :], MX[:, k:k + 1], None,
                                              ALU.mult).then_inc(s_dg, 1)
                        if v is not None:
                            keep_mix(dve)

                if v is not None:
                    @block.gpsimd
                    def _(pool):
                        def part(i, u, first):
                            if u not in psums:
                                return
                            k = psums.index(u)
                            j = i * STEP + u
                            pool.wait_ge(s_pr, vbase + j + 1)
                            if first and k == 0:
                                pool.tensor_copy(LS[:, 1, :], slot(j)).then_inc(s_sp, 1)
                            else:
                                pool.wait_ge(s_sp, pbase + i * len(psums) + k)
                                pool.tensor_tensor(LS[:, 1, :], slot(j), LS[:, 1, :], ALU.add).then_inc(s_sp, 1)

                        in_steps(pool, part)
                        pool.wait_ge(s_pr, vbase + TILES)
                        pool.wait_ge(s_sp, pbase + STEPS * len(psums))
                        l = LS[0:TAIL, 1, :]
                        pool.tensor_tensor(l, tail_slot, l, ALU.add).then_inc(s_sp, 1)

        def attend(meanwhile=None):
            attend_stage(None, 0, meanwhile)
            attend_stage(0, 1)
            attend_stage(1, None)

        def mix_stage(w_value, dst, base, meanwhile=None, loads=None):
            n = xc["n"]
            with nc.Block() as block:
                if meanwhile is not None:
                    block.gpsimd(meanwhile)

                if loads is not None:
                    block.sync(loads)

                @block.tensor
                def _(pe):
                    for t in range(TT):
                        pe.matmul(PS[:, t // HT, (t % HT) * P:(t % HT + 1) * P], OT[:, t * P:(t + 1) * P],
                                  w_value, start=True, stop=True).then_inc(s_on, 1)

                @block.vector
                def _(dve):
                    for t in range(TT):
                        dve.wait_ge(s_on, n * TT + (t // HT + 1) * HT)
                        dve.scalar_tensor_tensor(out=dst[:, t, :], in0=PS[:, t // HT, (t % HT) * P:(t % HT + 1) * P],
                                                 scalar=RL[:, t:t + 1], in1=base[:, t, :], op0=ALU.mult,
                                                 op1=ALU.add).then_inc(s_of, 1)
            xc["n"] += 1

        ROLES = ((0, 0), (0, 1), (1, 0), (0, 2), (2, 0), (1, 1))
        PAIRS_ALL = HEADS // 2
        HROWS = P // 2
        MAXROW = HD * len(ROLES)

        def work16(at, *shape):
            v = BIG[:, at:at + shape[0] * shape[1] // 2].bitcast(BF16)
            return v.rearrange("p (a b) -> p a b", b=shape[1])

        QS = work16(0, HEADS, TOKENS)
        KS = work16(8192, PAIRS_ALL, TOKENS)
        VA = work(12288, TT, HEADS, STRIP)
        PB = work(16384, 3 * HPG, HALF).rearrange("p (s i) q -> p s i q", i=HPG)
        QP = work16(16384, 3, TOKENS)
        KP = work16(17920, 3, TOKENS)
        AT3 = work(22528, GROUPS - 1, TOKENS)
        AT = [AT3[:, g, :] for g in range(GROUPS - 1)] + [OT[:, :]]
        RST = sb("RST", [P, 2, HALF])
        LOTS = 2 * GROUPS
        MXC = sb("MXC", [P, LOTS, HT, HPG, 2])
        MXN = sb("MXN", [P, HT, HPG])
        MXL = sb("MXL", [P, HT, HPG])
        MXP = sb("MXP", [P, HT, HPG, 3], BF16)
        MP = sb("MP", [3 * HPG, HALF], BF16)
        s_cq0, s_ck1, s_cv0 = (sem(n) for n in ("causal_q_cleared", "causal_k_ones", "causal_v_set"))
        TWO_ONES = 1.0 + 0x3F80 * 2.0 ** -23

        def clear_queries(pool, k):
            heads = slice(k * HEADS // 2, (k + 1) * HEADS // 2)
            pool.memset(QS[:, heads, :].bitcast(F32), 0.0).then_inc(s_cq0, 1)

        def ones_in_keys(pool, a):
            pool.memset(KS[HROWS * a + STRIP:HROWS * (a + 1), :, :].bitcast(F32), TWO_ONES).then_inc(s_ck1, 1)

        def ones_in_values(pool):
            pool.memset(VA, 0.0).then_inc(s_cv0, 1)
            pool.wait_ge(s_cv0, 1)
            pool.memset(VA[:, :, :, HD:HD + 1], 1.0).then_inc(s_cv0, 1)

        norm_stage(X, XN, 1e-5)
        def over_tokens(row):
            return row.unsqueeze(1).broadcast_to([P, TT, P])

        s_pb = sem("rows_added")

        def add_biases(pool):
            pool.tensor_tensor(XN[:, :, :], XN[:, :, :], over_tokens(R["L0_xattn_bv"]), ALU.add).then_inc(s_pb, 1)
            pool.tensor_tensor(X[:, :, :], X[:, :, :], over_tokens(R["L0_xattn_beta"]), ALU.add).then_inc(s_pb, 1)

        query_stage(W["L0_xattn_Wq"][:, :], C["L0_xattn_bq"][:, 0:1], W["xwk_t"][:, :], C["L0_xattn_bk"][:, 0:1])
        attend(add_biases)
        mix_stage(W["L0_xattn_Wv"], NAT, XN, meanwhile=ones_in_values)

        norm_stage(NAT, NAT, 1e-5, turn=False, gain=R["L0_xattn_gamma"], pool_after=lambda pool: clear_queries(pool, 0))

        norm_stage(X, XN, 1e-5, pool_after=lambda pool: clear_queries(pool, 1))
        linear_stage(MIX[:, :], R["L0_ffn_bias"], False, lambda pool: ones_in_keys(pool, 0))

        norm_stage(X, XN, 1e-5)
        s_cp, s_ch, s_cr1, s_cm, s_cl, s_cv, s_cst, s_cst2 = (sem(n) for n in (
            "causal_projected", "causal_high", "causal_rest", "causal_middle", "causal_low", "causal_values",
            "causal_stacked", "causal_keys_high_stacked"))
        with nc.Block() as block:
            def stack(eng, dst, src, side, roles, done, stacked):
                if side:
                    eng.wait_ge(s_ck1, 2)
                else:
                    eng.wait_ge(s_cq0, 2)
                for r in roles:
                    part = ROLES[r][side]
                    eng.wait_ge(done[part][0], done[part][1])
                    for a in range(2):
                        row = HROWS * a + HD * r
                        to = dst[row:row + HD, :, :] if side else dst[row:row + HD, a:HEADS:2, :]
                        eng.dma_start(to, src[HROWS * a:HROWS * (a + 1), part, :]
                                      ).then_inc(stacked, 16)

            @block.gpsimd
            def _(pool):
                ones_in_keys(pool, 1)
                stack(pool, KS, KP, 1, (0, 2, 4), ((s_ch, 4),), s_cst2)

            @block.tensor
            def _(pe):
                for u in range(4):
                    w = W["wqc_t"] if u < 2 else W["wkc_t"]
                    pe.matmul(PS[:, u, :], w[:, :], XT[:, (u % 2) * HALF:(u % 2 + 1) * HALF], start=True,
                              stop=True).then_inc(s_cp, 1)
                for t in range(TT):
                    pe.matmul(PS[:, 4 + t // HT, (t % HT) * P:(t % HT + 1) * P], XT[:, t * P:(t + 1) * P],
                              W["wvc_t"][:, :], start=True, stop=True).then_inc(s_cp, 1)

            def parts(u):
                cols = slice((u % 2) * HALF, (u % 2 + 1) * HALF)
                return [(QP if u < 2 else KP)[:, k, cols] for k in range(3)]

            @block.scalar
            def _(act):
                for u in range(4):
                    act.wait_ge(s_cp, u + 1)
                    act.activation(parts(u)[0], PS[:, u, :], ACT.Copy).then_inc(s_ch, 1)
                for u in range(4):
                    act.wait_ge(s_cr1, u + 1)
                    act.activation(parts(u)[1], RST[:, u % 2, :], ACT.Copy).then_inc(s_cm, 1)
                stack(act, KS, KP, 1, (1, 5, 3), ((s_ch, 4), (s_cm, 4), (s_cl, 4)), s_cst)

            @block.vector
            def _(dve):
                def rest(u):
                    dve.wait_ge(s_ch, u + 1)
                    if u >= 2:
                        dve.wait_ge(s_cl, u - 1)
                    dve.tensor_tensor(RST[:, u % 2, :], PS[:, u, :], parts(u)[0], ALU.subtract).then_inc(s_cr1, 1)

                def low(u):
                    dve.wait_ge(s_cm, u + 1)
                    dve.tensor_tensor(parts(u)[2], RST[:, u % 2, :], parts(u)[1], ALU.subtract).then_inc(s_cl, 1)

                rest(0)
                rest(1)
                low(0)
                rest(2)
                low(1)
                rest(3)
                low(2)
                low(3)
                dve.wait_ge(s_cv0, 2)
                for h in range(2):
                    dve.wait_ge(s_cp, 4 + (h + 1) * HT)
                    dve.tensor_copy(VA[:, h * HT:(h + 1) * HT, :, 0:HD],
                                    PS[:, 4 + h, :].rearrange("p (t h d) -> p t h d", h=HEADS, d=HD)
                                    ).then_inc(s_cv, 1)

            @block.sync
            def _(sp):
                stack(sp, QS, QP, 0, (0, 1, 3, 2, 5, 4), ((s_ch, 2), (s_cm, 2), (s_cl, 2)), s_cst)

        s_c1, s_c1m, s_c1j, s_c1k, s_c1n, s_c1q = (sem(n) for n in (
            "causal_rows", "causal_rows_used", "causal_row_max_joined", "causal_max_rest", "causal_max_part",
            "causal_q_with_max"))
        s_c2, s_c2e, s_c2v, s_c2a = (sem(n) for n in ("causal_scores", "causal_probs", "causal_mixed", "causal_mix_kept"))
        SHORT_AT_END = 2
        LOT = ([(g, 0) for g in range(GROUPS - SHORT_AT_END)] + [(g, 1) for g in range(GROUPS)]
               + [(g, 0) for g in range(GROUPS - SHORT_AT_END, GROUPS)])
        TURN_AFTER = 6
        WHILE_TURNED = 10
        ITEMS, LAST_ROW = [], []
        for lot, (g, h) in enumerate(LOT):
            rows_of_lot = [("rows", lot, t, c, i) for t in range(h * HT, (h + 1) * HT) for c in range(h + 1)
                           for i in range(HPG)]
            if lot >= 1:
                rows_of_lot.insert(TURN_AFTER, ("turn", lot - 1))
            ITEMS += rows_of_lot
            LAST_ROW.append(len(ITEMS))
        ITEMS.append(("turn", LOTS - 1))
        STEPS2 = [(lot, k) for lot, (g, h) in enumerate(LOT) for k in range((h + 1) * HT)]
        N2 = len(STEPS2)
        START2 = [STEPS2.index((lot, 0)) for lot in range(LOTS)]
        END2 = START2[1:] + [N2]

        def columns(h, k):
            first = max(0, k * P - h * HALF)
            return first, HALF - first

        def row_width(t, c):
            return min(HALF, (t + 1) * P - c * HALF)

        def item_work(item):
            return 0 if item[0] == "turn" else row_width(item[2], item[3]) + 64

        def plan():
            turn_at = [ITEMS.index(("turn", lot)) + 1 for lot in range(LOTS)]
            ahead = turn_at[0] + WHILE_TURNED
            done, per_step = ahead, []
            for n in range(N2):
                quota = 0.0
                for lot in range(LOTS):
                    steps = START2[lot] - 2 - n
                    if turn_at[lot] > done:
                        need = sum(item_work(i) for i in ITEMS[done:turn_at[lot]])
                        mine = columns(LOT[STEPS2[n][0]][1], STEPS2[n][1])[1]
                        span = sum(columns(LOT[STEPS2[m][0]][1], STEPS2[m][1])[1] for m in range(n, n + max(steps, 1)))
                        quota = max(quota, need * mine / span)
                upto = done
                while upto < len(ITEMS) and quota > 0:
                    quota -= item_work(ITEMS[upto])
                    upto += 1
                if len(ITEMS) - upto == 1:
                    upto += 1
                per_step.append(range(done, upto))
                done = upto
            return ahead, per_step

        AHEAD, WITH_STEP = plan()
        BANK = [((4, 5, 7, 0, 1, 2, 3)[j % 7] if j < AHEAD else (4, 5, 7)[j % 3]) for j in range(len(ITEMS))]
        USER_BEFORE = [max([m for m in range(j) if BANK[m] == BANK[j]], default=None) for j in range(len(ITEMS))]

        with nc.Block() as block:
            @block.tensor
            def _(pe):
                def pass1(j):
                    item, b = ITEMS[j], BANK[j]
                    if USER_BEFORE[j] is not None:
                        pe.wait_ge(s_c1m, USER_BEFORE[j] + 1)
                    if item[0] == "turn":
                        pe.wait_ge(s_c1n, 3 * (item[1] + 1))
                        for t in range(HT):
                            mm = pe.matmul(PS[0:3 * HPG, b, t * P:(t + 1) * P],
                                           MXP[:, t, :, :].rearrange("p i k -> p (i k)"), IDB[:, :],
                                           start=True, stop=True)
                        mm.then_inc(s_c1, 1)
                        return
                    _, lot, t, c, i = item
                    g, width, diagonal = LOT[lot][0], row_width(t, c), c == t // HT
                    if diagonal:
                        pe.matmul(PS[:, b, width - P:width], IDB[:, :], MASKN[:, :], start=True, stop=False,
                                  skip_group_check=True)
                    pe.matmul(PS[:, b, 0:width], QS[:, g * HPG + i, t * P:(t + 1) * P],
                              KS[:, 2 * g + i // 2, c * HALF:c * HALF + width], start=not diagonal, stop=True,
                              skip_group_check=True).then_inc(s_c1, 1)

                def scores(n, pair):
                    lot, k = STEPS2[n]
                    g, h = LOT[lot]
                    first, width = columns(h, k)
                    diagonal = k * P >= h * HALF
                    if n >= 1:
                        pe.wait_ge(s_c2e, 2 * n + pair - 1)
                    b = 2 * pair
                    if diagonal:
                        for a in range(2):
                            pe.matmul(PS[:, b + a, 0:P], IDB[:, :], MASKT[:, :], start=True, stop=False,
                                      skip_group_check=True)
                    for a in range(2):
                        mm = pe.matmul(PS[:, b + a, 0:width], KS[:, 2 * g + pair, k * P:(k + 1) * P],
                                       QS[:, g * HPG + 2 * pair + a, h * HALF + first:(h + 1) * HALF],
                                       start=not diagonal, stop=True, skip_group_check=True)
                    mm.then_inc(s_c2, 1)

                def values(n):
                    lot, k = STEPS2[n]
                    g, h = LOT[lot]
                    first, width = columns(h, k)
                    if k == 0 and lot >= 1:
                        pe.wait_ge(s_c2a, lot)
                    pe.wait_ge(s_c2e, 2 * (n + 1))
                    for i in range(HPG):
                        mm = pe.matmul(PS[STRIP * i:STRIP * (i + 1), 6, first:HALF], VA[:, k, g * HPG + i, :],
                                       PB[:, n % 3, i, 0:width], start=(k == 0),
                                       stop=(k == (h + 1) * HT - 1), skip_group_check=True)
                    mm.then_inc(s_c2v, 1)

                pe.wait_ge(s_cst, 16 * 3 * len(ROLES))
                pe.wait_ge(s_cst2, 16 * len(ROLES))
                for j in range(AHEAD):
                    pass1(j)
                pe.wait_ge(s_c1m, AHEAD)
                for n in range(N2):
                    lot, k = STEPS2[n]
                    if k == 0:
                        pe.wait_ge(s_c1q, 16 * HPG * (lot + 1))
                    mine = WITH_STEP[n]
                    scores(n, 0)
                    for j in mine[:len(mine) // 2]:
                        pass1(j)
                    scores(n, 1)
                    for j in mine[len(mine) // 2:]:
                        pass1(j)
                    if n >= 1:
                        values(n - 1)
                values(N2 - 1)

            @block.scalar
            def _(act):
                def keep(lot):
                    g, h = LOT[lot]
                    act.wait_ge(s_c2v, END2[lot])
                    act.activation(AT[g][:, h * HALF:(h + 1) * HALF], PS[:, 6, :], ACT.Copy).then_inc(s_c2a, 1)

                for n in range(N2):
                    lot, k = STEPS2[n]
                    first, width = columns(LOT[lot][1], k)
                    for pair in range(2):
                        act.wait_ge(s_c2, 2 * n + pair + 1)
                        if n >= 3:
                            act.wait_ge(s_c2v, n - 2)
                        act.activation(PB[:, n % 3, 2 * pair:2 * pair + 2, 0:width],
                                       PS[:, 2 * pair:2 * pair + 2, 0:width], ACT.Exp,
                                       scale=float(HD) ** -0.5).then_inc(s_c2e, 1)
                    if k == 0 and lot >= 1:
                        keep(lot - 1)
                keep(LOTS - 1)

            @block.vector
            def _(dve):
                def join(lot):
                    dve.wait_ge(s_c1m, LAST_ROW[lot])
                    if lot >= 1:
                        dve.wait_ge(s_c1k, 3 * lot)
                    dve.tensor_tensor(MXL[:, :, :], MXC[:, lot, :, :, 0], MXC[:, lot, :, :, 1],
                                      ALU.max).then_inc(s_c1j, 1)

                for j, item in enumerate(ITEMS):
                    for lot in range(LOTS):
                        if LOT[lot][1] == 1 and j == LAST_ROW[lot] + 1:
                            join(lot)
                    dve.wait_ge(s_c1, j + 1)
                    if item[0] == "turn":
                        if item[1] >= 1:
                            dve.wait_ge(s_c1q, 16 * HPG * item[1])
                        dve.tensor_copy(MP[:, :], PS[0:3 * HPG, BANK[j], :]).then_inc(s_c1m, 1)
                        continue
                    _, lot, t, c, i = item
                    dve.tensor_reduce(MXC[:, lot, t % HT, i:i + 1, c], PS[:, BANK[j], 0:row_width(t, c)], AX.X,
                                      ALU.max).then_inc(s_c1m, 1)

            @block.gpsimd
            def _(pool):
                for lot, (g, h) in enumerate(LOT):
                    high, middle, low = (MXP[:, :, :, k] for k in range(3))
                    pool.wait_ge(s_c1m, LAST_ROW[lot])
                    if h == 1:
                        pool.wait_ge(s_c1j, sum(x[1] for x in LOT[:lot + 1]))
                        maxima = MXL[:, :, :]
                    else:
                        maxima = MXC[:, lot, :, :, 0]
                    pool.tensor_scalar(MXN[:, :, :], maxima, -1.0, None, ALU.mult).then_inc(s_c1k, 1)
                    if lot >= 1:
                        pool.wait_ge(s_c1m, ITEMS.index(("turn", lot - 1)) + 1)
                    pool.wait_ge(s_c1k, 3 * lot + 1)
                    pool.tensor_copy(high, MXN[:, :, :]).then_inc(s_c1n, 1)
                    pool.wait_ge(s_c1n, 3 * lot + 1)
                    pool.tensor_tensor(MXN[:, :, :], MXN[:, :, :], high, ALU.subtract).then_inc(s_c1k, 1)
                    pool.wait_ge(s_c1k, 3 * lot + 2)
                    pool.tensor_copy(middle, MXN[:, :, :]).then_inc(s_c1n, 1)
                    pool.wait_ge(s_c1n, 3 * lot + 2)
                    pool.tensor_tensor(MXN[:, :, :], MXN[:, :, :], middle, ALU.subtract).then_inc(s_c1k, 1)
                    pool.wait_ge(s_c1k, 3 * lot + 3)
                    pool.tensor_copy(low, MXN[:, :, :]).then_inc(s_c1n, 1)
                    if lot + 1 < LOTS:
                        pool.wait_ge(s_c1n, 3 * lot + 3)

            @block.sync
            def _(sp):
                for lot, (g, h) in enumerate(LOT):
                    sp.wait_ge(s_c1m, ITEMS.index(("turn", lot)) + 1)
                    if lot >= 1:
                        sp.wait_ge(s_c1q, 16 * HPG * lot)
                    for i in range(HPG):
                        row = HROWS * (i % 2) + MAXROW
                        sp.dma_start(QS[row:row + 3, g * HPG + i, h * HALF:(h + 1) * HALF],
                                     MP[3 * i:3 * (i + 1), :]).then_inc(s_c1q, 16)

        s_ct1, s_cr, s_ca, s_ct2, s_ca2, s_co, s_cx = (sem(n) for n in (
            "causal_turned", "causal_recip", "causal_divided", "causal_turned_back", "causal_turned_kept",
            "causal_out", "causal_added"))
        RN = sb("RN", [P, TT, HEADS])
        AN = work(16384, TT, P)
        ANT = work(17408, TOKENS)
        with nc.Block() as block:
            @block.tensor
            def _(pe):
                for t in range(TT):
                    if t >= 4:
                        pe.wait_ge(s_ca, t - 3)
                    for g in range(GROUPS):
                        mm = pe.transpose(PS[:, t % 4, g * P:(g + 1) * P], AT[g][:, t * P:(t + 1) * P], ident[:, :])
                    mm.then_inc(s_ct1, 1)
                for t in range(TT):
                    pe.wait_ge(s_ca, t + 1)
                    pe.transpose(PS[:, 4 + t // HT, (t % HT) * P:(t % HT + 1) * P], AN[:, t, :],
                                 ident[:, :]).then_inc(s_ct2, 1)
                for t in range(TT):
                    pe.wait_ge(s_ca2, t // HT + 1)
                    pe.matmul(PS[:, 6 + t // HT, (t % HT) * P:(t % HT + 1) * P], ANT[:, t * P:(t + 1) * P],
                              W["woc_t"][:, :], start=True, stop=True).then_inc(s_co, 1)

            @block.scalar
            def _(act):
                for h in range(2):
                    act.wait_ge(s_ct2, (h + 1) * HT)
                    act.activation(ANT[:, h * HALF:(h + 1) * HALF], PS[:, 4 + h, :], ACT.Copy).then_inc(s_ca2, 1)

            @block.vector
            def _(dve):
                for t in range(TT):
                    src = PS[:, t % 4, :].rearrange("p (h s) -> p h s", s=STRIP)
                    dve.wait_ge(s_ct1, t + 1)
                    dve.reciprocal(RN[:, t, :], src[:, :, HD]).then_inc(s_cr, 1)
                    dve.wait_ge(s_cr, t + 1)
                    dve.tensor_tensor(AN[:, t, :].rearrange("p (h d) -> p h d", d=HD), src[:, :, 0:HD],
                                      RN[:, t, :].unsqueeze(2).broadcast_to([P, HEADS, HD]),
                                      ALU.mult).then_inc(s_ca, 1)
                for h in range(2):
                    dve.wait_ge(s_co, (h + 1) * HT)
                    v = X[:, h * HT:(h + 1) * HT, :]
                    dve.tensor_tensor(v, PS[:, 6 + h, :].rearrange("p (t d) -> p t d", d=P), v, ALU.add).then_inc(s_cx, 1)

        ACC = work(0, TT, P)
        HID = work(1024, 2, HC, HALF)
        RAW = work(5120, 2, 2, HIDDEN)
        B1 = work(7168, EXPERTS * HC)
        B1S = work(7208, 2, HC)
        B2 = work(7232, P)
        GW = work(7360, EXPERTS)
        LG = work(7424, TT, EXPERTS)
        G1 = work(7488, TT, EXPERTS, EXPERTS)
        G2 = work(8000, TT, EXPERTS, EXPERTS)
        LOW = work(8512, EXPERTS, EXPERTS)
        RK = work(8576, TT, EXPERTS)
        S8 = work(8640, TT)
        CMB = work(8704, TT, EXPERTS)
        CMT = work(8768, TOKENS)

        def half_words(at, n):
            return BIG[:, at:at + n // 2].bitcast(F16)

        XH, XL = half_words(9792, TOKENS), half_words(10304, TOKENS)
        WH, WL = (half_words(at, 4 * HIDDEN).rearrange("p (s w h) -> p s w h", s=2, w=2) for at in (10816, 11840))
        HH, HL = (half_words(at, 2 * HC * HALF).rearrange("p (h c q) -> p h c q", h=2, c=HC) for at in (12864, 14912))
        s_wa, s_wb, s_ws, s_wh, s_wl, s_xh, s_xl = (sem(n) for n in (
            "expert_weights_a", "expert_weights_b", "expert_weights_scaled", "expert_weights_high",
            "expert_weights_low", "expert_x_high", "expert_x_low"))

        FACTORS = sb("FACTORS", [P, 2])

        def load_expert(sp, e, k):
            s = s_wa if k == 0 else s_wb
            sp.dma_start(RAW[:, k, 0, :], a["L1_ffn_W1"][bass.ds(e, 1), :, :].rearrange("e d h -> d (e h)")
                         ).then_inc(s, 16)
            sp.dma_start(RAW[:, k, 1, :].rearrange("p (c d) -> p c d", d=P),
                         a["L1_ffn_W2"][bass.ds(e, 1), :, :].rearrange("e (c p) d -> p (e c) d", p=P)
                         ).then_inc(s, 16)

        def split_expert(pool, i, k, free=None):
            e = i * 2 + k
            def by(k):
                return FACTORS[:, k:k + 1].unsqueeze(2).broadcast_to([P, 2, HIDDEN])

            raw, high, low = RAW[:, k, :, :], WH[:, k, :, :], WL[:, k, :, :]
            pool.wait_ge(s_wa if k == 0 else s_wb, 32 * i + 32)
            pool.tensor_tensor(raw, raw, by(1), ALU.mult).then_inc(s_ws, 1)
            if free is not None:
                free()
            pool.wait_ge(s_ws, e + 1)
            pool.tensor_tensor(high, raw, by(0), ALU.mult).then_inc(s_wh, 1)
            pool.wait_ge(s_wh, e + 1)
            pool.tensor_tensor(low, raw, high, ALU.subtract).then_inc(s_wl, 1)

        s_fs, s_sb, s_gw, s_b1, s_gl, s_gc, s_ge, s_ct, s_ctc, s_sg, s_b2 = (sem(n) for n in (
            "factors_set", "shared_biased", "gate_loaded", "hidden_biases_loaded", "gate_logits", "gate_chain", "gate_exp", "combine_turned", "combine_kept",
            "shared_gelu", "bias_mixed"))
        def load_gate_and_first(sp):
            sp.dma_start(GW, a["L1_ffn_gate_W"]).then_inc(s_gw, 16)
            sp.dma_start(LOW.rearrange("p a b -> p (a b)"), a["lower"].partition_broadcast(P)).then_inc(s_gw, 16)
            sp.dma_start(B2[0:EXPERTS, :], a["L1_ffn_b2"]).then_inc(s_gw, 16)
            load_expert(sp, 0, 0)
            sp.dma_start(B1, a["b1_cols"]).then_inc(s_b1, 16)
            load_expert(sp, 1, 1)

        norm_stage(X, XN, 1e-5)
        query_stage(W["w1x_t"][:, :], C["L1_xattn_b"][:, 0:1], W["L1_xattn_W"][:, :], C["L1_xattn_b"][:, 0:1])
        attend()
        mix_stage(ident, X, X, loads=load_gate_and_first)

        norm_stage(X, XN, 1e-5)
        s_ai, s_bc, s_hd, s_h, s_hg, s_hh, s_hl, s_y, s_acc = (sem(n) for n in (
            "accumulator_started", "expert_biases_set", "expert_rounded", "expert_hidden", "expert_gelu",
            "expert_gelu_high", "expert_gelu_low", "expert_out", "expert_added"))
        PAIRS = EXPERTS // 2
        UPP = 4
        DVE_ROUNDS = 2
        with nc.Block() as block:
            @block.sync
            def _(sp):
                with sp.Fori(1, PAIRS) as i:
                    for k in range(2):
                        sp.wait_ge(s_wl, i * 2 + k - 1)
                        load_expert(sp, i * 2 + k, k)

            @block.gpsimd
            def _(pool):
                pool.memset(FACTORS[:, 0:1], 1.0).then_inc(s_fs, 1)
                pool.memset(FACTORS[:, 1:2], WSCALE).then_inc(s_fs, 1)
                pool.wait_ge(s_fs, 2)
                split_expert(pool, 0, 0)
                split_expert(pool, 0, 1)
                pool.tensor_tensor(X[:, :, :], X[:, :, :], over_tokens(R["L1_ffn_beta"]), ALU.add).then_inc(s_pb, 1)
                with pool.Fori(1, PAIRS) as i:
                    for k in range(2):
                        split_expert(pool, i, k, lambda: pool.wait_ge(s_y, HT * (UPP * (i - 1) + 2 * k + 2)))

            @block.tensor
            def _(pe):
                def turn_combination():
                    pe.wait_ge(s_gc, 14)
                    for t in range(TT):
                        mm = pe.transpose(PS[0:EXPERTS, 6 + t // HT, (t % HT) * P:(t % HT + 1) * P], CMB[:, t, :],
                                          ident[:, :])
                    mm.then_inc(s_ct, 1)

                def mix_biases():
                    pe.wait_ge(s_ctc, 1)
                    for t in range(TT):
                        mm = pe.matmul(PS[:, 6 + t // HT, (t % HT) * P:(t % HT + 1) * P],
                                       CMT[0:EXPERTS, t * P:(t + 1) * P], B2[0:EXPERTS, :], start=True, stop=True)
                    mm.then_inc(s_b2, 1)

                def product(o, high, low, rhs_high, rhs_low, start, stop):
                    pe.matmul(o, high, rhs_high, start=start, stop=False)
                    pe.matmul(o, high, rhs_low, start=False, stop=False)
                    return pe.matmul(o, low, rhs_high, start=False, stop=stop)

                def hidden(i, k, first):
                    slot, h = k // 2, k % 2
                    half = slice(h * HALF, (h + 1) * HALF)
                    if h == 0:
                        pe.wait_ge(s_wl, i * 2 + slot + 1)
                    for c in range(HC):
                        if not (first and k == 0):
                            pe.wait_ge(s_hh, (i * UPP + k - 1) * HC + c + 1)
                        cols = slice(c * P, (c + 1) * P)
                        product(PS[:, c, :], WH[:, slot, 0, cols], WL[:, slot, 0, cols], XH[:, half], XL[:, half],
                                True, True).then_inc(s_h, 1)

                def output(i, k, early):
                    slot, h = k // 2, k % 2
                    pe.wait_ge(s_hl, (i * UPP + k + 1) * HC)
                    pe.wait_ge(s_hh, (i * UPP + k + 1) * HC)
                    if not early:
                        pe.wait_ge(s_acc, (i * UPP + k - 1) * HT)
                    else:
                        pe.wait_ge(s_sb, 1)
                    for t in range(HT):
                        for c in range(HC):
                            cols, mine = slice(c * P, (c + 1) * P), slice(t * P, (t + 1) * P)
                            mm = product(PS[:, 4 + k % 2, mine], HH[:, h, c, mine], HL[:, h, c, mine],
                                         WH[:, slot, 1, cols], WL[:, slot, 1, cols], c == 0, c == HC - 1)
                        mm.then_inc(s_y, 1)

                def step(i, first):
                    for k in range(UPP):
                        hidden(i, k, first)
                        if first and k == 1:
                            turn_combination()
                        if k > 0:
                            output(i, k - 1, first and k - 1 < 2)
                        elif not first:
                            output(i - 1, UPP - 1, False)
                        if first and k == 1:
                            mix_biases()

                pe.wait_ge(s_gw, 48)
                for t in range(TT):
                    mm = pe.matmul(PS[:, 7, t * EXPERTS:(t + 1) * EXPERTS], XT[:, t * P:(t + 1) * P], GW,
                                   start=True, stop=True)
                mm.then_inc(s_gl, 1)
                for t in range(TT):
                    mm = pe.matmul(PS[:, 4 + t // HT, (t % HT) * P:(t % HT + 1) * P], XT[:, t * P:(t + 1) * P],
                                   W["L1_ffn_shared_W"][:, :], start=True, stop=True)
                mm.then_inc(s_gl, 1)
                pe.wait_ge(s_xh, 2)
                pe.wait_ge(s_xl, 2)
                step(0, True)
                with pe.Fori(1, PAIRS) as i:
                    step(i, False)
                output(PAIRS - 1, UPP - 1, False)

            @block.scalar
            def _(act):
                def step(i, first):
                    for k in range(UPP):
                        slot, h = k // 2, k % 2
                        if h == 0:
                            act.activation(B1S[:, slot, :], B1[:, bass.ds(i * (2 * HC) + slot * HC, HC)],
                                           ACT.Copy).then_inc(s_bc, 1)
                            act.wait_ge(s_bc, i * 2 + slot + 1)
                        if not (first and k < 2):
                            act.wait_ge(s_y, (i * UPP + k - 1) * HT)
                        for c in range(HC):
                            act.wait_ge(s_h, (i * UPP + k) * HC + c + 1)
                            bias = B1S[:, slot, c:c + 1]
                            act.activation(HID[:, h, c, :], PS[:, c, :], ACT.Gelu, bias=bias,
                                           scale=1.0 / WSCALE).then_inc(s_hg if c < DVE_ROUNDS else s_hh, 1)
                            if c < DVE_ROUNDS:
                                act.activation(HH[:, h, c, :], PS[:, c, :], ACT.Gelu, bias=bias,
                                               scale=1.0 / WSCALE).then_inc(s_hh, 1)

                for h in range(2):
                    half = slice(h * HALF, (h + 1) * HALF)
                    act.activation(XH[:, half], XT[:, half], ACT.Copy).then_inc(s_xh, 1)
                act.wait_ge(s_gc, 2)
                act.activation(LG, LG, ACT.Exp).then_inc(s_ge, 1)
                act.wait_ge(s_sb, 1)
                act.activation(NAT[:, :, :], NAT[:, :, :], ACT.Gelu).then_inc(s_sg, 1)
                act.wait_ge(s_b1, 16)
                step(0, True)
                with act.Fori(1, PAIRS) as i:
                    step(i, False)

            @block.vector
            def _(dve):
                def across(v):
                    return v.unsqueeze(2).broadcast_to([P, TT, EXPERTS])

                for h in range(2):
                    half = slice(h * HALF, (h + 1) * HALF)
                    dve.wait_ge(s_xh, h + 1)
                    dve.tensor_tensor(XL[:, half], XT[:, half], XH[:, half], ALU.subtract).then_inc(s_xl, 1)
                dve.wait_ge(s_gl, 1)
                dve.tensor_reduce(S8, PS[:, 7, 0:TT * EXPERTS].rearrange("p (t e) -> p t e", e=EXPERTS), AX.X,
                                  ALU.max).then_inc(s_gc, 1)
                dve.wait_ge(s_gc, 1)
                dve.tensor_tensor(LG, PS[:, 7, 0:TT * EXPERTS].rearrange("p (t e) -> p t e", e=EXPERTS),
                                  across(S8), ALU.subtract).then_inc(s_gc, 1)
                dve.wait_ge(s_gl, 2)
                dve.tensor_tensor(NAT[:, :, :].rearrange("p (h t) d -> p h t d", h=2),
                                  PS[:, 4:6, :].rearrange("p h (t d) -> p h t d", d=P),
                                  R["L1_ffn_shared_b"][:, :].unsqueeze(1).unsqueeze(1).broadcast_to([P, 2, HT, P]),
                                  ALU.add).then_inc(s_sb, 1)
                dve.wait_ge(s_ge, 1)
                dve.tensor_reduce(S8, LG, AX.X, ALU.add).then_inc(s_gc, 1)
                dve.wait_ge(s_gc, 3)
                dve.reciprocal(S8, S8).then_inc(s_gc, 1)
                dve.wait_ge(s_gc, 4)
                dve.tensor_tensor(LG, LG, across(S8), ALU.mult).then_inc(s_gc, 1)
                dve.wait_ge(s_gc, 5)
                mine = LG.unsqueeze(3).broadcast_to([P, TT, EXPERTS, EXPERTS])
                other = LG.unsqueeze(2).broadcast_to([P, TT, EXPERTS, EXPERTS])
                dve.tensor_tensor(G1, other, mine, ALU.is_gt).then_inc(s_gc, 1)
                dve.tensor_tensor(G2, other, mine, ALU.is_equal).then_inc(s_gc, 1)
                dve.wait_ge(s_gc, 7)
                dve.wait_ge(s_gw, 48)
                dve.tensor_tensor(G2, G2, LOW.unsqueeze(1).broadcast_to([P, TT, EXPERTS, EXPERTS]),
                                  ALU.mult).then_inc(s_gc, 1)
                dve.wait_ge(s_gc, 8)
                dve.tensor_tensor(G1, G1, G2, ALU.add).then_inc(s_gc, 1)
                dve.wait_ge(s_gc, 9)
                dve.tensor_reduce(RK, G1, AX.X, ALU.add).then_inc(s_gc, 1)
                dve.wait_ge(s_gc, 10)
                dve.scalar_tensor_tensor(out=CMB, in0=RK, scalar=1.5, in1=LG, op0=ALU.is_lt,
                                         op1=ALU.mult).then_inc(s_gc, 1)
                dve.wait_ge(s_gc, 11)
                dve.tensor_reduce(S8, CMB, AX.X, ALU.add).then_inc(s_gc, 1)
                dve.wait_ge(s_gc, 12)
                dve.reciprocal(S8, S8).then_inc(s_gc, 1)
                dve.wait_ge(s_gc, 13)
                dve.tensor_tensor(CMB, CMB, across(S8), ALU.mult).then_inc(s_gc, 1)
                def keep_turned():
                    dve.wait_ge(s_ct, 1)
                    dve.tensor_copy(CMT[0:EXPERTS, :].rearrange("p (h q) -> p h q", h=2),
                                    PS[0:EXPERTS, 6:8, :]).then_inc(s_ctc, 1)
                    dve.tensor_scalar(CMB, CMB, 1.0 / WSCALE, None, ALU.mult).then_inc(s_ctc, 1)

                def start_accumulator():
                    dve.wait_ge(s_sg, 1)
                    dve.wait_ge(s_b2, 1)
                    dve.scalar_tensor_tensor(out=ACC.rearrange("p t d -> p (t d)").rearrange("p (h q) -> p h q", h=2),
                                             in0=NAT[:, :, :].rearrange("p t d -> p (t d)").rearrange(
                                                 "p (h q) -> p h q", h=2),
                                             scalar=0.5, in1=PS[:, 6:8, :], op0=ALU.mult, op1=ALU.add).then_inc(s_ai, 1)
                    dve.wait_ge(s_ai, 1)
                    dve.wait_ge(s_ctc, 2)
                def low(i, k):
                    h = k % 2
                    for c in range(HC):
                        dve.wait_ge(s_hh, (i * UPP + k) * HC + c + 1)
                        if c < DVE_ROUNDS:
                            dve.tensor_tensor(HL[:, h, c, :], HID[:, h, c, :], HH[:, h, c, :],
                                              ALU.subtract).then_inc(s_hl, 1)
                        else:
                            dve.tensor_copy(HH[:, h, c, :], HID[:, h, c, :]).then_inc(s_hd, 1)
                    for c in range(DVE_ROUNDS, HC):
                        dve.wait_ge(s_hd, (i * UPP + k) * (HC - DVE_ROUNDS) + c - DVE_ROUNDS + 1)
                        dve.tensor_tensor(HL[:, h, c, :], HID[:, h, c, :], HH[:, h, c, :],
                                          ALU.subtract).then_inc(s_hl, 1)

                def accumulate(i, k):
                    slot, h = k // 2, k % 2
                    dve.wait_ge(s_y, (i * UPP + k + 1) * HT)
                    for t in range(HT):
                        v = ACC[:, h * HT + t, :]
                        dve.scalar_tensor_tensor(out=v, in0=PS[:, 4 + k % 2, t * P:(t + 1) * P],
                                                 scalar=CMB[:, h * HT + t, bass.ds(i * 2 + slot, 1)], in1=v,
                                                 op0=ALU.mult, op1=ALU.add).then_inc(s_acc, 1)

                def step(i, first):
                    for k in range(UPP):
                        low(i, k)
                        if first and k == 0:
                            keep_turned()
                        if first and k == 1:
                            start_accumulator()
                        if k > 0:
                            accumulate(i, k - 1)
                        elif not first:
                            accumulate(i - 1, UPP - 1)

                step(0, True)
                with dve.Fori(1, PAIRS) as i:
                    step(i, False)
                accumulate(PAIRS - 1, UPP - 1)

        norm_stage(ACC, NAT, 1e-5, turn=False, gain=R["L1_ffn_gamma"], store=True)


def kernel(**inputs):
    import ml_dtypes
    import numpy as np
    import concourse.bacc as bacc
    from concourse.bass_utils import run_bass_kernel_spmd

    f = {k: np.ascontiguousarray(v) for k, v in inputs.items()}
    bf16 = ml_dtypes.bfloat16

    f["xwk_t"] = f["L0_xattn_Wk"].T
    f["w1x_t"] = f["L1_xattn_W"].T
    for name, w in (("wqc_t", "L1_attn_q_proj"), ("wkc_t", "L1_attn_k_proj")):
        f[name] = f[w].reshape(HEADS // 2, 2, HD, P).transpose(1, 2, 0, 3).reshape(P, P).T
    f["wvc_t"] = f["L1_attn_v_proj"].T
    f["woc_t"] = f["L1_attn_o_proj"].T
    f["b1_cols"] = f["L1_ffn_b1"].reshape(EXPERTS * HC, P).T

    k = np.arange(P)
    turn = 2.0 * np.pi * (np.outer(k, k) % P) / P
    f["ident"] = np.eye(P, dtype=np.float32)
    f["cos"] = np.cos(turn).astype(np.float32)
    f["sin"] = np.sin(turn).astype(np.float32)
    f["nsin"] = -f["sin"]
    f["blocks"] = np.kron(np.eye(HEADS), np.ones((HD, HD))).astype(np.float32)
    f["wfb_f"], f["wfb_r"] = f["L0_attn_Wfb"][0:P], f["L0_attn_Wfb"][P:2 * P]
    f["wr"], f["wi"] = f["L0_ffn_w_freq_real"], f["L0_ffn_w_freq_imag"]
    f["bf_squares"] = np.stack([np.eye(P), np.where(k[None, :] > k[:, None], MASKED, 0.0),
                                np.where(k[:, None] > k[None, :], MASKED, 0.0)], axis=1).astype(bf16)
    f["squares"] = np.stack([f[n] for n in SQ], axis=1)
    f["columns"] = np.stack([f[n] for n in COLS], axis=1)
    f["rows"] = np.concatenate([f[n] for n in ROWS])
    e = np.arange(EXPERTS)
    f["lower"] = (e[None, :] < e[:, None]).astype(np.float32).reshape(-1)

    used = ("x", "ctx_1024", "squares", "bf_squares", "columns", "rows", "lower", "b1_cols", "L1_ffn_b2", "L1_ffn_gate_W",
            "L1_ffn_W1", "L1_ffn_W2")
    nc = bacc.Bacc("TRN2", target_bir_lowering=False, num_devices=1)
    arrays, aps = {}, {}
    for name in used:
        v = np.ascontiguousarray(f[name])
        arrays[f"in_{name}"] = v
        aps[name] = nc.dram_tensor(f"in_{name}", v.shape, mybir.dt.from_np(v.dtype), kind="ExternalInput").ap()
    out = nc.dram_tensor("out_0", (1, TOKENS, P), F32, kind="ExternalOutput").ap()
    decoder_kernel(nc, aps, out)
    r = run_bass_kernel_spmd(nc, [arrays], core_ids=[0])
    return r.results[0]["out_0"]
```
